# Optimizing a Trainium2 kernel written in Bass

```python
import numpy as np
import jax
import jax.numpy as jnp

def _softmax(x, axis=-1):
    return jax.nn.softmax(x, axis=axis)

def _gelu(x):
    return jax.nn.gelu(x, approximate=True)

def _silu(x):
    return jax.nn.silu(x)

def _sigmoid(x):
    return jax.nn.sigmoid(x)

def _layernorm(x, axis=-1, eps=1e-05):
    m = jnp.mean(x, axis=axis, keepdims=True)
    v = jnp.var(x, axis=axis, keepdims=True)
    return (x - m) / jnp.sqrt(v + eps)

def _scatter_add(tgt, idx, src, axis=0):
    return tgt.at[idx].add(src)

def _segment_sum(src, seg, n):
    return jax.ops.segment_sum(src, seg, n)
kernel_name = 'mk_xattn_ffn_d1_seqx_r4_d318eb'

def setup_inputs(seed: int=0):
    np.random.seed(seed)
    _w = jnp.asarray

    def _rec_inputs():
        import jax
        import jax.numpy as jnp
        _rk = jax.random.key(seed)
        x = -0.0002928 + 1 * jax.random.normal(jax.random.fold_in(_rk, 1), (16, 256, 256), jnp.float32)
        _lenS = 256 - jax.random.randint(jax.random.fold_in(_rk, 7), (16,), 0, max(1, 256 // 4) + 1, jnp.int32)
        _lenS2 = 256 - jax.random.randint(jax.random.fold_in(_rk, 8), (16,), 0, max(1, 256 // 4) + 1, jnp.int32)
        _ctx_1024P = jax.random.normal(jax.random.fold_in(_rk, 11), (16, 16, 256), jnp.float32)
        _ctx_1024c = jax.random.dirichlet(jax.random.fold_in(_rk, 511), 0.3 * jnp.ones((16,), jnp.float32), (16, 256))
        _ctx_1024t = jnp.einsum('bsk,bkd->bsd', _ctx_1024c, _ctx_1024P)
        _ctx_1024t = _ctx_1024t * jax.lax.rsqrt(jnp.mean(jnp.square(_ctx_1024t)) + 1e-12) * 0.953939
        ctx_1024 = -1.39393e-06 + 0.999914 * (_ctx_1024t + 0.3 * jax.random.normal(jax.random.fold_in(_rk, 611), (16, 256, 256), jnp.float32))
        return (x, ctx_1024)
    x, ctx_1024 = _rec_inputs()

    def _L0_xattn_setup():
        import jax, jax.numpy as jnp
        import numpy as np
        B, S, H, NH = (2, 512, 256, 4)
        DH = H // NH
        EPS = 1e-06

        def _parallel_stabilized(qh, kh, vh, ig, fg):
            log_fg = jax.nn.log_sigmoid(fg)
            cs = jnp.cumsum(log_fg, axis=2)
            ltr = jnp.tril(jnp.ones((qh.shape[2], qh.shape[2]), dtype=bool))
            log_fg_mat = jnp.where(ltr, cs - jnp.swapaxes(cs, 2, 3), -jnp.inf)
            log_D = log_fg_mat + jnp.swapaxes(ig, 2, 3)
            max_log_D = jnp.max(log_D, axis=-1, keepdims=True)
            D = jnp.exp(log_D - max_log_D)
            qk = jnp.einsum('bhsd,bhtd->bhst', qh, kh) / jnp.sqrt(jnp.float32(DH))
            C = qk * D
            normalizer = jnp.maximum(jnp.abs(jnp.sum(C, axis=-1, keepdims=True)), jnp.exp(-max_log_D))
            return jnp.einsum('bhst,bhtd->bhsd', C / (normalizer + EPS), vh)
        key = jax.random.key(seed)
        ks = jax.random.split(key, 6)
        q = jax.random.normal(ks[0], (B, S, H), dtype=jnp.float32)
        k = jax.random.normal(ks[1], (B, S, H), dtype=jnp.float32)
        v = jax.random.normal(ks[2], (B, S, H), dtype=jnp.float32)
        igate_kernel = jax.random.normal(ks[3], (3 * H, NH), dtype=jnp.float32) * 0.02
        fgate_kernel = jax.random.normal(ks[4], (3 * H, NH), dtype=jnp.float32) * 0.02
        igate_bias = jax.random.normal(ks[5], (NH,), dtype=jnp.float32) * 0.1
        fgate_bias = jnp.linspace(3.0, 6.0, NH, dtype=jnp.float32)
        outnorm_scale = jnp.ones((H,), dtype=jnp.float32)
        return {'q': q, 'k': k, 'v': v, 'igate_kernel': igate_kernel, 'igate_bias': igate_bias, 'fgate_kernel': fgate_kernel, 'fgate_bias': fgate_bias, 'outnorm_scale': outnorm_scale}
    _L0_xattn_all = _L0_xattn_setup()
    _L0_xattn_in = {k: v for k, v in _L0_xattn_all.items() if k in ('igate_kernel', 'igate_bias', 'fgate_kernel', 'fgate_bias', 'outnorm_scale')}
    del _L0_xattn_all

    def _L0_ffn_setup():
        import jax, jax.numpy as jnp
        import numpy as np
        BLOCK = 32
        W_BITS = 4
        ACT_BITS = 16

        def act_qdq(x):
            qmax = 2.0 ** (ACT_BITS - 1) - 1.0
            scale = jnp.maximum(jnp.max(jnp.abs(x)) / qmax, 1e-12)
            return jnp.clip(jnp.round(x / scale), -qmax - 1.0, qmax) * scale

        def fixed_qdq_u16(x):
            scale = 1.0 / 65536.0
            return jnp.clip(jnp.round(x / scale), 0.0, 65535.0) * scale

        def lpbq_dequant(w):
            O, I = w.shape
            qmax = 2.0 ** (W_BITS - 1) - 1.0
            wb = w.reshape(O, I // BLOCK, BLOCK)
            s = jnp.maximum(jnp.max(jnp.abs(wb), axis=-1, keepdims=True) / qmax, 1e-12)
            wq = jnp.clip(jnp.round(wb / s), -qmax - 1.0, qmax) * s
            return wq.reshape(O, I)
        key = jax.random.key(seed)
        k1, k2, k3, k4 = jax.random.split(key, 4)
        B, S, H, I = (2, 1024, 256, 768)
        x = jax.random.normal(k1, (B, S, H), jnp.float32)
        w_gate = jax.random.normal(k2, (I, H), jnp.float32) * 0.02
        w_up = jax.random.normal(k3, (I, H), jnp.float32) * 0.02
        w_down = jax.random.normal(k4, (H, I), jnp.float32) * 0.02
        return {'x': x, 'w_gate': w_gate, 'w_up': w_up, 'w_down': w_down}
    _L0_ffn_all = _L0_ffn_setup()
    _L0_ffn_in = {k: v for k, v in _L0_ffn_all.items() if k in ('w_gate', 'w_up', 'w_down')}
    del _L0_ffn_all
    return {'x': x, 'ctx_1024': ctx_1024, 'L0_xattn_igate_kernel': _L0_xattn_in['igate_kernel'], 'L0_xattn_igate_bias': _L0_xattn_in['igate_bias'], 'L0_xattn_fgate_kernel': _L0_xattn_in['fgate_kernel'], 'L0_xattn_fgate_bias': _L0_xattn_in['fgate_bias'], 'L0_xattn_outnorm_scale': _L0_xattn_in['outnorm_scale'], 'L0_ffn_w_gate': _L0_ffn_in['w_gate'], 'L0_ffn_w_up': _L0_ffn_in['w_up'], 'L0_ffn_w_down': _L0_ffn_in['w_down']}

def reference(x, ctx_1024, L0_xattn_igate_kernel, L0_xattn_igate_bias, L0_xattn_fgate_kernel, L0_xattn_fgate_bias, L0_xattn_outnorm_scale, L0_ffn_w_gate, L0_ffn_w_up, L0_ffn_w_down):
    import jax
    import jax.numpy as jnp

    def _L0_xattn_ref(q, k, v, igate_kernel, igate_bias, fgate_kernel, fgate_bias, outnorm_scale):
        import jax, jax.numpy as jnp
        import numpy as np
        B, S, H, NH = (2, 512, 256, 4)
        DH = H // NH
        EPS = 1e-06

        def _parallel_stabilized(qh, kh, vh, ig, fg):
            log_fg = jax.nn.log_sigmoid(fg)
            cs = jnp.cumsum(log_fg, axis=2)
            ltr = jnp.tril(jnp.ones((qh.shape[2], qh.shape[2]), dtype=bool))
            log_fg_mat = jnp.where(ltr, cs - jnp.swapaxes(cs, 2, 3), -jnp.inf)
            log_D = log_fg_mat + jnp.swapaxes(ig, 2, 3)
            max_log_D = jnp.max(log_D, axis=-1, keepdims=True)
            D = jnp.exp(log_D - max_log_D)
            qk = jnp.einsum('bhsd,bhtd->bhst', qh, kh) / jnp.sqrt(jnp.float32(DH))
            C = qk * D
            normalizer = jnp.maximum(jnp.abs(jnp.sum(C, axis=-1, keepdims=True)), jnp.exp(-max_log_D))
            return jnp.einsum('bhst,bhtd->bhsd', C / (normalizer + EPS), vh)
        Bq, Sq, Hq = q.shape
        x = jnp.concatenate([q, k, v], axis=-1)
        ig = x @ igate_kernel + igate_bias
        fg = x @ fgate_kernel + fgate_bias
        ig = jnp.transpose(ig, (0, 2, 1))[..., None]
        fg = jnp.transpose(fg, (0, 2, 1))[..., None]
        qh = jnp.transpose(q.reshape(Bq, Sq, NH, DH), (0, 2, 1, 3))
        kh = jnp.transpose(k.reshape(Bq, Sq, NH, DH), (0, 2, 1, 3))
        vh = jnp.transpose(v.reshape(Bq, Sq, NH, DH), (0, 2, 1, 3))
        h = _parallel_stabilized(qh, kh, vh, ig, fg)
        mean = jnp.mean(h, axis=-1, keepdims=True)
        var = jnp.mean((h - mean) ** 2, axis=-1, keepdims=True)
        h_norm = (h - mean) * jax.lax.rsqrt(var + 1e-05)
        h_norm = h_norm * outnorm_scale.reshape(1, NH, 1, DH)
        out = jnp.transpose(h_norm, (0, 2, 1, 3)).reshape(Bq, Sq, Hq)
        return out

    def _L0_ffn_ref(x, w_gate, w_up, w_down):
        import jax, jax.numpy as jnp
        import numpy as np
        BLOCK = 32
        W_BITS = 4
        ACT_BITS = 16

        def act_qdq(x):
            qmax = 2.0 ** (ACT_BITS - 1) - 1.0
            scale = jnp.maximum(jnp.max(jnp.abs(x)) / qmax, 1e-12)
            return jnp.clip(jnp.round(x / scale), -qmax - 1.0, qmax) * scale

        def fixed_qdq_u16(x):
            scale = 1.0 / 65536.0
            return jnp.clip(jnp.round(x / scale), 0.0, 65535.0) * scale

        def lpbq_dequant(w):
            O, I = w.shape
            qmax = 2.0 ** (W_BITS - 1) - 1.0
            wb = w.reshape(O, I // BLOCK, BLOCK)
            s = jnp.maximum(jnp.max(jnp.abs(wb), axis=-1, keepdims=True) / qmax, 1e-12)
            wq = jnp.clip(jnp.round(wb / s), -qmax - 1.0, qmax) * s
            return wq.reshape(O, I)
        x = act_qdq(x)
        up = act_qdq(x @ lpbq_dequant(w_up).T)
        gate = act_qdq(x @ lpbq_dequant(w_gate).T)
        sig = fixed_qdq_u16(jax.nn.sigmoid(gate))
        gate = act_qdq(gate * sig)
        o = act_qdq(gate * up)
        return o @ lpbq_dequant(w_down).T
    x = x + _L0_xattn_ref(_layernorm(x, axis=-1), ctx_1024, ctx_1024, L0_xattn_igate_kernel, L0_xattn_igate_bias, L0_xattn_fgate_kernel, L0_xattn_fgate_bias, L0_xattn_outnorm_scale)
    x = x + _L0_ffn_ref(_layernorm(x, axis=-1), L0_ffn_w_gate, L0_ffn_w_up, L0_ffn_w_down)
    return x

_drawn_inputs = setup_inputs


def setup_inputs(seed=0):
    import zlib

    import numpy as np

    out = dict(_drawn_inputs(seed))
    spreads = {'L0_xattn_outnorm_scale': (1.0, 0.2)}
    factors = {'L0_xattn_igate_bias': 8.0,
     'L0_ffn_w_gate': 3.124,
     'L0_ffn_w_up': 2.991,
     'L0_ffn_w_down': 2.997}
    for name, (base, spread) in spreads.items():
        noise = np.random.default_rng([zlib.crc32(name.encode()), seed]).standard_normal(out[name].shape)
        drawn = base * np.exp(spread * noise) if base else spread * noise
        out[name] = jnp.asarray(drawn.astype(out[name].dtype))
    for name, factor in factors.items():
        out[name] = (out[name] * factor).astype(out[name].dtype)
    return out
```

```python
from contextlib import ExitStack

import concourse.bass as bass
from concourse import mybir

F32 = mybir.dt.float32
F16 = mybir.dt.float16
I16 = mybir.dt.int16
U16 = mybir.dt.uint16
U32 = mybir.dt.uint32
ALU = mybir.AluOpType
ACT = mybir.ActivationFunctionType
AX = mybir.AxisListType

P = 128
BATCH = 16
SEQ = 256
HID = 256
NH = 4
DH = HID // NH
FF = 768
HALVES = SEQ // P
KT = HID // P
UNROLL = 4
PAIR = 2
PAIRS = BATCH // PAIR
VC = DH + 2
GC = 3 * NH
SCORES = NH * (SEQ + P)
CH = 512
CHUNKS = BATCH * SEQ // CH
FT = FF // P
SLOT = FT * CH
PAIRC = 2 * CH
FP = FT // 2
BLOCK = 32
STRIPS = 3 * FF * HID // (P * HID)
QMAX16 = 2.0 ** 15 - 1.0
QMAX4 = 7.0
LN_EPS = 1e-5
NORM_EPS = 1e-6
TINY = 1e-12
W_UNIT = 4096.0
NEVER = 1.0e30


def bass_xattn_ffn(nc, x, ctx_nat, ctx_t, gate_w, gate_b, norm_scale, w_gate, w_up, w_down, out):
    x1_dram = nc.dram_tensor("x1_spill", (PAIRS, P, PAIR * HALVES * HID), F32, kind="Internal").ap()
    max_dram = nc.dram_tensor("running_max", (BATCH * NH, SEQ), F32, kind="Internal").ap()
    up_dram = nc.dram_tensor("up_spill", (4, P, SLOT), F32, kind="Internal").ap()

    es = ExitStack()
    with es:
        def sb(name, shape, dt=F32):
            return es.enter_context(nc.sbuf_tensor(name, shape, dt))

        def sem(name):
            return es.enter_context(nc.semaphore(name))

        A_TMP = 8 * SLOT
        A_X = 12 * SLOT
        arena = sb("arena", [P, A_X + BATCH * HALVES * HID])

        def at(off, n):
            return arena[:, off:off + n]

        def at_dyn(off, n):
            return arena[:, bass.ds(off, n)]

        def slot_pair(slot, j):
            if isinstance(slot, int):
                return at(slot * SLOT + j * PAIRC, PAIRC)
            return at_dyn(slot * SLOT + j * PAIRC, PAIRC)

        wg_parts = sb("wg_parts", [P, 2, KT, FF], F16)
        wu_parts = sb("wu_parts", [P, 2, KT, FF], F16)
        wd_parts = sb("wd_parts", [P, 2, FT, HID], F16)
        gates = sb("gates", [P, HALVES, BATCH, GC])
        scale_row = sb("scale_row", [P, HID])
        ident = sb("ident", [P, P])
        tri = sb("tri", [P, P])
        ones = sb("ones", [P, P])
        gate_w_raw = sb("gate_w_raw", [P, 3 * KT, 2 * NH])
        ctx_gate_w = sb("ctx_gate_w", [P, KT, GC])
        gate_bias = sb("gate_bias", [P, 2 * NH])
        a_nat = sb("a_nat", [P, HALVES, BATCH * NH])
        floor_nat = sb("floor_nat", [P, HALVES, BATCH * NH])
        run_max = sb("run_max", [BATCH * NH, SEQ])
        sigq_buf = sb("sigq_buf", [P, PAIRC], U16)
        bn_raw = sb("bn_raw", [P, 2, HALVES, 6])
        mean_var = sb("mean_var", [P, 2, HALVES, 2])
        rstd = sb("rstd", [P, 2, HALVES, 1])
        minus_half = sb("minus_half", [P, HALVES * NH])
        o_cols = sb("o_cols", [P, 2, HALVES * NH, 2])
        floor_n = sb("floor_n", [P, 2, HALVES * NH])
        floor_w = sb("floor_w", [P, 2, HALVES * NH])
        floor_w2 = sb("floor_w2", [P, 2, HALVES * NH])
        sumsq = sb("sumsq", [P, 2, HALVES * NH])
        head_var = sb("head_var", [P, 2, HALVES * NH])
        head_gain = sb("head_gain", [P, 2, HALVES * NH])
        xmax = sb("xmax", [P, BATCH])
        gmax = sb("gmax", [P, CHUNKS * FP])
        umax = sb("umax", [P, CHUNKS * FP])
        gsmax = sb("gsmax", [P, CHUNKS * FP])
        omax = sb("omax", [P, CHUNKS * FP])
        red = sb("red", [P, 8])
        allmax = sb("allmax", [P, 8])
        sc = sb("sc", [P, 32])
        block_max = sb("block_max", [P, STRIPS * 8])
        block_s = sb("block_s", [P, STRIPS * 8])
        block_inv = sb("block_inv", [P, STRIPS * 8])

        q_nat = [at(A_TMP + i * 512, 512) for i in range(2)]
        q_t = [at(A_TMP + 1024 + i * 512, 512).rearrange("p (k t) -> p k t", k=KT) for i in range(2)]
        ctx_t_sb = [at(A_TMP + 2048 + i * 1024, 1024) for i in range(2)]
        w_nat = at(A_TMP + 4096, STRIPS * HID)
        w_int = at(A_TMP + 4096 + STRIPS * HID, STRIPS * HID // 2).bitcast(I16)
        w_tmp = [at(A_TMP + 4096 + STRIPS * HID * 3 // 2 + i * 512, 512) for i in range(2)]
        fz, fabs, fexp, fln, lf, csum, eneg = [
            at(A_TMP + i * P, P).rearrange("p (s b h) -> p s b h", s=HALVES, b=BATCH) for i in range(7)]
        a_row = at(A_TMP + 1024, SEQ)[0:BATCH * NH, :]
        max_bc = [at(A_TMP + i * 1024, 1024).rearrange("p (h s) -> p h s", h=NH) for i in range(2)]
        max_hi = [at(A_TMP + 2048 + i * 512, 512).rearrange("p (h s) -> p h s", h=NH) for i in range(2)]
        decay = [at(A_TMP + 3072 + i * SCORES, SCORES) for i in range(2)]
        v_raw = [at(A_TMP + 6144 + i * 1024, 1024) for i in range(2)]
        v_aug = [at(A_TMP + 8192 + i * 528, 528).rearrange("p (s h c) -> p s h c", s=HALVES, h=NH) for i in range(2)]
        head = [at(A_TMP + 9248 + i * 512, 512) for i in range(2)]
        square = at(A_TMP + 10272, 512)
        xn = [at(A_TMP + 10784 + i * 512, 512) for i in range(2)]
        x_int = [at(A_TMP + i * 512, 512).bitcast(I16) for i in range(2)]
        xq = arena[:, A_X:A_X + 8192].bitcast(F16)
        wg_free = wg_parts[:, :, :, :].rearrange("p i k f -> p (i k f)").bitcast(I16)
        wu_free = wu_parts[:, :, :, :].rearrange("p i k f -> p (i k f)").bitcast(I16)
        gq_buf = [wg_free[:, j * PAIRC:(j + 1) * PAIRC] for j in range(FP)]
        gsq_buf = gq_buf
        uq_buf = [wu_free[:, j * PAIRC:(j + 1) * PAIRC] for j in range(FP)]
        o_parts = [at(i * SLOT, SLOT).bitcast(F16) for i in range(2)]
        o_int = [at(2 * SLOT + i * SLOT // 4, SLOT // 4).bitcast(I16) for i in range(2)]
        x1_in = [at(3 * SLOT + i * 1024, 1024) for i in range(2)]
        y_out = [at(6 * SLOT + i * 1024, 1024) for i in range(2)]

        x_res = at(A_X, BATCH * HALVES * HID)

        SX, INV_X, CG, SG, INV_G, SGK, CU, SU, INV_U, SGS, INV_GS, SO_, SO, INV_O, CO, WMUL, WFAC, WP2, SGU = range(19)

        def col(i):
            return sc[:, i:i + 1]

        psum = es.enter_context(nc.psum_tensor("psum", [P, 8, CH], F32))
        bank = [psum[:, i, :] for i in range(8)]
        bank_pair = [psum[:, 2 * i:2 * i + 2, :].rearrange("p i n -> p (i n)") for i in range(4)]
        ORDER = [4, 5, 6, 7, 0, 1, 2, 3]
        O_SLOTS = [8, 9, 10, 11, 12, 13, 4, 5]
        passed = sem("passed")
        consts_loaded = sem("consts_loaded")
        w_loaded = sem("w_loaded")
        consts_set = sem("consts_set")
        tri_zero = sem("tri_zero")
        ident_zero = sem("ident_zero")
        w_bmax = sem("w_bmax")
        w_rowmax = sem("w_rowmax")
        w_allmax = sem("w_allmax")
        w_inv = sem("w_inv")
        w_s = sem("w_s")
        w_div = sem("w_div")
        w_intd = sem("w_intd")
        w_dq = sem("w_dq")
        w_p2 = sem("w_p2")
        w_p2g = sem("w_p2g")
        w_rcp = sem("w_rcp")
        w_fac = sem("w_fac")
        w_tr = sem("w_tr")
        w_sc = sem("w_sc")
        w_hi = sem("w_hi")
        w_parts = sem("w_parts")
        stats_raw = sem("stats_raw")
        stats_done = sem("stats_done")
        rstd_eps = sem("rstd_eps")
        rstd_ready = sem("rstd_ready")
        q_ready = sem("q_ready")
        q_trans = sem("q_trans")
        qt_ready = sem("qt_ready")
        gates_done = sem("gates_done")
        gates_evac = sem("gates_evac")
        scores_ready = sem("scores_ready")
        scores_evac = sem("scores_evac")
        ctxw_zero = sem("ctxw_zero")
        ctxw_ready = sem("ctxw_ready")
        m_fz = sem("m_fz")
        m_abs = sem("m_abs")
        m_exp = sem("m_exp")
        m_ln = sem("m_ln")
        m_lf = sem("m_lf")
        m_ib = sem("m_ib")
        m_cs = sem("m_cs")
        m_csc = sem("m_csc")
        m_a = sem("m_a")
        m_at = sem("m_at")
        m_ac = sem("m_ac")
        m_scan = sem("m_scan")
        m_max_stored = sem("m_max_stored")
        m_mt = sem("m_mt")
        m_add = sem("m_add")
        m_floor = sem("m_floor")
        masked = sem("masked")
        v_ready = sem("v_ready")
        exp_done = sem("exp_done")
        c_ready = sem("c_ready")
        pv_done = sem("pv_done")
        cols_ready = sem("cols_ready")
        head_ready = sem("head_ready")
        sq_ready = sem("sq_ready")
        ssq_ready = sem("ssq_ready")
        n_half = sem("n_half")
        n_ready = sem("n_ready")
        w_ready = sem("w_ready")
        w2_ready = sem("w2_ready")
        var_ready = sem("var_ready")
        gain_ready = sem("gain_ready")
        y_ready = sem("y_ready")
        ys_ready = sem("ys_ready")
        x1_ready = sem("x1_ready")
        bn2_raw = sem("bn2_raw")
        bn2_done = sem("bn2_done")
        rstd2_eps = sem("rstd2_eps")
        rstd2_ready = sem("rstd2_ready")
        xn_ready = sem("xn_ready")
        xnt_psum = sem("xnt_psum")
        xnt_ready = sem("xnt_ready")
        xmax_ready = sem("xmax_ready")
        x1_stored = sem("x1_stored")
        red_x = sem("red_x")
        all_x = sem("all_x")
        sx0 = sem("sx0")
        sx1 = sem("sx1")
        inv_x0 = sem("inv_x0")
        inv_x = sem("inv_x")
        xi_ready = sem("xi_ready")
        x_hi = sem("x_hi")
        xq_ready = sem("xq_ready")
        g_psum = sem("g_psum")
        g_evac = sem("g_evac")
        gmax_done = sem("gmax_done")
        red_g = sem("red_g")
        all_g = sem("all_g")
        sg0 = sem("sg0")
        sg1 = sem("sg1")
        sg2 = sem("sg2")
        inv_g = sem("inv_g")
        u_psum = sem("u_psum")
        u_evac = sem("u_evac")
        umax_done = sem("umax_done")
        gq_ready = sem("gq_ready")
        sig_ready = sem("sig_ready")
        sigq_ready = sem("sigq_ready")
        gs_ready = sem("gs_ready")
        gsmax_done = sem("gsmax_done")
        red_gs = sem("red_gs")
        all_gs = sem("all_gs")
        sgs0 = sem("sgs0")
        inv_gs = sem("inv_gs")
        red_u = sem("red_u")
        all_u = sem("all_u")
        su0 = sem("su0")
        su1 = sem("su1")
        su2 = sem("su2")
        sgu = sem("sgu")
        inv_u = sem("inv_u")
        uq_ready = sem("uq_ready")
        gsq_ready = sem("gsq_ready")
        o_ready = sem("o_ready")
        omax_done = sem("omax_done")
        red_o = sem("red_o")
        all_o = sem("all_o")
        so0 = sem("so0")
        so1 = sem("so1")
        so2 = sem("so2")
        inv_o = sem("inv_o")
        co_ready = sem("co_ready")
        oi_ready = sem("oi_ready")
        o_hi = sem("o_hi")
        op_ready = sem("op_ready")
        y_psum = sem("y_psum")
        yo_ready = sem("yo_ready")
        x_loaded = [sem(f"x_loaded{i}") for i in range(2)]
        max_loaded = [sem(f"max_loaded{i}") for i in range(2)]
        v_loaded = [sem(f"v_loaded{i}") for i in range(2)]
        up_spilled = [sem(f"up_spilled{i}") for i in range(4)]
        up_back = [sem(f"up_back{i}") for i in range(4)]
        x1_back = [sem(f"x1_back{i}") for i in range(2)]
        y_stored = [sem(f"y_stored{i}") for i in range(2)]

        def due(count):
            return not isinstance(count, int) or count > 0

        def apart(eng, count):
            if not isinstance(count, int):
                eng.sem_inc(passed, 1)

        def over_batches(eng, steps, tail=0):
            for b in range(UNROLL):
                steps(b, b)
            with eng.Fori(1, BATCH // UNROLL) as it:
                for u in range(UNROLL):
                    steps(it * UNROLL + u, u)
            for b in range(BATCH, BATCH + tail):
                steps(b, b % UNROLL)

        def lagging(part, lag, b, u):
            n = b - lag
            if isinstance(b, int) and not 0 <= n < BATCH:
                return
            part(n, (u - lag) % UNROLL)

        def over_chunks(eng, steps, tail):
            steps(0)
            with eng.Fori(1, CHUNKS) as c:
                steps(c)
            for c in range(CHUNKS, CHUNKS + tail):
                steps(c)

        def place(h):
            return (h % 2) * 2 + h // 2

        def x_of(n, half):
            off = A_X + n * (HALVES * HID) + half * HID
            return at(off, HID) if isinstance(n, int) else at_dyn(off, HID)

        def x_batch(n):
            off = A_X + n * (HALVES * HID)
            return at(off, HALVES * HID) if isinstance(n, int) else at_dyn(off, HALVES * HID)

        def scores_of(n, off, size):
            o = n * SCORES + off
            return at(o, size) if isinstance(n, int) else at_dyn(o, size)

        def chunk_xq(c, part, k):
            o = c * (4 * CH) + part * (2 * CH) + k * CH
            return xq[:, o:o + CH] if isinstance(c, int) else xq[:, bass.ds(o, CH)]

        block = es.enter_context(nc.Block())

        @block.sync
        def _(sp):
            sp.dma_start(gate_w_raw[:, :, :].rearrange("p k g -> p (k g)"), gate_w).then_inc(consts_loaded, 16)
            sp.dma_start(gate_bias[:, :], gate_b.partition_broadcast(P)).then_inc(consts_loaded, 16)
            sp.dma_start(scale_row[:, :], norm_scale.partition_broadcast(P)).then_inc(consts_loaded, 16)

            def x_pair(b):
                off = A_X + b * (HALVES * HID)
                return at(off, PAIR * HALVES * HID) if isinstance(b, int) else at_dyn(off, PAIR * HALVES * HID)

            def dram_pair(t, pair):
                return t[pair, :, :] if isinstance(pair, int) else t[bass.ds(pair, 1), :, :].rearrange("a p n -> (a p) n")

            def load_inputs(g):
                for p in range(UNROLL // PAIR):
                    pair, b = g * (UNROLL // PAIR) + p, g * UNROLL + p * PAIR
                    if due((b - 2) * 2):
                        sp.wait_ge(scores_ready, (b - 2) * 2)
                    sp.dma_start(x_pair(b), dram_pair(x, pair)).then_inc(x_loaded[p], 16)
                    sp.dma_start(ctx_t_sb[p], dram_pair(ctx_t, pair)).then_inc(x_loaded[p], 16)

            load_inputs(0)
            for i, w in enumerate((w_gate, w_up)):
                sp.dma_start(w_nat[:, i * FT * HID:(i + 1) * FT * HID].rearrange("p (s k) -> p s k", k=HID),
                             w.rearrange("(s p) k -> p s k", p=P)).then_inc(w_loaded, 16)
            sp.dma_start(w_nat[:, 2 * FT * HID:].rearrange("p (r k) -> p r k", k=FF),
                         w_down.rearrange("(r p) k -> p r k", p=P)).then_inc(w_loaded, 16)
            with sp.Fori(1, BATCH // UNROLL) as g:
                load_inputs(g)

            sp.wait_ge(m_scan, 1)
            sp.dma_start(max_dram, run_max[:, :]).then_inc(m_max_stored, 16)
            sp.wait_ge(m_max_stored, 16)
            sp.wait_ge(m_floor, 1)
            sp.wait_ge(w_parts, 9)

            def loads3(g):
                for u in range(UNROLL):
                    n, p = g * UNROLL + u, u // PAIR
                    if u % PAIR == 0:
                        if due(n - 2):
                            sp.wait_ge(v_ready, n - 2)
                        sp.dma_start(v_raw[p], dram_pair(ctx_nat, g * (UNROLL // PAIR) + p)).then_inc(v_loaded[p], 16)
                    if due(n - 1):
                        sp.wait_ge(exp_done, n - 1)
                    rows = max_dram[n * NH:(n + 1) * NH, :] if isinstance(n, int) else max_dram[bass.ds(n * NH, NH), :]
                    sp.dma_start(max_bc[u % 2].rearrange("p h s -> p (h s)"),
                                 rows.rearrange("h s -> (h s)").partition_broadcast(P)).then_inc(max_loaded[u % 2], 16)
                    if u % PAIR == 1:
                        store_x1(g - 1, u)

            def store_x1(g, u):
                if isinstance(g, int) and g < 0:
                    return
                n = g * UNROLL + u
                sp.wait_ge(x1_ready, n + 1)
                sp.dma_start(dram_pair(x1_dram, g * (UNROLL // PAIR) + u // PAIR), x_pair(n - 1)).then_inc(x1_stored, 16)

            loads3(0)
            with sp.Fori(1, BATCH // UNROLL) as g:
                loads3(g)
            for u in range(1, UNROLL, PAIR):
                store_x1(BATCH // UNROLL - 1, u)

            for c in range(4):
                sp.wait_ge(umax_done, (c + 1) * FP)
                sp.dma_start(up_dram[c, :, :], at((c + 8) * SLOT, SLOT)).then_inc(up_spilled[c], 16)
            for c in range(4):
                sp.wait_ge(up_spilled[c], 16)
            sp.wait_ge(u_psum, CHUNKS * FP)
            for c in range(4):
                if c >= 2:
                    if due(FP * (c - 1)):
                        sp.wait_ge(o_ready, FP * (c - 1))
                sp.dma_start(at(O_SLOTS[c + 4] * SLOT, SLOT), up_dram[c, :, :]).then_inc(up_back[c], 16)

            sp.wait_ge(omax_done, CHUNKS * FP)
            def store_y(k):
                sp.wait_ge(yo_ready, (k + 1) * 4)
                sp.dma_start(out[ORDER[k], :, :], y_out[k % 2]).then_inc(y_stored[k % 2], 16)

            for k in range(CHUNKS):
                if due((k - 1) * 4):
                    sp.wait_ge(yo_ready, (k - 1) * 4)
                sp.dma_start(x1_in[k % 2], x1_dram[ORDER[k], :, :]).then_inc(x1_back[k % 2], 16)
                if k >= 1:
                    store_y(k - 1)
            store_y(CHUNKS - 1)
            for i in range(2):
                sp.wait_ge(y_stored[i], 16 * CHUNKS // 2)

        @block.gpsimd
        def _(pool):
            pool.memset(ident[:, :], 0.0).then_inc(ident_zero, 1)
            pool.memset(tri[:, :], 1.0).then_inc(tri_zero, 1)
            pool.memset(ones[:, :], 1.0)
            pool.memset(minus_half[:, :], -0.5)
            pool.wait_ge(ident_zero, 1)
            pool.affine_select(out=ident[:, :], in_=ident[:, :], compare_op=ALU.not_equal, fill=1.0, base=0,
                               pattern=[[-1, P]], channel_multiplier=1)
            pool.wait_ge(tri_zero, 1)
            pool.affine_select(out=tri[:, :], in_=tri[:, :], compare_op=ALU.is_ge, fill=0.0, base=0,
                               pattern=[[1, P]], channel_multiplier=-1).then_inc(consts_set, 1)

            def rstd1(n, v):
                s = v % 2
                pool.wait_ge(stats_done, n + 1)
                apart(pool, n + 1)
                pool.tensor_scalar(rstd[:, s, :, :], mean_var[:, s, :, 1:2], LN_EPS, None, ALU.add).then_inc(rstd_eps, 1)
                pool.wait_ge(rstd_eps, n + 1)
                apart(pool, n + 1)
                pool.tensor_tensor(rstd[:, s, :, 0], rstd[:, s, :, 0], minus_half[:, 0:HALVES], ALU.pow).then_inc(rstd_ready, 1)

            over_batches(pool, lambda b, u: lagging(rstd1, 0, b, u), 0)

            pool.wait_ge(w_rowmax, 1)
            pool.partition_all_reduce(allmax[:, 0:1], red[:, 0:1], P, bass.bass_isa.ReduceOp.max).then_inc(w_allmax, 1)

            pool.wait_ge(m_floor, 1)
            pool.wait_ge(w_parts, 9)
            for i in range(2):
                pool.memset(v_aug[i][:, :, :, DH:DH + 1], 1.0)

            def prepare(n, v):
                s, p = v % 2, v // PAIR
                it16 = (n // UNROLL + 1) * 16 if isinstance(n, int) else None
                pool.wait_ge(v_loaded[p], it16 if it16 is not None else group_count(n, v))
                apart(pool, it16 if it16 is not None else group_count(n, v))
                if due(n - 1):
                    pool.wait_ge(pv_done, n - 1)
                    apart(pool, n - 1)
                raw = v_raw[p][:, (v % PAIR) * 512:(v % PAIR + 1) * 512]
                pool.tensor_copy(v_aug[s][:, :, :, 0:DH], raw.rearrange("p (s h c) -> p s h c", s=HALVES, h=NH))
                mean = gates[:, :, n, 2 * NH:GC] if isinstance(n, int) else gates[:, :, bass.ds(n, 1), 2 * NH:GC].rearrange("p s b h -> p s (b h)")
                pool.tensor_copy(v_aug[s][:, :, :, DH + 1], mean).then_inc(v_ready, 1)
                m16 = (n // 2 + 1) * 16 if isinstance(n, int) else group_count2(n, v)
                pool.wait_ge(max_loaded[s], m16)
                apart(pool, m16)
                pool.affine_select(out=max_hi[s], in_=max_bc[s][:, :, P:SEQ], compare_op=ALU.is_ge, fill=NEVER, base=0,
                                   pattern=[[0, NH], [1, P]], channel_multiplier=-1)
                pool.affine_select(out=max_bc[s][:, :, 0:P], in_=max_bc[s][:, :, 0:P], compare_op=ALU.is_ge, fill=NEVER,
                                   base=0, pattern=[[0, NH], [1, P]], channel_multiplier=-1).then_inc(masked, 1)

            reg = [None]

            def group_count(n, v):
                return reg[0] * 16 + 16

            def group_count2(n, v):
                return reg[0] * 32 + (v // 2 + 1) * 16

            def gain(n, v):
                s = v % 2
                pool.wait_ge(var_ready, n + 1)
                apart(pool, n + 1)
                pool.tensor_tensor(head_gain[:, s, :], head_var[:, s, :], minus_half[:, :], ALU.pow).then_inc(gain_ready, 1)

            def residual(n, v):
                s = v % 2
                pool.wait_ge(y_ready, n + 1)
                apart(pool, n + 1)
                h2 = head[s].rearrange("p (s c) -> p s c", s=HALVES)
                pool.tensor_tensor(h2, h2, scale_row[:, :].unsqueeze(1).broadcast_to([P, HALVES, HID]), ALU.mult).then_inc(ys_ready, 1)
                pool.wait_ge(ys_ready, n + 1)
                apart(pool, n + 1)
                pool.tensor_tensor(x_batch(n), x_batch(n), head[s], ALU.add).then_inc(x1_ready, 1)

            def rstd2(n, v):
                s = v % 2
                pool.wait_ge(bn2_done, n + 1)
                apart(pool, n + 1)
                pool.tensor_scalar(rstd[:, s, :, :], mean_var[:, s, :, 1:2], LN_EPS, None, ALU.add).then_inc(rstd2_eps, 1)
                pool.wait_ge(rstd2_eps, n + 1)
                apart(pool, n + 1)
                pool.tensor_tensor(rstd[:, s, :, 0], rstd[:, s, :, 0], minus_half[:, 0:HALVES], ALU.pow).then_inc(rstd2_ready, 1)

            def step3(b, u):
                lagging(prepare, 0, b, u)
                lagging(rstd2, 3, b, u)
                lagging(residual, 2, b, u)
                lagging(gain, 1, b, u)

            for b in range(UNROLL):
                step3(b, b)
            with pool.Fori(1, BATCH // UNROLL) as it:
                reg[0] = it
                for u in range(UNROLL):
                    step3(it * UNROLL + u, u)
            for b in range(BATCH, BATCH + 3):
                step3(b, b % UNROLL)

            def over_partitions(i, local, everywhere):
                pool.wait_ge(local, 1)
                pool.partition_all_reduce(allmax[:, i:i + 1], red[:, i:i + 1], P, bass.bass_isa.ReduceOp.max).then_inc(everywhere, 1)

            over_partitions(1, red_x, all_x)
            over_partitions(2, red_g, all_g)
            over_partitions(3, red_gs, all_gs)
            over_partitions(4, red_u, all_u)
            over_partitions(5, red_o, all_o)

        @block.scalar
        def _(act):
            def evac_gates(n, v):
                act.wait_ge(gates_done, n + 1)
                apart(act, n + 1)
                dst = gates[:, :, n, :] if isinstance(n, int) else gates[:, :, bass.ds(n, 1), :].rearrange("p s b g -> p s (b g)")
                act.activation(dst, bank[2][:, 0:HALVES * GC].rearrange("p (s g) -> p s g", s=HALVES), ACT.Copy).then_inc(gates_evac, 1)

            def evac_scores(n, v):
                for key_half in range(HALVES):
                    width = 2 * (SEQ - key_half * P)
                    act.wait_ge(scores_ready, n * 2 + (key_half + 1))
                    apart(act, n * 2 + (key_half + 1))
                    act.activation(scores_of(n, key_half * NH * SEQ, 2 * width).rearrange("p (i n) -> p i n", i=2),
                                   psum[:, 3 + 2 * key_half:5 + 2 * key_half, 0:width], ACT.Copy,
                                   scale=DH ** -0.5).then_inc(scores_evac, 1)

            def step1(b, u):
                lagging(evac_gates, 1, b, u)
                lagging(evac_scores, 1, b, u)

            over_batches(act, step1, 1)

            act.wait_ge(w_fac, 1)
            for r in range(9):
                act.wait_ge(w_tr, r + 1)
                apart(act, r + 1)
                if due(r - 1):
                    act.wait_ge(w_parts, r - 1)
                    apart(act, r - 1)
                act.activation(w_tmp[r % 2], bank[7 - 7 * (r % 2)][:, :], ACT.Copy, scale=col(WMUL)).then_inc(w_sc, 1)

            act.wait_ge(m_fz, 1)
            act.activation(fabs, fz, ACT.Abs).then_inc(m_abs, 1)
            act.wait_ge(m_abs, 1)
            act.activation(fexp, fabs, ACT.Exp, scale=-1.0).then_inc(m_exp, 1)
            act.wait_ge(m_exp, 1)
            act.activation(fln, fexp, ACT.Ln, bias=1.0).then_inc(m_ln, 1)
            act.wait_ge(m_add, 1)
            act.activation(floor_nat[:, :, :], eneg.rearrange("p s b h -> p s (b h)"), ACT.Exp, scale=-1.0).then_inc(m_floor, 1)

            def a_col(half, n, h):
                return a_nat[:, half, n * NH + h:n * NH + h + 1] if isinstance(n, int) else \
                    a_nat[:, half, bass.ds(n * NH + h, 1)]

            def decays(n, v):
                s = v % 2
                act.wait_ge(masked, n + 1)
                apart(act, n + 1)
                if due(n - 1):
                    act.wait_ge(pv_done, n - 1)
                    apart(act, n - 1)
                for h in range(NH):
                    act.activation(decay[s][:, place(h) * SEQ:(place(h) + 1) * SEQ], max_bc[s][:, h, :], ACT.Exp,
                                   bias=a_col(0, n, h), scale=-1.0)
                for h in range(NH):
                    last = act.activation(decay[s][:, NH * SEQ + place(h) * P:NH * SEQ + (place(h) + 1) * P], max_hi[s][:, h, :], ACT.Exp,
                                          bias=a_col(1, n, h), scale=-1.0)
                last.then_inc(exp_done, 1)

            def squares(n, v):
                act.wait_ge(head_ready, n + 1)
                apart(act, n + 1)
                if due(n):
                    act.wait_ge(ssq_ready, n)
                    apart(act, n)
                act.activation(square, head[v % 2], ACT.Square).then_inc(sq_ready, 1)

            def evac_xnt(n, v):
                act.wait_ge(xnt_psum, n + 1)
                apart(act, n + 1)
                act.activation(scores_of(n, 0, 512), bank[4 + v % 2][:, :], ACT.Copy).then_inc(xnt_ready, 1)

            def step3(b, u):
                lagging(decays, 0, b, u)
                lagging(squares, 1, b, u)
                lagging(evac_xnt, 4, b, u)

            over_batches(act, step3, 4)

            def quant_x(c):
                o = c * (PAIR * SCORES)
                v = at(o, PAIR * SCORES) if isinstance(c, int) else at_dyn(o, PAIR * SCORES)
                if due(c):
                    act.wait_ge(xq_ready, c)
                    apart(act, c)
                act.activation(x_int[0].rearrange("p (k b t) -> p b k t", k=KT, b=PAIR),
                               v.rearrange("p (b n) -> p b n", b=PAIR)[:, :, 0:512].rearrange("p b (k t) -> p b k t", k=KT),
                               ACT.Copy, scale=col(INV_X)).then_inc(xi_ready, 1)

            def evac_proj(psum_sem, evac_sem, c, slot):
                for j in range(FP):
                    act.wait_ge(psum_sem, c * FP + (j + 1))
                    apart(act, c * FP + (j + 1))
                    act.activation(slot_pair(slot, j), bank_pair[j], ACT.Copy).then_inc(evac_sem, 1)

            act.wait_ge(inv_x, 1)
            quant_x(0)
            with act.Fori(1, CHUNKS) as c:
                quant_x(c)
                evac_proj(g_psum, g_evac, c - 1, c - 1)
            evac_proj(g_psum, g_evac, CHUNKS - 1, CHUNKS - 1)

            def gate_chain(c):
                for j in range(FP):
                    g = slot_pair(c, j)
                    if due(c * FP + (j - 2)):
                        act.wait_ge(gs_ready, c * FP + (j - 2))
                        apart(act, c * FP + (j - 2))
                    act.activation(gq_buf[j], g, ACT.Copy, scale=col(INV_G)).then_inc(gq_ready, 1)
                    act.wait_ge(gq_ready, c * FP + (j + 1))
                    apart(act, c * FP + (j + 1))
                    act.activation(g, gq_buf[j], ACT.Sigmoid, scale=col(SG)).then_inc(sig_ready, 1)

            act.wait_ge(inv_g, 1)
            gate_chain(0)
            evac_proj(u_psum, u_evac, 0, 8)
            with act.Fori(1, 4) as c:
                gate_chain(c)
                evac_proj(u_psum, u_evac, c, c + 8)
            for c in range(4, CHUNKS):
                gate_chain(c)
                act.wait_ge(up_spilled[c - 4], 16)
                evac_proj(u_psum, u_evac, c, c + 4)

            def quant_u(k, slot):
                for j in range(FP):
                    if due(k * FP + (j - 2)):
                        act.wait_ge(o_ready, k * FP + (j - 2))
                        apart(act, k * FP + (j - 2))
                    act.activation(uq_buf[j], slot_pair(slot, j), ACT.Copy, scale=col(INV_U)).then_inc(uq_ready, 1)

            act.wait_ge(inv_u, 1)
            quant_u(0, O_SLOTS[0])
            with act.Fori(1, 4) as k:
                quant_u(k, k + 8)
            for k in range(4, CHUNKS):
                act.wait_ge(up_back[k - 4], 16)
                quant_u(k, O_SLOTS[k])

            act.wait_ge(inv_o, 1)
            for k in range(CHUNKS):
                for j in range(2):
                    if due(2 * k + j - 1):
                        act.wait_ge(op_ready, 2 * k + j - 1)
                        apart(act, 2 * k + j - 1)
                    act.activation(o_int[j], at(O_SLOTS[k] * SLOT + j * SLOT // 2, SLOT // 2), ACT.Copy,
                                   scale=col(INV_O)).then_inc(oi_ready, 1)

        @block.tensor
        def _(pe):
            pe.wait_ge(consts_set, 1)
            pe.wait_ge(ctxw_ready, 1)

            def transposes(n, v):
                s = v % 2
                pe.wait_ge(q_ready, n + 1)
                for k in range(KT):
                    for half in range(HALVES):
                        last = pe.transpose(bank[s][:, k * SEQ + half * P:k * SEQ + (half + 1) * P],
                                            q_nat[s][:, half * HID + k * P:half * HID + (k + 1) * P], ident[:, :])
                last.then_inc(q_trans, 1)

            def gates_and_scores(n, v):
                s, p = v % 2, v // PAIR
                ct = ctx_t_sb[p][:, (v % PAIR) * 512:(v % PAIR + 1) * 512].rearrange("p (k t) -> p k t", k=KT)
                if due(n):
                    pe.wait_ge(gates_evac, n)
                pe.wait_ge(qt_ready, n + 1)
                for half in range(HALVES):
                    o = bank[2][:, half * GC:(half + 1) * GC]
                    t = slice(half * P, (half + 1) * P)
                    for k in range(KT):
                        pe.matmul(o, ct[:, k, t], ctx_gate_w[:, k, :], start=(k == 0), stop=False)
                    for k in range(KT):
                        last = pe.matmul(o[:, 0:2 * NH], q_t[s][:, k, t], gate_w_raw[:, k, :], start=False, stop=(k == KT - 1))
                last.then_inc(gates_done, 1)
                for key_half in range(HALVES):
                    if due((n - 1) * 2 + (key_half + 1)):
                        pe.wait_ge(scores_evac, (n - 1) * 2 + (key_half + 1))
                    width = SEQ - key_half * P
                    for h in range(NH):
                        r, odd = DH * (h % 2), h % 2
                        last = pe.matmul(bank[3 + 2 * key_half + odd][:, (h // 2) * width:(h // 2 + 1) * width],
                                         ct[r:r + DH, h // 2, key_half * P:(key_half + 1) * P],
                                         q_t[s][r:r + DH, h // 2, key_half * P:SEQ], start=True, stop=True)
                    last.then_inc(scores_ready, 1)

            def step1(b, u):
                lagging(transposes, 0, b, u)
                lagging(gates_and_scores, 1, b, u)

            over_batches(pe, step1, 1)

            pe.wait_ge(w_dq, 1)
            for r in range(9):
                if due(r - 1):
                    pe.wait_ge(w_sc, r - 1)
                for i in range(2):
                    for j in range(2):
                        if r < 6:
                            src = w_nat[:, ((r // 3) * 6 + 2 * (r % 3) + j) * HID + i * P:][:, 0:P]
                        else:
                            src = w_nat[:, 12 * HID + j * FF + (2 * (r - 6) + i) * P:][:, 0:P]
                        last = pe.transpose(bank[7 - 7 * (r % 2)][:, (2 * i + j) * P:(2 * i + j + 1) * P], src, ident[:, :])
                last.then_inc(w_tr, 1)

            pe.wait_ge(m_lf, 1)
            lfv = lf.rearrange("p s b h -> p s (b h)")
            C = BATCH * NH
            pe.matmul(bank[0][:, 0:C], tri[:, :], lfv[:, 0, :], start=True, stop=True)
            pe.matmul(bank[0][:, C:2 * C], tri[:, :], lfv[:, 1, :], start=True, stop=False)
            pe.matmul(bank[0][:, C:2 * C], ones[:, :], lfv[:, 0, :], start=False, stop=True).then_inc(m_cs, 1)
            pe.wait_ge(m_a, 1)
            for half in range(HALVES):
                last = pe.transpose(bank[1][0:C, half * P:(half + 1) * P], a_nat[:, half, :], ident[:, :])
            last.then_inc(m_at, 1)
            pe.wait_ge(m_scan, 1)
            for half in range(HALVES):
                last = pe.transpose(bank[2][:, half * C:(half + 1) * C], run_max[:, half * P:(half + 1) * P], ident[0:C, 0:C])
            last.then_inc(m_mt, 1)

            def weighted_sum(n, v):
                s = v % 2
                pe.wait_ge(c_ready, n + 1)
                pe.wait_ge(v_ready, n + 1)
                if due(n - 1):
                    pe.wait_ge(head_ready, n - 1)
                for half in range(HALVES):
                    for h in range(NH):
                        o = bank[2 * s + half][:, h * VC:(h + 1) * VC]
                        pe_last = pe.matmul(o, decay[s][:, place(h) * SEQ + half * P:place(h) * SEQ + (half + 1) * P],
                                            v_aug[s][:, 0, h, :], start=True, stop=(half == 0))
                        if half == 1:
                            pe_last = pe.matmul(o, decay[s][:, NH * SEQ + place(h) * P:NH * SEQ + (place(h) + 1) * P],
                                                v_aug[s][:, 1, h, :], start=False, stop=True)
                pe_last.then_inc(pv_done, 1)

            def xn_transposes(n, v):
                s = v % 2
                pe.wait_ge(xn_ready, n + 1)
                if due(n):
                    pe.wait_ge(xnt_ready, n)
                for k in range(KT):
                    for half in range(HALVES):
                        last = pe.transpose(bank[4 + s][:, k * SEQ + half * P:k * SEQ + (half + 1) * P],
                                            xn[s][:, half * HID + k * P:half * HID + (k + 1) * P], ident[:, :])
                last.then_inc(xnt_psum, 1)

            def step3(b, u):
                lagging(weighted_sum, 0, b, u)
                lagging(xn_transposes, 3, b, u)

            over_batches(pe, step3, 3)

            def project(parts, sem_name, evac_name):
                def f(c):
                    for j in range(FP):
                        if due((c - 1) * FP + (j + 1)):
                            pe.wait_ge(evac_name, (c - 1) * FP + (j + 1))
                        for i in range(2):
                            ft = 2 * j + i
                            for n, (wp, xp) in enumerate(((0, 0), (0, 1), (1, 0))):
                                for k in range(KT):
                                    last = pe.matmul(bank[ft][:, :], parts[:, wp, k, ft * P:(ft + 1) * P], chunk_xq(c, xp, k),
                                                     start=(n == 0 and k == 0), stop=(n == 2 and k == KT - 1))
                        last.then_inc(sem_name, 1)
                return f

            gate_of = project(wg_parts, g_psum, g_evac)
            up_of = project(wu_parts, u_psum, u_evac)
            pe.wait_ge(w_parts, 9)
            pe.wait_ge(xnt_ready, BATCH)
            pe.wait_ge(xq_ready, 1)
            gate_of(0)
            with pe.Fori(1, CHUNKS) as c:
                pe.wait_ge(xq_ready, c + 1)
                gate_of(c)
            pe.wait_ge(g_evac, CHUNKS * FP)
            up_of(0)
            with pe.Fori(1, CHUNKS) as c:
                up_of(c)

            def down(n, v):
                pe.wait_ge(op_ready, 2 * n + 2)
                for t in range(4):
                    if due(4 * n + (t - 3)):
                        pe.wait_ge(yo_ready, 4 * n + (t - 3))
                    for q, (op, wp) in enumerate(((0, 0), (0, 1), (1, 0))):
                        for k in range(FT):
                            o = (op * FT + k) * CH + t * P
                            last = pe.matmul(bank[t][:, 0:HID], o_parts[v][:, o:o + P], wd_parts[:, wp, k, :],
                                             start=(q == 0 and k == 0), stop=(q == 2 and k == FT - 1))
                    last.then_inc(y_psum, 1)

            pe.wait_ge(u_evac, CHUNKS * FP)
            for v in range(2):
                down(v, v)
            with pe.Fori(1, CHUNKS // 2) as g:
                for v in range(2):
                    down(g * 2 + v, v)

        @block.vector
        def _(dve):
            dve.wait_ge(consts_loaded, 48)
            dve.memset(ctx_gate_w[:, :, 2 * NH:GC], 0.0).then_inc(ctxw_zero, 1)
            dve.wait_ge(ctxw_zero, 1)
            for h in range(NH):
                dve.memset(ctx_gate_w[(h % 2) * DH:(h % 2 + 1) * DH, h // 2, 2 * NH + h:2 * NH + h + 1], 1.0 / DH)
            dve.tensor_tensor(ctx_gate_w[:, :, 0:2 * NH], gate_w_raw[:, KT:2 * KT, :], gate_w_raw[:, 2 * KT:3 * KT, :],
                              ALU.add).then_inc(ctxw_ready, 1)

            reg = [None]

            def stats(n, v):
                s, p = v % 2, v // PAIR
                dve.wait_ge(x_loaded[p], 32 * (n // UNROLL + 1) if isinstance(n, int) else reg[0] * 32 + 32)
                for half in range(HALVES):
                    last = dve.bn_stats(bn_raw[:, s, half, :], x_of(n, half))
                last.then_inc(stats_raw, 1)
                dve.wait_ge(stats_raw, n + 1)
                apart(dve, n + 1)
                for half in range(HALVES):
                    last = dve.bn_aggr(mean_var[:, s, half, :], bn_raw[:, s, half, :])
                last.then_inc(stats_done, 1)

            def norm_q(n, v):
                s = v % 2
                dve.wait_ge(rstd_ready, n + 1)
                for half in range(HALVES):
                    last = dve.tensor_scalar(q_nat[s][:, half * HID:(half + 1) * HID], x_of(n, half),
                                             mean_var[:, s, half, 0:1], rstd[:, s, half, 0:1], ALU.subtract, ALU.mult)
                last.then_inc(q_ready, 1)

            def evac_qt(n, v):
                s = v % 2
                dve.wait_ge(q_trans, n + 1)
                if due((n - 1) * 2):
                    dve.wait_ge(scores_ready, (n - 1) * 2)
                dve.tensor_copy(q_t[s].rearrange("p k t -> p (k t)"), bank[s][:, :]).then_inc(qt_ready, 1)

            def step1(b, u):
                lagging(stats, 0, b, u)
                lagging(evac_qt, 1, b, u)
                lagging(norm_q, 0, b, u)

            for b in range(UNROLL):
                step1(b, b)
            with dve.Fori(1, BATCH // UNROLL) as it:
                reg[0] = it
                for u in range(UNROLL):
                    step1(it * UNROLL + u, u)
            step1(BATCH, 0)

            dve.wait_ge(w_loaded, 48)
            w3 = w_nat.rearrange("p (b k) -> p b k", k=BLOCK)
            dve.tensor_reduce(block_max[:, :], w3, AX.X, ALU.max, apply_absolute_value=True).then_inc(w_bmax, 1)
            dve.wait_ge(w_bmax, 1)
            dve.tensor_reduce(red[:, 0:1], block_max[:, :], AX.X, ALU.max).then_inc(w_rowmax, 1)
            dve.tensor_scalar(block_s[:, :], block_max[:, :], 1.0 / QMAX4, TINY, ALU.mult, ALU.max).then_inc(w_s, 1)
            dve.wait_ge(w_s, 1)
            dve.reciprocal(block_inv[:, :], block_s[:, :]).then_inc(w_inv, 1)
            dve.wait_ge(w_inv, 1)
            s_bc = block_s[:, :].unsqueeze(2).broadcast_to([P, STRIPS * 8, BLOCK])
            wi3 = w_int.rearrange("p (b k) -> p b k", k=BLOCK)
            inv_bc = block_inv[:, :].unsqueeze(2).broadcast_to([P, STRIPS * 8, BLOCK])
            dve.tensor_tensor(w3, w3, inv_bc, ALU.mult).then_inc(w_div, 1)
            dve.wait_ge(w_div, 1)
            dve.tensor_copy(w_int, w_nat).then_inc(w_intd, 1)
            dve.wait_ge(w_intd, 1)
            dve.tensor_tensor(w3, wi3, s_bc, ALU.mult).then_inc(w_dq, 1)
            dve.wait_ge(w_allmax, 1)
            dve.tensor_scalar(sc[:, WP2:WP2 + 1].bitcast(U32), allmax[:, 0:1].bitcast(U32), 0x7F800000, None, ALU.bitwise_and).then_inc(w_p2, 1)
            dve.wait_ge(w_p2, 1)
            dve.tensor_scalar(col(WP2), col(WP2), 2.0 ** -100, None, ALU.max).then_inc(w_p2g, 1)
            dve.wait_ge(w_p2g, 1)
            dve.reciprocal(col(CO), col(WP2)).then_inc(w_rcp, 1)
            dve.wait_ge(w_rcp, 1)
            dve.tensor_scalar(col(WMUL), col(CO), W_UNIT, None, ALU.mult)
            dve.tensor_scalar(col(WFAC), col(WP2), 1.0 / W_UNIT, None, ALU.mult).then_inc(w_fac, 1)
            for r in range(9):
                dve.wait_ge(w_sc, r + 1)
                t4 = w_tmp[r % 2].rearrange("p (i n) -> p i n", i=2)
                if r < 6:
                    w = (wg_parts, wu_parts)[r // 3]
                    hi, lo = (w[:, i, :, 2 * (r % 3) * P:(2 * (r % 3) + 2) * P] for i in range(2))
                else:
                    hi, lo = (wd_parts[:, i, 2 * (r - 6):2 * (r - 6) + 2, :] for i in range(2))
                dve.tensor_copy(hi, t4).then_inc(w_hi, 1)
                dve.wait_ge(w_hi, r + 1)
                dve.tensor_tensor(lo, t4, hi, ALU.subtract).then_inc(w_parts, 1)

            dve.wait_ge(gates_evac, BATCH)
            bias_bc = lambda i: gate_bias[:, i * NH:(i + 1) * NH].unsqueeze(1).unsqueeze(1).broadcast_to([P, HALVES, BATCH, NH])
            dve.tensor_tensor(fz, gates[:, :, :, NH:2 * NH], bias_bc(1), ALU.add).then_inc(m_fz, 1)
            dve.wait_ge(m_fz, 1)
            dve.tensor_tensor(csum, gates[:, :, :, 0:NH], bias_bc(0), ALU.add).then_inc(m_ib, 1)
            dve.wait_ge(m_ln, 1)
            flat = lambda t: t.rearrange("p s b h -> p (s b h)")
            dve.scalar_tensor_tensor(flat(lf), flat(fz), 0.0, flat(fln), ALU.min, ALU.subtract).then_inc(m_lf, 1)
            dve.wait_ge(m_cs, 1)
            dve.wait_ge(m_ib, 1)
            dve.tensor_copy(flat(eneg), bank[0][:, 0:P]).then_inc(m_csc, 1)
            dve.wait_ge(m_csc, 1)
            dve.tensor_tensor(a_nat[:, :, :].rearrange("p s c -> p (s c)"), flat(csum), flat(eneg), ALU.subtract).then_inc(m_a, 1)
            dve.wait_ge(m_at, 1)
            dve.tensor_copy(a_row, bank[1][0:BATCH * NH, 0:SEQ]).then_inc(m_ac, 1)
            dve.wait_ge(m_ac, 1)
            dve.tensor_tensor_scan(run_max[:, :], a_row, a_row, -3.0e38, ALU.max, ALU.max).then_inc(m_scan, 1)
            dve.wait_ge(m_mt, 1)
            dve.tensor_tensor(flat(eneg), flat(eneg), bank[2][:, 0:P], ALU.add).then_inc(m_add, 1)

            def head_center(n, v):
                s = v % 2
                dve.wait_ge(pv_done, n + 1)
                for half in range(HALVES):
                    o = bank[2 * s + half][:, 0:NH * VC].rearrange("p (h c) -> p h c", h=NH)
                    last = dve.tensor_copy(o_cols[:, s, half * NH:(half + 1) * NH, :], o[:, :, DH:VC])
                last.then_inc(cols_ready, 1)
                dve.wait_ge(cols_ready, n + 1)
                if due(n - 1):
                    dve.wait_ge(x1_ready, n - 1)
                for half in range(HALVES):
                    o = bank[2 * s + half][:, 0:NH * VC].rearrange("p (h c) -> p h c", h=NH)
                    mean = o_cols[:, s, half * NH:(half + 1) * NH, 1:2].broadcast_to([P, NH, DH])
                    last = dve.tensor_tensor(head[s][:, half * HID:(half + 1) * HID].rearrange("p (h c) -> p h c", h=NH),
                                             o[:, :, 0:DH], mean, ALU.subtract)
                last.then_inc(head_ready, 1)
                fl = floor_nat[:, :, n * NH:(n + 1) * NH] if isinstance(n, int) else floor_nat[:, :, bass.ds(n * NH, NH)]
                dve.scalar_tensor_tensor(floor_n[:, s, :].rearrange("p (s h) -> p s h", s=HALVES),
                                         o_cols[:, s, :, 0].rearrange("p (s h) -> p s h", s=HALVES), -1.0, fl,
                                         ALU.mult, ALU.max).then_inc(n_half, 1)
                dve.wait_ge(n_half, n + 1)
                dve.tensor_tensor(floor_n[:, s, :], floor_n[:, s, :], o_cols[:, s, :, 0], ALU.max).then_inc(n_ready, 1)
                dve.wait_ge(n_ready, n + 1)
                dve.tensor_scalar(floor_w[:, s, :], floor_n[:, s, :], NORM_EPS, LN_EPS ** 0.5, ALU.add, ALU.mult).then_inc(w_ready, 1)

            def products(n, v):
                s = v % 2
                dve.wait_ge(exp_done, n + 1)
                dve.tensor_tensor(decay[s], decay[s], scores_of(n, 0, SCORES), ALU.mult).then_inc(c_ready, 1)

            def head_variance(n, v):
                s = v % 2
                dve.wait_ge(w_ready, n + 1)
                dve.tensor_tensor(floor_w2[:, s, :], floor_w[:, s, :], floor_w[:, s, :], ALU.mult)
                dve.wait_ge(sq_ready, n + 1)
                dve.tensor_reduce(sumsq[:, s, :], square.rearrange("p (g c) -> p g c", c=DH), AX.X, ALU.add).then_inc(ssq_ready, 1)
                dve.wait_ge(ssq_ready, n + 1)
                dve.scalar_tensor_tensor(head_var[:, s, :], sumsq[:, s, :], 1.0 / DH, floor_w2[:, s, :],
                                         ALU.mult, ALU.add).then_inc(var_ready, 1)

            def head_scale(n, v):
                s = v % 2
                dve.wait_ge(gain_ready, n + 1)
                h3 = head[s].rearrange("p (g c) -> p g c", c=DH)
                dve.tensor_tensor(h3, h3, head_gain[:, s, :].unsqueeze(2).broadcast_to([P, HALVES * NH, DH]),
                                  ALU.mult).then_inc(y_ready, 1)

            def stats2(n, v):
                s = v % 2
                dve.wait_ge(x1_ready, n + 1)
                for half in range(HALVES):
                    last = dve.bn_stats(bn_raw[:, s, half, :], x_of(n, half))
                last.then_inc(bn2_raw, 1)
                dve.wait_ge(bn2_raw, n + 1)
                apart(dve, n + 1)
                for half in range(HALVES):
                    last = dve.bn_aggr(mean_var[:, s, half, :], bn_raw[:, s, half, :])
                last.then_inc(bn2_done, 1)

            def norm2(n, v):
                s = v % 2
                dve.wait_ge(rstd2_ready, n + 1)
                if due(n):
                    dve.wait_ge(xnt_psum, n)
                for half in range(HALVES):
                    last = dve.tensor_scalar(xn[s][:, half * HID:(half + 1) * HID], x_of(n, half),
                                             mean_var[:, s, half, 0:1], rstd[:, s, half, 0:1], ALU.subtract, ALU.mult)
                last.then_inc(xn_ready, 1)

            def max_xn(n, v):
                dve.wait_ge(xnt_ready, n + 1)
                dst = xmax[:, n:n + 1] if isinstance(n, int) else xmax[:, bass.ds(n, 1)]
                dve.tensor_reduce(dst, scores_of(n, 0, 512), AX.X, ALU.max, apply_absolute_value=True).then_inc(xmax_ready, 1)

            def step3(b, u):
                lagging(head_center, 1, b, u)
                lagging(stats2, 3, b, u)
                lagging(products, 0, b, u)
                lagging(head_scale, 2, b, u)
                lagging(head_variance, 1, b, u)
                lagging(norm2, 3, b, u)
                lagging(max_xn, 4, b, u)

            over_batches(dve, step3, 4)

            def partition_max(i, src, name):
                dve.tensor_reduce(red[:, i:i + 1], src, AX.X, ALU.max).then_inc(name, 1)

            dve.wait_ge(xmax_ready, BATCH)
            partition_max(1, xmax[:, :], red_x)
            dve.wait_ge(all_x, 1)
            dve.tensor_scalar(col(SX), allmax[:, 1:2], 1.0 / QMAX16, TINY, ALU.mult, ALU.max).then_inc(sx0, 1)
            dve.wait_ge(sx0, 1)
            dve.reciprocal(col(INV_X), col(SX)).then_inc(inv_x, 1)
            dve.tensor_tensor(col(CG), col(SX), col(WFAC), ALU.mult).then_inc(sx1, 1)
            dve.wait_ge(sx1, 1)

            dve.wait_ge(x1_stored, 16 * PAIRS)

            def split_x(c):
                dve.wait_ge(xi_ready, c + 1)
                o = c * (4 * CH)
                view = lambda part: (xq[:, o + part * 2 * CH:o + (part + 1) * 2 * CH] if isinstance(c, int)
                                     else xq[:, bass.ds(o + part * 2 * CH, 2 * CH)])
                dve.tensor_copy(view(0), x_int[0]).then_inc(x_hi, 1)
                dve.wait_ge(x_hi, c + 1)
                dve.tensor_tensor(view(1), x_int[0], view(0), ALU.subtract).then_inc(xq_ready, 1)

            def max_proj(evac, table, slot_of, done):
                def f(c):
                    for j in range(FP):
                        dve.wait_ge(evac, c * FP + (j + 1))
                        i = c * FP + j
                        dst = table[:, i:i + 1] if isinstance(i, int) else table[:, bass.ds(i, 1)]
                        dve.tensor_reduce(dst, slot_pair(slot_of(c), j), AX.X, ALU.max, apply_absolute_value=True).then_inc(done, 1)
                return f

            max_g = max_proj(g_evac, gmax, lambda c: c, gmax_done)
            split_x(0)
            with dve.Fori(1, CHUNKS) as c:
                split_x(c)
                max_g(c - 1)
            max_g(CHUNKS - 1)
            dve.wait_ge(gmax_done, CHUNKS * FP)
            partition_max(2, gmax[:, :], red_g)
            dve.wait_ge(all_g, 1)
            dve.tensor_tensor(col(SG), allmax[:, 2:3], col(CG), ALU.mult).then_inc(sg0, 1)
            dve.wait_ge(sg0, 1)
            dve.tensor_scalar(col(SG), col(SG), 1.0 / QMAX16, TINY, ALU.mult, ALU.max).then_inc(sg1, 1)
            dve.wait_ge(sg1, 1)
            dve.reciprocal(col(INV_G), col(SG)).then_inc(sg2, 1)
            dve.wait_ge(sg2, 1)
            dve.tensor_scalar(col(SGK), col(SG), 1.0 / 65536.0, None, ALU.mult)
            dve.tensor_tensor(col(INV_G), col(INV_G), col(CG), ALU.mult).then_inc(inv_g, 1)

            def gate_chain(c):
                for j in range(FP):
                    g = slot_pair(c, j)
                    dve.wait_ge(sig_ready, c * FP + (j + 1))
                    dve.tensor_scalar(sigq_buf[:, :], g, 65536.0, 65535.0, ALU.mult, ALU.min).then_inc(sigq_ready, 1)
                    dve.wait_ge(sigq_ready, c * FP + (j + 1))
                    dve.scalar_tensor_tensor(g, gq_buf[j], col(SGK), sigq_buf[:, :], ALU.mult, ALU.mult).then_inc(gs_ready, 1)
                    dve.wait_ge(gs_ready, c * FP + (j + 1))
                    i = c * FP + j
                    dve.tensor_reduce(gsmax[:, bass.ds(i, 1)], g, AX.X, ALU.max, apply_absolute_value=True).then_inc(gsmax_done, 1)

            with dve.Fori(0, 4) as c:
                gate_chain(c)
                max_proj(u_evac, umax, lambda cc: c + 8, umax_done)(c)
            with dve.Fori(4, CHUNKS) as c:
                gate_chain(c)
                max_proj(u_evac, umax, lambda cc: c + 4, umax_done)(c)

            dve.wait_ge(umax_done, CHUNKS * FP)
            dve.wait_ge(gsmax_done, CHUNKS * FP)
            dve.tensor_reduce(red[:, 3:4], gsmax[:, :], AX.X, ALU.max).then_inc(red_gs, 1)
            dve.tensor_reduce(red[:, 4:5], umax[:, :], AX.X, ALU.max).then_inc(red_u, 1)
            dve.wait_ge(all_gs, 1)
            dve.tensor_scalar(col(SGS), allmax[:, 3:4], 1.0 / QMAX16, TINY, ALU.mult, ALU.max).then_inc(sgs0, 1)
            dve.wait_ge(sgs0, 1)
            dve.reciprocal(col(INV_GS), col(SGS)).then_inc(inv_gs, 1)
            dve.wait_ge(inv_gs, 1)
            dve.wait_ge(all_u, 1)
            dve.tensor_tensor(col(SU), allmax[:, 4:5], col(CG), ALU.mult).then_inc(su0, 1)
            dve.wait_ge(su0, 1)
            dve.tensor_scalar(col(SU), col(SU), 1.0 / QMAX16, TINY, ALU.mult, ALU.max).then_inc(su1, 1)
            dve.wait_ge(su1, 1)
            dve.reciprocal(col(CU), col(SU)).then_inc(su2, 1)
            dve.wait_ge(su2, 1)
            dve.tensor_tensor(col(INV_U), col(CU), col(CG), ALU.mult).then_inc(inv_u, 1)
            dve.tensor_tensor(col(SGU), col(SGS), col(SU), ALU.mult).then_inc(sgu, 1)
            dve.wait_ge(sgu, 1)

            def combine(k, gate_slot, up_slot):
                for j in range(FP):
                    g, o = slot_pair(gate_slot, j), slot_pair(up_slot, j)
                    dve.tensor_scalar(gsq_buf[j], g, col(INV_GS), None, ALU.mult).then_inc(gsq_ready, 1)
                    dve.wait_ge(gsq_ready, k * FP + (j + 1))
                    dve.wait_ge(uq_ready, k * FP + (j + 1))
                    dve.tensor_tensor(o, gsq_buf[j], uq_buf[j], ALU.mult).then_inc(o_ready, 1)
                    dve.wait_ge(o_ready, k * FP + (j + 1))
                    i = k * FP + j
                    dst = omax[:, i:i + 1] if isinstance(i, int) else omax[:, bass.ds(i, 1)]
                    dve.tensor_reduce(dst, o, AX.X, ALU.max, apply_absolute_value=True).then_inc(omax_done, 1)

            with dve.Fori(0, 4) as i:
                combine(i, i + 4, i + 8)
            for k in range(4, CHUNKS):
                combine(k, k - 4, O_SLOTS[k])

            dve.wait_ge(omax_done, CHUNKS * FP)
            partition_max(5, omax[:, :], red_o)
            dve.wait_ge(all_o, 1)
            dve.tensor_tensor(col(SO), allmax[:, 5:6], col(SGU), ALU.mult).then_inc(so0, 1)
            dve.wait_ge(so0, 1)
            dve.tensor_scalar(col(SO), col(SO), 1.0 / QMAX16, TINY, ALU.mult, ALU.max).then_inc(so1, 1)
            dve.wait_ge(so1, 1)
            dve.reciprocal(col(CO), col(SO)).then_inc(so2, 1)
            dve.wait_ge(so2, 1)
            dve.tensor_tensor(col(INV_O), col(CO), col(SGU), ALU.mult).then_inc(inv_o, 1)
            dve.tensor_tensor(col(SO_), col(SO), col(WFAC), ALU.mult).then_inc(co_ready, 1)
            dve.wait_ge(co_ready, 1)

            def split_o(n, v):
                for j in range(2):
                    dve.wait_ge(oi_ready, 2 * n + (j + 1))
                    if due(4 * n - 4):
                        dve.wait_ge(y_psum, 4 * n - 4)
                    hi, lo = (o_parts[v][:, (i * FT + 3 * j) * CH:(i * FT + 3 * j + 3) * CH] for i in range(2))
                    dve.tensor_copy(hi, o_int[j]).then_inc(o_hi, 1)
                    dve.wait_ge(o_hi, 2 * n + (j + 1))
                    dve.tensor_tensor(lo, o_int[j], hi, ALU.subtract).then_inc(op_ready, 1)

            def finish(n, v, count):
                dve.wait_ge(x1_back[v], count * 16 + 16)
                if due(count * 16):
                    dve.wait_ge(y_stored[v], count * 16)
                for t in range(4):
                    dve.wait_ge(y_psum, 4 * n + (t + 1))
                    sl = slice(t * HID, (t + 1) * HID)
                    dve.scalar_tensor_tensor(y_out[v][:, sl], bank[t][:, 0:HID], col(SO_), x1_in[v][:, sl],
                                             ALU.mult, ALU.add).then_inc(yo_ready, 1)

            split_o(0, 0)
            split_o(1, 1)
            finish(0, 0, 0)
            def two_chunks(g):
                split_o(g * 2, 0)
                finish(g * 2 - 1, 1, g - 1)
                split_o(g * 2 + 1, 1)
                finish(g * 2, 0, g)

            two_chunks(1)
            with dve.Fori(2, CHUNKS // 2) as g:
                two_chunks(g)
            finish(CHUNKS - 1, 1, CHUNKS // 2 - 1)


def kernel(x, ctx_1024, L0_xattn_igate_kernel, L0_xattn_igate_bias, L0_xattn_fgate_kernel, L0_xattn_fgate_bias,
           L0_xattn_outnorm_scale, L0_ffn_w_gate, L0_ffn_w_up, L0_ffn_w_down):
    import numpy as np
    import concourse.bacc as bacc
    from concourse.bass_utils import run_bass_kernel_spmd

    x, c = np.asarray(x), np.asarray(ctx_1024)
    natural = lambda t: t.reshape(PAIRS, PAIR, HALVES, P, HID).transpose(0, 3, 1, 2, 4).reshape(PAIRS, P, -1)
    gate_w = np.concatenate([np.asarray(L0_xattn_igate_kernel), np.asarray(L0_xattn_fgate_kernel)], axis=1)
    arrays = {
        "x": natural(x),
        "ctx_nat": natural(c),
        "ctx_t": c.reshape(PAIRS, PAIR, SEQ, KT, P).transpose(0, 4, 1, 3, 2).reshape(PAIRS, P, -1),
        "gate_w": gate_w.reshape(3 * KT, P, 2 * NH).transpose(1, 0, 2).reshape(P, -1),
        "gate_b": np.concatenate([np.asarray(L0_xattn_igate_bias), np.asarray(L0_xattn_fgate_bias)]),
        "norm_scale": np.asarray(L0_xattn_outnorm_scale),
        "w_gate": np.asarray(L0_ffn_w_gate),
        "w_up": np.asarray(L0_ffn_w_up),
        "w_down": np.asarray(L0_ffn_w_down),
    }
    arrays = {n: np.ascontiguousarray(a) for n, a in arrays.items()}
    nc = bacc.Bacc("TRN2", target_bir_lowering=False, num_devices=1)
    args = [nc.dram_tensor(n, a.shape, mybir.dt.from_np(a.dtype), kind="ExternalInput").ap() for n, a in arrays.items()]
    out = nc.dram_tensor("out", (PAIRS, P, PAIR * HALVES * HID), F32, kind="ExternalOutput").ap()
    bass_xattn_ffn(nc, *args, out)
    y = run_bass_kernel_spmd(nc, [arrays], core_ids=[0]).results[0]["out"]
    return y.reshape(PAIRS, P, PAIR, HALVES, HID).transpose(0, 2, 3, 1, 4).reshape(BATCH, SEQ, HID)
```

```python
from contextlib import ExitStack

import concourse.bass as bass
from concourse import mybir

F32 = mybir.dt.float32
F16 = mybir.dt.float16
I16 = mybir.dt.int16
I32 = mybir.dt.int32
U32 = mybir.dt.uint32
ALU = mybir.AluOpType
ACT = mybir.ActivationFunctionType
AX = mybir.AxisListType

P = 128
BATCH = 16
SEQ = 256
HID = 256
NH = 4
DH = HID // NH
FF = 768
HALVES = SEQ // P
KT = HID // P
UNROLL = 4
PAIR = 2
PAIRS = BATCH // PAIR
VC = DH + 2
GC = 3 * NH
GW = 2 * GC
SCORES = NH * (SEQ + P)
CH = 512
CHUNKS = BATCH * SEQ // CH
FT = FF // P
SLOT = FT * CH
PAIRC = 2 * CH
FP = FT // 2
BLOCK = 32
STRIPS = 3 * FF * HID // (P * HID)
QMAX16 = 2.0 ** 15 - 1.0
QMAX4 = 7.0
LN_EPS = 1e-5
NORM_EPS = 1e-6
TINY = 1e-12
W_UNIT = 4096.0
Q_UNIT = 256.0
NEVER = 1.0e30


def bass_xattn_ffn(nc, x, ctx_nat, ctx_t, gate_w, gate_b, norm_scale, w_gate, w_up, w_down, out):
    x1_dram = nc.dram_tensor("x1_spill", (PAIRS, P, PAIR * HALVES * HID), F32, kind="Internal").ap()
    max_dram = nc.dram_tensor("running_max", (BATCH * NH, SEQ), F32, kind="Internal").ap()
    up_dram = nc.dram_tensor("up_spill", (4, P, SLOT), F32, kind="Internal").ap()

    es = ExitStack()
    with es:
        def sb(name, shape, dt=F32):
            return es.enter_context(nc.sbuf_tensor(name, shape, dt))

        def sem(name):
            return es.enter_context(nc.semaphore(name))

        A_TMP = 8 * SLOT
        A_X = 12 * SLOT
        arena = sb("arena", [P, A_X + BATCH * HALVES * HID])

        def at(off, n):
            return arena[:, off:off + n]

        def at_dyn(off, n):
            return arena[:, bass.ds(off, n)]

        def slot_pair(slot, j):
            if isinstance(slot, int):
                return at(slot * SLOT + j * PAIRC, PAIRC)
            return at_dyn(slot * SLOT + j * PAIRC, PAIRC)

        def int_pair(slot, j):
            return slot_pair(slot, j).bitcast(I32)

        wg_area = sb("wg_area", [P, 2 * FP * PAIRC], F16)
        wg_parts = wg_area[:, 0:2 * KT * FF].rearrange("p (i k f) -> p i k f", i=2, k=KT)
        wu_parts = sb("wu_parts", [P, 2, KT, FF], F16)
        wd_parts = sb("wd_parts", [P, 2, FT, HID], F16)
        gates = sb("gates", [P, HALVES, BATCH, GC])
        scale_row = sb("scale_row", [P, HID])
        ident = sb("ident", [P, P])
        tri = sb("tri", [P, P])
        ones = sb("ones", [P, P])
        gate_w_raw = sb("gate_w_raw", [P, 3 * KT, 2 * NH])
        gate_w_sum = sb("gate_w_sum", [P, 2 * KT, 2 * NH])
        gate_w_parts = sb("gate_w_parts", [P, 2 * KT, GW], F16)
        gate_bias = sb("gate_bias", [P, 2 * NH])
        a_nat = sb("a_nat", [P, HALVES, BATCH * NH])
        floor_nat = sb("floor_nat", [P, HALVES, BATCH * NH])
        run_max = sb("run_max", [BATCH * NH, SEQ])
        bn_raw = sb("bn_raw", [P, 2, HALVES, 6])
        mean_var = sb("mean_var", [P, 2, HALVES, 2])
        rstd = sb("rstd", [P, 2, HALVES, 1])
        minus_half = sb("minus_half", [P, HALVES * NH])
        o_cols = sb("o_cols", [P, 2, HALVES * NH, 2])
        floor_n = sb("floor_n", [P, 2, HALVES * NH])
        floor_w = sb("floor_w", [P, 2, HALVES * NH])
        floor_w2 = sb("floor_w2", [P, 2, HALVES * NH])
        sumsq = sb("sumsq", [P, 2, HALVES * NH])
        head_var = sb("head_var", [P, 2, HALVES * NH])
        head_gain = sb("head_gain", [P, 2, HALVES * NH])
        xmax = sb("xmax", [P, BATCH])
        gmax = sb("gmax", [P, CHUNKS * FP])
        umax = sb("umax", [P, CHUNKS * FP])
        gsmax = sb("gsmax", [P, CHUNKS * FP])
        omax = sb("omax", [P, CHUNKS * FP])
        red = sb("red", [P, 8])
        allmax = sb("allmax", [P, 8])
        sc = sb("sc", [P, 32])

        q_nat = [at(A_TMP + i * 512, 512) for i in range(2)]
        q_parts = [at(A_TMP + 1024 + i * 512, 512).bitcast(F16) for i in range(2)]
        c_parts = [at(A_TMP + 2048 + i * 512, 512).bitcast(F16) for i in range(2)]
        gates_raw = at(A_TMP + 3072, HALVES * BATCH * 2 * GW).rearrange("p (s b g) -> p s b g", s=HALVES, b=BATCH)
        w_nat = at(A_TMP, STRIPS * HID)
        w_int = at(A_TMP + STRIPS * HID, STRIPS * HID // 2).bitcast(I16)
        w_tmp = [at(A_TMP + STRIPS * HID * 3 // 2 + i * 512, 512) for i in range(2)]
        block_max, block_s, block_inv = [at(A_TMP + 8192 + i * STRIPS * 8, STRIPS * 8) for i in range(3)]
        gate_sum = at(A_TMP + 4608, HALVES * BATCH * 2 * GC).rearrange("p (b i g) -> p b i g", i=2, g=GC)
        A_CTX = BATCH * (SCORES - KT * SEQ)
        fz, fabs, fexp, fln, lf, csum, eneg = [
            at(A_TMP + i * P, P).rearrange("p (s b h) -> p s b h", s=HALVES, b=BATCH) for i in range(7)]
        a_row = at(A_TMP + 1024, SEQ)[0:BATCH * NH, :]
        max_bc = [at(A_TMP + i * 1024, 1024).rearrange("p (h s) -> p h s", h=NH) for i in range(2)]
        max_hi = [at(A_TMP + 2048 + i * 512, 512).rearrange("p (h s) -> p h s", h=NH) for i in range(2)]
        decay = [at(A_TMP + 3072 + i * SCORES, SCORES) for i in range(2)]
        head = [at(A_TMP + 6144 + i * 512, 512) for i in range(2)]
        square = at(A_TMP + 7168, 512)
        xn = [at(A_TMP + 7680 + i * 512, 512) for i in range(2)]
        v_aug = [at(A_TMP + 8704 + i * PAIR * HALVES * NH * VC, PAIR * HALVES * NH * VC)
                 .rearrange("p (b s h c) -> p b s h c", b=PAIR, s=HALVES, h=NH) for i in range(2)]
        x_int = [at(A_TMP + i * 512, 512).bitcast(I16) for i in range(2)]
        xq = arena[:, A_X:A_X + 8192].bitcast(F16)
        sig = [wg_area[:, 2 * j * PAIRC:2 * (j + 1) * PAIRC].bitcast(F32) for j in range(FP)]
        sigq = [wg_area[:, 2 * j * PAIRC:2 * (j + 1) * PAIRC].bitcast(I32) for j in range(FP)]
        o_parts = [at(i * SLOT, SLOT).bitcast(F16) for i in range(2)]
        o_int = [at(2 * SLOT + i * SLOT // 4, SLOT // 4).bitcast(I16) for i in range(2)]
        x1_in = [at(3 * SLOT + i * 1024, 1024) for i in range(2)]
        y_out = [at(6 * SLOT + i * 1024, 1024) for i in range(2)]

        x_res = at(A_X, BATCH * HALVES * HID)

        SX, INV_X, CG, SG, INV_G, SGK, CU, SU, INV_U, SGS, INV_GS, SO_, SO, INV_O, CO, WMUL, WFAC, WP2, SGU, \
            P2_G, P2_C, MUL_G, MUL_C, FAC_G, FAC_C, FAC_CG, FAC_QG, FAC_S = range(28)

        def col(i):
            return sc[:, i:i + 1]

        psum = es.enter_context(nc.psum_tensor("psum", [P, 8, CH], F32))
        bank = [psum[:, i, :] for i in range(8)]
        bank_pair = [psum[:, 2 * i:2 * i + 2, :].rearrange("p i n -> p (i n)") for i in range(4)]
        ORDER = [4, 5, 6, 7, 0, 1, 2, 3]
        O_SLOTS = [8, 9, 10, 11, 12, 13, 4, 5]
        passed = sem("passed")
        consts_loaded = sem("consts_loaded")
        w_loaded = sem("w_loaded")
        consts_set = sem("consts_set")
        tri_zero = sem("tri_zero")
        ident_zero = sem("ident_zero")
        w_step = sem("w_step")
        w_rowmax = sem("w_rowmax")
        w_allmax = sem("w_allmax")
        w_dq = sem("w_dq")
        w_fac = sem("w_fac")
        w_tr = sem("w_tr")
        w_sc = sem("w_sc")
        w_hi = sem("w_hi")
        w_parts = sem("w_parts")
        stats_raw = sem("stats_raw")
        stats_done = sem("stats_done")
        rstd_eps = sem("rstd_eps")
        rstd_ready = sem("rstd_ready")
        q_ready = sem("q_ready")
        q_trans = sem("q_trans")
        qt_ready = sem("qt_ready")
        gates_done = sem("gates_done")
        gates_evac = sem("gates_evac")
        scores_ready = sem("scores_ready")
        scores_evac = sem("scores_evac")
        gw_zero = sem("gw_zero")
        gw_sum = sem("gw_sum")
        gw_max = sem("gw_max")
        c_max = sem("c_max")
        gc_rowmax = sem("gc_rowmax")
        gc_allmax = sem("gc_allmax")
        gate_scale_step = sem("gate_scale_step")
        gc_fac2 = sem("gc_fac2")
        gw_ready = sem("gw_ready")
        c_hi = sem("c_hi")
        c_lo = sem("c_lo")
        q_hi = sem("q_hi")
        m_gsum = sem("m_gsum")
        m_gq = sem("m_gq")
        m_gates = sem("m_gates")
        m_fz = sem("m_fz")
        m_abs = sem("m_abs")
        m_exp = sem("m_exp")
        m_ln = sem("m_ln")
        m_lf = sem("m_lf")
        m_ib = sem("m_ib")
        m_cs = sem("m_cs")
        m_csc = sem("m_csc")
        m_a = sem("m_a")
        m_at = sem("m_at")
        m_ac = sem("m_ac")
        m_scan = sem("m_scan")
        m_max_stored = sem("m_max_stored")
        m_mt = sem("m_mt")
        m_add = sem("m_add")
        m_floor = sem("m_floor")
        masked = sem("masked")
        v_ready = sem("v_ready")
        exp_done = sem("exp_done")
        c_ready = sem("c_ready")
        pv_done = sem("pv_done")
        cols_ready = sem("cols_ready")
        head_ready = sem("head_ready")
        sq_ready = sem("sq_ready")
        ssq_ready = sem("ssq_ready")
        n_half = sem("n_half")
        n_ready = sem("n_ready")
        w_ready = sem("w_ready")
        w2_ready = sem("w2_ready")
        var_ready = sem("var_ready")
        gain_ready = sem("gain_ready")
        y_ready = sem("y_ready")
        ys_ready = sem("ys_ready")
        x1_ready = sem("x1_ready")
        bn2_raw = sem("bn2_raw")
        bn2_done = sem("bn2_done")
        rstd2_eps = sem("rstd2_eps")
        rstd2_ready = sem("rstd2_ready")
        xn_ready = sem("xn_ready")
        xnt_psum = sem("xnt_psum")
        xnt_ready = sem("xnt_ready")
        xmax_ready = sem("xmax_ready")
        x1_stored = sem("x1_stored")
        red_x = sem("red_x")
        all_x = sem("all_x")
        sx0 = sem("sx0")
        sx1 = sem("sx1")
        inv_x0 = sem("inv_x0")
        inv_x = sem("inv_x")
        xi_ready = sem("xi_ready")
        x_hi = sem("x_hi")
        xq_ready = sem("xq_ready")
        g_psum = sem("g_psum")
        g_evac = sem("g_evac")
        gmax_done = sem("gmax_done")
        red_g = sem("red_g")
        all_g = sem("all_g")
        g_scale_step = sem("g_scale_step")
        inv_g = sem("inv_g")
        u_psum = sem("u_psum")
        u_evac = sem("u_evac")
        umax_done = sem("umax_done")
        gq_ready = sem("gq_ready")
        sig_ready = sem("sig_ready")
        sigq_ready = sem("sigq_ready")
        gs_ready = sem("gs_ready")
        gsmax_done = sem("gsmax_done")
        red_gs = sem("red_gs")
        all_gs = sem("all_gs")
        gs_scale_step = sem("gs_scale_step")
        inv_gs = sem("inv_gs")
        red_u = sem("red_u")
        all_u = sem("all_u")
        u_scale_step = sem("u_scale_step")
        inv_u = sem("inv_u")
        uq_ready = sem("uq_ready")
        gsq_first = sem("gsq_first")
        gsq_rest = sem("gsq_rest")
        o_first = sem("o_first")
        o_rest = sem("o_rest")
        omax_done = sem("omax_done")
        red_o = sem("red_o")
        all_o = sem("all_o")
        o_scale_step = sem("o_scale_step")
        inv_o = sem("inv_o")
        co_ready = sem("co_ready")
        oi_ready = sem("oi_ready")
        o_hi = sem("o_hi")
        op_ready = sem("op_ready")
        y_psum = sem("y_psum")
        yo_ready = sem("yo_ready")
        x_loaded = [sem(f"x_loaded{i}") for i in range(2)]
        ctx_loaded = [sem(f"ctx_loaded{i}") for i in range(BATCH // UNROLL)]
        max_loaded = [sem(f"max_loaded{i}") for i in range(2)]
        v_loaded = [sem(f"v_loaded{i}") for i in range(2)]
        up_spilled = [sem(f"up_spilled{i}") for i in range(4)]
        up_back = [sem(f"up_back{i}") for i in range(4)]
        x1_back = [sem(f"x1_back{i}") for i in range(2)]
        y_stored = [sem(f"y_stored{i}") for i in range(2)]

        def due(count):
            return not isinstance(count, int) or count > 0

        def apart(eng, count):
            if not isinstance(count, int):
                eng.sem_inc(passed, 1)

        def over_batches(eng, steps, tail=0):
            for b in range(UNROLL):
                steps(b, b)
            with eng.Fori(1, BATCH // UNROLL) as it:
                for u in range(UNROLL):
                    steps(it * UNROLL + u, u)
            for b in range(BATCH, BATCH + tail):
                steps(b, b % UNROLL)

        def lagging(part, lag, b, u):
            n = b - lag
            if isinstance(b, int) and not 0 <= n < BATCH:
                return
            part(n, (u - lag) % UNROLL)

        def over_chunks(eng, steps, tail):
            steps(0)
            with eng.Fori(1, CHUNKS) as c:
                steps(c)
            for c in range(CHUNKS, CHUNKS + tail):
                steps(c)

        def place(h):
            return (h % 2) * 2 + h // 2

        def x_of(n, half):
            off = A_X + n * (HALVES * HID) + half * HID
            return at(off, HID) if isinstance(n, int) else at_dyn(off, HID)

        def x_batch(n):
            off = A_X + n * (HALVES * HID)
            return at(off, HALVES * HID) if isinstance(n, int) else at_dyn(off, HALVES * HID)

        def ctx_of(n):
            off = A_CTX + n * (KT * SEQ)
            return at(off, KT * SEQ) if isinstance(n, int) else at_dyn(off, KT * SEQ)

        def scores_of(n, off, size):
            o = n * SCORES + off
            return at(o, size) if isinstance(n, int) else at_dyn(o, size)

        def chunk_xq(c, part, k):
            o = c * (4 * CH) + part * (2 * CH) + k * CH
            return xq[:, o:o + CH] if isinstance(c, int) else xq[:, bass.ds(o, CH)]

        block = es.enter_context(nc.Block())

        @block.sync
        def _(sp):
            sp.dma_start(gate_w_raw[:, :, :].rearrange("p k g -> p (k g)"), gate_w).then_inc(consts_loaded, 16)
            sp.dma_start(gate_bias[:, :], gate_b.partition_broadcast(P)).then_inc(consts_loaded, 16)
            sp.dma_start(scale_row[:, :], norm_scale.partition_broadcast(P)).then_inc(consts_loaded, 16)

            def x_pair(b):
                off = A_X + b * (HALVES * HID)
                return at(off, PAIR * HALVES * HID) if isinstance(b, int) else at_dyn(off, PAIR * HALVES * HID)

            def dram_pair(t, pair):
                return t[pair, :, :] if isinstance(pair, int) else t[bass.ds(pair, 1), :, :].rearrange("a p n -> (a p) n")

            for i, w in enumerate((w_gate, w_up)):
                sp.dma_start(w_nat[:, i * FT * HID:(i + 1) * FT * HID].rearrange("p (s k) -> p s k", k=HID),
                             w.rearrange("(s p) k -> p s k", p=P)).then_inc(w_loaded, 16)
            sp.dma_start(w_nat[:, 2 * FT * HID:].rearrange("p (r k) -> p r k", k=FF),
                         w_down.rearrange("(r p) k -> p r k", p=P)).then_inc(w_loaded, 16)
            for i in range(BATCH // UNROLL):
                n = UNROLL * KT * SEQ
                sp.dma_start(at(A_CTX + i * n, n), ctx_t[i, :, :]).then_inc(ctx_loaded[i], 16)

            def load_x(g):
                for p in range(UNROLL // PAIR):
                    if due(g * 16):
                        sp.wait_ge(x_loaded[p], g * 16)
                    sp.dma_start(x_pair(g * UNROLL + p * PAIR), dram_pair(x, g * (UNROLL // PAIR) + p)).then_inc(x_loaded[p], 16)

            load_x(0)
            with sp.Fori(1, BATCH // UNROLL) as g:
                load_x(g)

            def load_v(pair, p):
                for i in range(PAIR):
                    sp.dma_start(v_aug[p][:, i, :, :, 0:DH],
                                 dram_pair(ctx_nat, pair)[:, i * HALVES * HID:(i + 1) * HALVES * HID]
                                 .rearrange("p (s h c) -> p s h c", s=HALVES, h=NH)).then_inc(v_loaded[p], 16)

            sp.wait_ge(w_parts, 9)
            for p in range(2):
                load_v(p, p)

            sp.wait_ge(m_scan, 1)
            sp.dma_start(max_dram, run_max[:, :]).then_inc(m_max_stored, 16)
            sp.wait_ge(m_max_stored, 16)
            sp.wait_ge(m_floor, 1)

            def load_max(n, u):
                if due((n - 1) * 2):
                    sp.wait_ge(exp_done, (n - 1) * 2)
                rows = max_dram[n * NH:(n + 1) * NH, :] if isinstance(n, int) else max_dram[bass.ds(n * NH, NH), :]
                sp.dma_start(max_bc[u % 2].rearrange("p h s -> p (h s)"),
                             rows.rearrange("h s -> (h s)").partition_broadcast(P)).then_inc(max_loaded[u % 2], 16)

            def loads3(g):
                for u in range(UNROLL):
                    n = g * UNROLL + u
                    load_max(n, u)
                    if u % PAIR == 0 and not isinstance(g, int):
                        sp.wait_ge(pv_done, n - 2)
                        load_v(g * (UNROLL // PAIR) + u // PAIR, u // PAIR)
                    if u % PAIR == 1:
                        store_x1(g - 1, u)

            def store_x1(g, u):
                if isinstance(g, int) and g < 0:
                    return
                n = g * UNROLL + u
                sp.wait_ge(x1_ready, n + 1)
                sp.dma_start(dram_pair(x1_dram, g * (UNROLL // PAIR) + u // PAIR), x_pair(n - 1)).then_inc(x1_stored, 16)

            loads3(0)
            with sp.Fori(1, BATCH // UNROLL) as g:
                loads3(g)
            for u in range(1, UNROLL, PAIR):
                store_x1(BATCH // UNROLL - 1, u)

            for c in range(4):
                sp.wait_ge(umax_done, (c + 1) * FP)
                sp.dma_start(up_dram[c, :, :], at((c + 8) * SLOT, SLOT)).then_inc(up_spilled[c], 16)
            for c in range(4):
                sp.wait_ge(up_spilled[c], 16)
            sp.wait_ge(u_psum, CHUNKS * FP)
            for c in range(4):
                if c >= 2:
                    sp.wait_ge(o_first, c - 1)
                    sp.wait_ge(o_rest, (FP - 1) * (c - 1))
                sp.dma_start(at(O_SLOTS[c + 4] * SLOT, SLOT), up_dram[c, :, :]).then_inc(up_back[c], 16)

            sp.wait_ge(omax_done, CHUNKS * FP)
            def store_y(k):
                sp.wait_ge(yo_ready, (k + 1) * 4)
                sp.dma_start(out[ORDER[k], :, :], y_out[k % 2]).then_inc(y_stored[k % 2], 16)

            for k in range(CHUNKS):
                if due((k - 1) * 4):
                    sp.wait_ge(yo_ready, (k - 1) * 4)
                sp.dma_start(x1_in[k % 2], x1_dram[ORDER[k], :, :]).then_inc(x1_back[k % 2], 16)
                if k >= 1:
                    store_y(k - 1)
            store_y(CHUNKS - 1)
            for i in range(2):
                sp.wait_ge(y_stored[i], 16 * CHUNKS // 2)

        @block.gpsimd
        def _(pool):
            pool.memset(ident[:, :], 0.0).then_inc(ident_zero, 1)
            pool.memset(tri[:, :], 1.0).then_inc(tri_zero, 1)
            pool.memset(ones[:, :], 1.0)
            pool.memset(minus_half[:, :], -0.5)
            pool.wait_ge(ident_zero, 1)
            pool.affine_select(out=ident[:, :], in_=ident[:, :], compare_op=ALU.not_equal, fill=1.0, base=0,
                               pattern=[[-1, P]], channel_multiplier=1)
            pool.wait_ge(tri_zero, 1)
            pool.affine_select(out=tri[:, :], in_=tri[:, :], compare_op=ALU.is_ge, fill=0.0, base=0,
                               pattern=[[1, P]], channel_multiplier=-1).then_inc(consts_set, 1)

            def rstd1(n, v):
                s = v % 2
                pool.wait_ge(stats_done, n + 1)
                apart(pool, n + 1)
                pool.tensor_scalar(rstd[:, s, :, :], mean_var[:, s, :, 1:2], LN_EPS, None, ALU.add).then_inc(rstd_eps, 1)
                pool.wait_ge(rstd_eps, n + 1)
                apart(pool, n + 1)
                pool.tensor_tensor(rstd[:, s, :, 0], rstd[:, s, :, 0], minus_half[:, 0:HALVES], ALU.pow).then_inc(rstd_ready, 1)

            pool.wait_ge(w_rowmax, 1)
            pool.partition_all_reduce(allmax[:, 0:1], red[:, 0:1], P, bass.bass_isa.ReduceOp.max).then_inc(w_allmax, 1)
            pool.wait_ge(gw_max, 1)
            pool.wait_ge(gc_rowmax, 1)
            pool.partition_all_reduce(allmax[:, 6:8], red[:, 6:8], P, bass.bass_isa.ReduceOp.max).then_inc(gc_allmax, 1)

            pool.wait_ge(w_parts, 9)
            for i in range(2):
                pool.memset(v_aug[i][:, :, :, :, DH:DH + 1], 1.0)

            over_batches(pool, lambda b, u: lagging(rstd1, 0, b, u), 0)

            pool.wait_ge(m_floor, 1)

            def v_means(n, v):
                p = v // PAIR
                loads = (n // UNROLL + 1) * 32 if isinstance(n, int) else v_count(v)
                pool.wait_ge(v_loaded[p], loads)
                apart(pool, loads)
                mean = gates[:, :, n, 2 * NH:GC] if isinstance(n, int) else gates[:, :, bass.ds(n, 1), 2 * NH:GC].rearrange("p s b h -> p s (b h)")
                pool.tensor_copy(v_aug[p][:, v % PAIR, :, :, DH + 1], mean).then_inc(v_ready, 1)

            def masks(n, v):
                s = v % 2
                loads = (n // 2 + 1) * 16 if isinstance(n, int) else max_count(v)
                pool.wait_ge(max_loaded[s], loads)
                apart(pool, loads)
                pool.affine_select(out=max_hi[s], in_=max_bc[s][:, :, P:SEQ], compare_op=ALU.is_ge, fill=NEVER, base=0,
                                   pattern=[[0, NH], [1, P]], channel_multiplier=-1)
                pool.affine_select(out=max_bc[s][:, :, 0:P], in_=max_bc[s][:, :, 0:P], compare_op=ALU.is_ge, fill=NEVER,
                                   base=0, pattern=[[0, NH], [1, P]], channel_multiplier=-1).then_inc(masked, 1)

            reg = [None]

            def v_count(v):
                return reg[0] * 32 if v == UNROLL - 1 else reg[0] * 32 + 32

            def max_count(v):
                return reg[0] * 32 + (v // 2 + 1) * 16

            def gain(n, v):
                s = v % 2
                pool.wait_ge(var_ready, n + 1)
                apart(pool, n + 1)
                pool.tensor_tensor(head_gain[:, s, :], head_var[:, s, :], minus_half[:, :], ALU.pow).then_inc(gain_ready, 1)

            def residual(n, v):
                s = v % 2
                pool.wait_ge(y_ready, n + 1)
                apart(pool, n + 1)
                h2 = head[s].rearrange("p (s c) -> p s c", s=HALVES)
                pool.tensor_tensor(h2, h2, scale_row[:, :].unsqueeze(1).broadcast_to([P, HALVES, HID]), ALU.mult).then_inc(ys_ready, 1)
                pool.wait_ge(ys_ready, n + 1)
                apart(pool, n + 1)
                pool.tensor_tensor(x_batch(n), x_batch(n), head[s], ALU.add).then_inc(x1_ready, 1)

            def rstd2(n, v):
                s = v % 2
                pool.wait_ge(bn2_done, n + 1)
                apart(pool, n + 1)
                pool.tensor_scalar(rstd[:, s, :, :], mean_var[:, s, :, 1:2], LN_EPS, None, ALU.add).then_inc(rstd2_eps, 1)
                pool.wait_ge(rstd2_eps, n + 1)
                apart(pool, n + 1)
                pool.tensor_tensor(rstd[:, s, :, 0], rstd[:, s, :, 0], minus_half[:, 0:HALVES], ALU.pow).then_inc(rstd2_ready, 1)

            def step3(b, u):
                lagging(masks, 0, b, u)
                lagging(gain, 3, b, u)
                lagging(rstd2, 4, b, u)
                lagging(v_means, 1, b, u)
                lagging(residual, 3, b, u)

            for b in range(UNROLL):
                step3(b, b)
            with pool.Fori(1, BATCH // UNROLL) as it:
                reg[0] = it
                for u in range(UNROLL):
                    step3(it * UNROLL + u, u)
            for b in range(BATCH, BATCH + 4):
                step3(b, b % UNROLL)

            def over_partitions(i, local, everywhere):
                pool.wait_ge(local, 1)
                pool.partition_all_reduce(allmax[:, i:i + 1], red[:, i:i + 1], P, bass.bass_isa.ReduceOp.max).then_inc(everywhere, 1)

            over_partitions(1, red_x, all_x)
            over_partitions(2, red_g, all_g)

            with pool.Fori(0, CHUNKS) as c:
                for j in range(FP):
                    pool.wait_ge(sigq_ready, c * FP + (j + 1))
                    pool.sem_inc(passed, 1)
                    pool.tensor_tensor(int_pair(c, j), int_pair(c, j), sigq[j], ALU.mult).then_inc(gs_ready, 1)

            over_partitions(3, red_gs, all_gs)
            over_partitions(4, red_u, all_u)

            def combine_rest(k, gate_slot, up_slot):
                for j in range(1, FP):
                    pool.wait_ge(gsq_rest, k * (FP - 1) + j)
                    apart(pool, k * (FP - 1) + j)
                    pool.wait_ge(uq_ready, k * FP + (j + 1))
                    apart(pool, k * FP + (j + 1))
                    pool.tensor_tensor(int_pair(up_slot, j), int_pair(gate_slot, j), int_pair(up_slot, j), ALU.mult).then_inc(o_rest, 1)

            combine_rest(0, 4, O_SLOTS[0])
            with pool.Fori(1, 4) as k:
                combine_rest(k, k + 4, k + 8)
            for k in range(4, CHUNKS):
                combine_rest(k, k - 4, O_SLOTS[k])

            over_partitions(5, red_o, all_o)

        @block.scalar
        def _(act):
            act.wait_ge(w_fac, 1)
            for r in range(9):
                act.wait_ge(w_tr, r + 1)
                if due(r - 1):
                    act.wait_ge(w_parts, r - 1)
                act.activation(w_tmp[r % 2], bank[7 - 7 * (r % 2)][:, :], ACT.Copy, scale=col(WMUL)).then_inc(w_sc, 1)

            def context_high(n, v):
                if due((n - 1) * 2):
                    act.wait_ge(scores_ready, (n - 1) * 2)
                    apart(act, (n - 1) * 2)
                act.activation(c_parts[v % 2][:, 0:KT * SEQ], ctx_of(n), ACT.Copy, scale=col(MUL_C)).then_inc(c_hi, 1)

            def query_high(n, v):
                act.wait_ge(q_trans, n + 1)
                apart(act, n + 1)
                if due((n - 1) * 2):
                    act.wait_ge(scores_ready, (n - 1) * 2)
                    apart(act, (n - 1) * 2)
                act.activation(q_parts[v % 2][:, 0:KT * SEQ], bank[v % 2][:, :], ACT.Copy, scale=Q_UNIT).then_inc(q_hi, 1)

            def evac_gates(n, v):
                act.wait_ge(gates_done, n + 1)
                apart(act, n + 1)
                dst = gates_raw[:, :, n, :] if isinstance(n, int) else \
                    gates_raw[:, :, bass.ds(n, 1), :].rearrange("p s b g -> p s (b g)")
                act.activation(dst, bank[2][:, 0:HALVES * 2 * GW].rearrange("p (s g) -> p s g", s=HALVES), ACT.Copy).then_inc(gates_evac, 1)

            def evac_scores(n, v):
                for key_half in range(HALVES):
                    width = 2 * (SEQ - key_half * P)
                    act.wait_ge(scores_ready, n * 2 + (key_half + 1))
                    apart(act, n * 2 + (key_half + 1))
                    act.activation(scores_of(n, key_half * NH * SEQ, 2 * width).rearrange("p (i n) -> p i n", i=2),
                                   psum[:, 3 + 2 * key_half:5 + 2 * key_half, 0:width], ACT.Copy,
                                   scale=col(FAC_S)).then_inc(scores_evac, 1)

            def step1(b, u):
                lagging(context_high, 1, b, u)
                lagging(query_high, 1, b, u)
                lagging(evac_gates, 2, b, u)
                lagging(evac_scores, 2, b, u)

            act.wait_ge(gc_fac2, 1)
            over_batches(act, step1, 2)

            act.wait_ge(m_fz, 1)
            act.activation(fabs, fz, ACT.Abs).then_inc(m_abs, 1)
            act.wait_ge(m_abs, 1)
            act.activation(fexp, fabs, ACT.Exp, scale=-1.0).then_inc(m_exp, 1)
            act.wait_ge(m_exp, 1)
            act.activation(fln, fexp, ACT.Ln, bias=1.0).then_inc(m_ln, 1)
            act.wait_ge(m_add, 1)
            act.activation(floor_nat[:, :, :], eneg.rearrange("p s b h -> p s (b h)"), ACT.Exp, scale=-1.0).then_inc(m_floor, 1)

            def a_col(half, n, h):
                return a_nat[:, half, n * NH + h:n * NH + h + 1] if isinstance(n, int) else \
                    a_nat[:, half, bass.ds(n * NH + h, 1)]

            def decays_low(n, v):
                s = v % 2
                act.wait_ge(masked, n + 1)
                apart(act, n + 1)
                if due(n - 1):
                    act.wait_ge(pv_done, n - 1)
                    apart(act, n - 1)
                for h in range(NH):
                    last = act.activation(decay[s][:, place(h) * SEQ:(place(h) + 1) * SEQ], max_bc[s][:, h, :], ACT.Exp,
                                          bias=a_col(0, n, h), scale=-1.0)
                last.then_inc(exp_done, 1)

            def decays_high(n, v):
                s = v % 2
                for h in range(NH):
                    last = act.activation(decay[s][:, NH * SEQ + place(h) * P:NH * SEQ + (place(h) + 1) * P], max_hi[s][:, h, :], ACT.Exp,
                                          bias=a_col(1, n, h), scale=-1.0)
                last.then_inc(exp_done, 1)

            def squares(n, v):
                act.wait_ge(head_ready, n + 1)
                apart(act, n + 1)
                if due(n):
                    act.wait_ge(ssq_ready, n)
                    apart(act, n)
                act.activation(square, head[v % 2], ACT.Square).then_inc(sq_ready, 1)

            def evac_xnt(n, v):
                act.wait_ge(xnt_psum, n + 1)
                apart(act, n + 1)
                act.activation(scores_of(n, 0, 512), bank[4 + v % 2][:, :], ACT.Copy).then_inc(xnt_ready, 1)

            def step3(b, u):
                lagging(decays_low, 0, b, u)
                lagging(squares, 2, b, u)
                lagging(decays_high, 0, b, u)
                lagging(evac_xnt, 4, b, u)

            over_batches(act, step3, 4)

            def quant_x(c):
                o = c * (PAIR * SCORES)
                v = at(o, PAIR * SCORES) if isinstance(c, int) else at_dyn(o, PAIR * SCORES)
                if due(c):
                    act.wait_ge(xq_ready, c)
                    apart(act, c)
                act.activation(x_int[0].rearrange("p (k b t) -> p b k t", k=KT, b=PAIR),
                               v.rearrange("p (b n) -> p b n", b=PAIR)[:, :, 0:512].rearrange("p b (k t) -> p b k t", k=KT),
                               ACT.Copy, scale=col(INV_X)).then_inc(xi_ready, 1)

            def evac_proj(psum_sem, evac_sem, c, slot):
                for j in range(FP):
                    act.wait_ge(psum_sem, c * FP + (j + 1))
                    apart(act, c * FP + (j + 1))
                    act.activation(slot_pair(slot, j), bank_pair[j], ACT.Copy).then_inc(evac_sem, 1)

            act.wait_ge(inv_x, 1)
            quant_x(0)
            with act.Fori(1, CHUNKS) as c:
                quant_x(c)
                evac_proj(g_psum, g_evac, c - 1, c - 1)
            evac_proj(g_psum, g_evac, CHUNKS - 1, CHUNKS - 1)

            def gate_chain(c, up_slot):
                for j in range(FP):
                    act.activation(int_pair(c, j), slot_pair(c, j), ACT.Copy, scale=col(INV_G)).then_inc(gq_ready, 1)
                    act.wait_ge(u_psum, c * FP + (j + 1))
                    apart(act, c * FP + (j + 1))
                    act.activation(slot_pair(up_slot, j), bank_pair[j], ACT.Copy).then_inc(u_evac, 1)
                    act.wait_ge(gq_ready, c * FP + (j + 1))
                    apart(act, c * FP + (j + 1))
                    if due((c - 1) * FP + (j + 1)):
                        act.wait_ge(gs_ready, (c - 1) * FP + (j + 1))
                        apart(act, (c - 1) * FP + (j + 1))
                    act.activation(sig[j], int_pair(c, j), ACT.Sigmoid, scale=col(SG)).then_inc(sig_ready, 1)

            act.wait_ge(inv_g, 1)
            gate_chain(0, 8)
            with act.Fori(1, 4) as c:
                gate_chain(c, c + 8)
            for c in range(4, CHUNKS):
                act.wait_ge(up_spilled[c - 4], 16)
                gate_chain(c, c + 4)

            def quant(k, gate_slot, up_slot):
                for j in range(FP):
                    if j > 0:
                        g = int_pair(gate_slot, j)
                        act.activation(g, g, ACT.Copy, scale=col(INV_GS)).then_inc(gsq_rest, 1)
                    act.activation(int_pair(up_slot, j), slot_pair(up_slot, j), ACT.Copy, scale=col(INV_U)).then_inc(uq_ready, 1)

            act.wait_ge(inv_u, 1)
            quant(0, 4, O_SLOTS[0])
            with act.Fori(1, 4) as k:
                quant(k, k + 4, k + 8)
            for k in range(4, CHUNKS):
                act.wait_ge(up_back[k - 4], 16)
                quant(k, k - 4, O_SLOTS[k])

            act.wait_ge(inv_o, 1)
            for k in range(CHUNKS):
                for j in range(2):
                    if due(2 * k + j - 1):
                        act.wait_ge(op_ready, 2 * k + j - 1)
                        apart(act, 2 * k + j - 1)
                    act.activation(o_int[j], at(O_SLOTS[k] * SLOT + j * SLOT // 2, SLOT // 2).bitcast(I32), ACT.Copy,
                                   scale=col(INV_O)).then_inc(oi_ready, 1)

        @block.tensor
        def _(pe):
            pe.wait_ge(consts_set, 1)

            pe.wait_ge(w_dq, 1)
            for r in range(9):
                if due(r - 1):
                    pe.wait_ge(w_sc, r - 1)
                for i in range(2):
                    for j in range(2):
                        if r < 6:
                            src = w_nat[:, ((r // 3) * 6 + 2 * (r % 3) + j) * HID + i * P:][:, 0:P]
                        else:
                            src = w_nat[:, 12 * HID + j * FF + (2 * (r - 6) + i) * P:][:, 0:P]
                        last = pe.transpose(bank[7 - 7 * (r % 2)][:, (2 * i + j) * P:(2 * i + j + 1) * P], src, ident[:, :])
                last.then_inc(w_tr, 1)

            def transposes(n, v):
                s = v % 2
                pe.wait_ge(q_ready, n + 1)
                for k in range(KT):
                    for half in range(HALVES):
                        last = pe.transpose(bank[s][:, k * SEQ + half * P:k * SEQ + (half + 1) * P],
                                            q_nat[s][:, half * HID + k * P:half * HID + (k + 1) * P], ident[:, :])
                last.then_inc(q_trans, 1)

            def gates_and_scores(n, v):
                s = v % 2
                ct, qt = (t[s].rearrange("p (i k t) -> p i k t", i=2, k=KT) for t in (c_parts, q_parts))
                if due(n):
                    pe.wait_ge(gates_evac, n)
                pe.wait_ge(qt_ready, n + 1)
                pe.wait_ge(c_lo, n + 1)
                for half in range(HALVES):
                    t = slice(half * P, (half + 1) * P)
                    for i, parts in enumerate((ct, qt)):
                        o = bank[2][:, (half * 2 + i) * GW:(half * 2 + i + 1) * GW]
                        for k in range(KT):
                            pe.matmul(o, parts[:, 0, k, t], gate_w_parts[:, i * KT + k, :], start=(k == 0), stop=False)
                        for k in range(KT):
                            last = pe.matmul(o[:, 0:GC], parts[:, 1, k, t], gate_w_parts[:, i * KT + k, 0:GC],
                                             start=False, stop=(k == KT - 1))
                last.then_inc(gates_done, 1)
                for key_half in range(HALVES):
                    if due((n - 1) * 2 + (key_half + 1)):
                        pe.wait_ge(scores_evac, (n - 1) * 2 + (key_half + 1))
                    width = SEQ - key_half * P
                    for hp in range(NH // 2):
                        for i, (cp, qp) in enumerate(((0, 0), (0, 1), (1, 0))):
                            for odd in range(2):
                                r = DH * odd
                                last = pe.matmul(bank[3 + 2 * key_half + odd][:, hp * width:(hp + 1) * width],
                                                 ct[r:r + DH, cp, hp, key_half * P:(key_half + 1) * P],
                                                 qt[r:r + DH, qp, hp, key_half * P:SEQ], start=(i == 0), stop=(i == 2))
                    last.then_inc(scores_ready, 1)

            def step1(b, u):
                lagging(transposes, 1, b, u)
                lagging(gates_and_scores, 2, b, u)

            pe.wait_ge(gw_ready, 1)
            over_batches(pe, step1, 2)

            pe.wait_ge(m_lf, 1)
            lfv = lf.rearrange("p s b h -> p s (b h)")
            C = BATCH * NH
            pe.matmul(bank[0][:, 0:C], tri[:, :], lfv[:, 0, :], start=True, stop=True)
            pe.matmul(bank[0][:, C:2 * C], tri[:, :], lfv[:, 1, :], start=True, stop=False)
            pe.matmul(bank[0][:, C:2 * C], ones[:, :], lfv[:, 0, :], start=False, stop=True).then_inc(m_cs, 1)
            pe.wait_ge(m_a, 1)
            for half in range(HALVES):
                last = pe.transpose(bank[1][0:C, half * P:(half + 1) * P], a_nat[:, half, :], ident[:, :])
            last.then_inc(m_at, 1)
            pe.wait_ge(m_scan, 1)
            for half in range(HALVES):
                last = pe.transpose(bank[2][:, half * C:(half + 1) * C], run_max[:, half * P:(half + 1) * P], ident[0:C, 0:C])
            last.then_inc(m_mt, 1)

            def weighted_sum(n, v, half):
                s = v % 2
                if half == 0:
                    pe.wait_ge(v_ready, n + 1)
                    if due(n - 1):
                        pe.wait_ge(head_ready, n - 1)
                pe.wait_ge(c_ready, 2 * n + (half + 1))
                for h in range(NH):
                    o = bank[2 * s + half][:, h * VC:(h + 1) * VC]
                    last = pe.matmul(o, decay[s][:, place(h) * SEQ + half * P:place(h) * SEQ + (half + 1) * P],
                                     v_aug[v // PAIR][:, v % PAIR, 0, h, :], start=True, stop=(half == 0))
                    if half == 1:
                        last = pe.matmul(o, decay[s][:, NH * SEQ + place(h) * P:NH * SEQ + (place(h) + 1) * P],
                                         v_aug[v // PAIR][:, v % PAIR, 1, h, :], start=False, stop=True)
                if half == HALVES - 1:
                    last.then_inc(pv_done, 1)

            def xn_transposes(n, v):
                s = v % 2
                pe.wait_ge(xn_ready, n + 1)
                if due(n):
                    pe.wait_ge(xnt_ready, n)
                for k in range(KT):
                    for half in range(HALVES):
                        last = pe.transpose(bank[4 + s][:, k * SEQ + half * P:k * SEQ + (half + 1) * P],
                                            xn[s][:, half * HID + k * P:half * HID + (k + 1) * P], ident[:, :])
                last.then_inc(xnt_psum, 1)

            def step3(b, u):
                lagging(lambda n, v: weighted_sum(n, v, 0), 0, b, u)
                lagging(xn_transposes, 3, b, u)
                lagging(lambda n, v: weighted_sum(n, v, 1), 0, b, u)

            over_batches(pe, step3, 3)

            def project(parts, sem_name, evac_name):
                def f(c):
                    for j in range(FP):
                        if due((c - 1) * FP + (j + 1)):
                            pe.wait_ge(evac_name, (c - 1) * FP + (j + 1))
                        for i in range(2):
                            ft = 2 * j + i
                            for n, (wp, xp) in enumerate(((0, 0), (0, 1), (1, 0))):
                                for k in range(KT):
                                    last = pe.matmul(bank[ft][:, :], parts[:, wp, k, ft * P:(ft + 1) * P], chunk_xq(c, xp, k),
                                                     start=(n == 0 and k == 0), stop=(n == 2 and k == KT - 1))
                        last.then_inc(sem_name, 1)
                return f

            gate_of = project(wg_parts, g_psum, g_evac)
            up_of = project(wu_parts, u_psum, u_evac)
            pe.wait_ge(w_parts, 9)
            pe.wait_ge(xnt_ready, BATCH)
            pe.wait_ge(xq_ready, 1)
            gate_of(0)
            with pe.Fori(1, CHUNKS) as c:
                pe.wait_ge(xq_ready, c + 1)
                gate_of(c)
            pe.wait_ge(g_evac, CHUNKS * FP)
            up_of(0)
            with pe.Fori(1, CHUNKS) as c:
                up_of(c)

            def down(n, v):
                pe.wait_ge(op_ready, 2 * n + 2)
                for t in range(4):
                    if due(4 * n + (t - 3)):
                        pe.wait_ge(yo_ready, 4 * n + (t - 3))
                    for q, (op, wp) in enumerate(((0, 0), (0, 1), (1, 0))):
                        for k in range(FT):
                            o = (op * FT + k) * CH + t * P
                            last = pe.matmul(bank[t][:, 0:HID], o_parts[v][:, o:o + P], wd_parts[:, wp, k, :],
                                             start=(q == 0 and k == 0), stop=(q == 2 and k == FT - 1))
                    last.then_inc(y_psum, 1)

            pe.wait_ge(u_evac, CHUNKS * FP)
            for v in range(2):
                down(v, v)
            with pe.Fori(1, CHUNKS // 2) as g:
                for v in range(2):
                    down(g * 2 + v, v)

        @block.vector
        def _(dve):
            dve.wait_ge(consts_loaded, 48)
            dve.tensor_reduce(red[:, 6:7], gate_w_raw[:, :, :], AX.XY, ALU.max, apply_absolute_value=True).then_inc(gw_max, 1)
            dve.tensor_copy(gate_w_sum[:, KT:2 * KT, :], gate_w_raw[:, 0:KT, :])
            dve.tensor_tensor(gate_w_sum[:, 0:KT, :], gate_w_raw[:, KT:2 * KT, :], gate_w_raw[:, 2 * KT:3 * KT, :],
                              ALU.add).then_inc(gw_sum, 1)
            dve.memset(gate_w_parts[:, :, :], 0.0).then_inc(gw_zero, 1)
            dve.wait_ge(gw_zero, 1)
            for h in range(NH):
                dve.memset(gate_w_parts[(h % 2) * DH:(h % 2 + 1) * DH, h // 2, 2 * NH + h:2 * NH + h + 1], 1.0 / DH)

            dve.wait_ge(w_loaded, 48)
            w3 = w_nat.rearrange("p (b k) -> p b k", k=BLOCK)
            dve.tensor_reduce(block_max[:, :], w3, AX.X, ALU.max, apply_absolute_value=True).then_inc(w_step, 1)
            dve.wait_ge(w_step, 1)
            dve.tensor_reduce(red[:, 0:1], block_max[:, :], AX.X, ALU.max).then_inc(w_rowmax, 1)
            dve.tensor_scalar(block_s[:, :], block_max[:, :], 1.0 / QMAX4, TINY, ALU.mult, ALU.max).then_inc(w_step, 1)
            dve.wait_ge(w_step, 2)
            dve.reciprocal(block_inv[:, :], block_s[:, :]).then_inc(w_step, 1)
            dve.wait_ge(w_step, 3)
            s_bc = block_s[:, :].unsqueeze(2).broadcast_to([P, STRIPS * 8, BLOCK])
            wi3 = w_int.rearrange("p (b k) -> p b k", k=BLOCK)
            inv_bc = block_inv[:, :].unsqueeze(2).broadcast_to([P, STRIPS * 8, BLOCK])
            dve.tensor_tensor(w3, w3, inv_bc, ALU.mult).then_inc(w_step, 1)
            dve.wait_ge(w_step, 4)
            dve.tensor_copy(w_int, w_nat).then_inc(w_step, 1)
            dve.wait_ge(w_step, 5)
            dve.tensor_tensor(w3, wi3, s_bc, ALU.mult).then_inc(w_dq, 1)
            dve.wait_ge(w_allmax, 1)
            dve.tensor_scalar(sc[:, WP2:WP2 + 1].bitcast(U32), allmax[:, 0:1].bitcast(U32), 0x7F800000, None, ALU.bitwise_and).then_inc(w_step, 1)
            dve.wait_ge(w_step, 6)
            dve.tensor_scalar(col(WP2), col(WP2), 2.0 ** -100, None, ALU.max).then_inc(w_step, 1)
            dve.wait_ge(w_step, 7)
            dve.reciprocal(col(CO), col(WP2)).then_inc(w_step, 1)
            dve.wait_ge(w_step, 8)
            dve.tensor_scalar(col(WMUL), col(CO), W_UNIT, None, ALU.mult)
            dve.tensor_scalar(col(WFAC), col(WP2), 1.0 / W_UNIT, None, ALU.mult).then_inc(w_fac, 1)
            for r in range(9):
                dve.wait_ge(w_sc, r + 1)
                t4 = w_tmp[r % 2].rearrange("p (i n) -> p i n", i=2)
                if r < 6:
                    w = (wg_parts, wu_parts)[r // 3]
                    hi, lo = (w[:, i, :, 2 * (r % 3) * P:(2 * (r % 3) + 2) * P] for i in range(2))
                else:
                    hi, lo = (wd_parts[:, i, 2 * (r - 6):2 * (r - 6) + 2, :] for i in range(2))
                dve.tensor_copy(hi, t4).then_inc(w_hi, 1)
                dve.wait_ge(w_hi, r + 1)
                dve.tensor_tensor(lo, t4, hi, ALU.subtract).then_inc(w_parts, 1)

            for i in range(BATCH // UNROLL):
                n = UNROLL * KT * SEQ
                dve.wait_ge(ctx_loaded[i], 16)
                dve.tensor_reduce(xmax[:, i:i + 1], at(A_CTX + i * n, n), AX.X, ALU.max, apply_absolute_value=True).then_inc(c_max, 1)
            dve.wait_ge(c_max, BATCH // UNROLL)
            dve.tensor_reduce(red[:, 7:8], xmax[:, 0:BATCH // UNROLL], AX.X, ALU.max).then_inc(gc_rowmax, 1)
            dve.wait_ge(gc_allmax, 1)
            dve.tensor_scalar(sc[:, P2_G:P2_C + 1].bitcast(U32), allmax[:, 6:8].bitcast(U32), 0x7F800000, None,
                              ALU.bitwise_and).then_inc(gate_scale_step, 1)
            dve.wait_ge(gate_scale_step, 1)
            dve.tensor_scalar(sc[:, P2_G:P2_C + 1], sc[:, P2_G:P2_C + 1], 2.0 ** -60, None, ALU.max).then_inc(gate_scale_step, 1)
            dve.wait_ge(gate_scale_step, 2)
            dve.reciprocal(sc[:, MUL_G:MUL_C + 1], sc[:, P2_G:P2_C + 1]).then_inc(gate_scale_step, 1)
            dve.wait_ge(gate_scale_step, 3)
            dve.tensor_scalar(sc[:, MUL_G:MUL_C + 1], sc[:, MUL_G:MUL_C + 1], W_UNIT, None, ALU.mult).then_inc(gate_scale_step, 1)
            dve.tensor_scalar(sc[:, FAC_G:FAC_C + 1], sc[:, P2_G:P2_C + 1], 1.0 / W_UNIT, None, ALU.mult).then_inc(gate_scale_step, 1)
            dve.wait_ge(gate_scale_step, 5)
            dve.tensor_tensor(col(FAC_CG), col(FAC_C), col(FAC_G), ALU.mult)
            dve.tensor_scalar(col(FAC_QG), col(FAC_G), 1.0 / Q_UNIT, None, ALU.mult)
            dve.wait_ge(gate_scale_step, 4)
            dve.tensor_scalar(col(FAC_S), col(FAC_C), DH ** -0.5 / Q_UNIT, None, ALU.mult).then_inc(gc_fac2, 1)
            dve.wait_ge(gw_sum, 1)
            dve.tensor_scalar(gate_w_sum[:, :, :], gate_w_sum[:, :, :], col(MUL_G), None, ALU.mult).then_inc(gate_scale_step, 1)
            dve.wait_ge(gate_scale_step, 6)
            dve.tensor_copy(gate_w_parts[:, :, 0:2 * NH], gate_w_sum[:, :, :]).then_inc(gate_scale_step, 1)
            dve.wait_ge(gate_scale_step, 7)
            dve.tensor_tensor(gate_w_parts[:, :, GC:GC + 2 * NH], gate_w_sum[:, :, :], gate_w_parts[:, :, 0:2 * NH],
                              ALU.subtract).then_inc(gw_ready, 1)

            reg = [None]

            def stats(n, v):
                s, p = v % 2, v // PAIR
                dve.wait_ge(x_loaded[p], 16 * (n // UNROLL + 1) if isinstance(n, int) else reg[0] * 16 + 16)
                for half in range(HALVES):
                    last = dve.bn_stats(bn_raw[:, s, half, :], x_of(n, half))
                last.then_inc(stats_raw, 1)
                dve.wait_ge(stats_raw, n + 1)
                apart(dve, n + 1)
                for half in range(HALVES):
                    last = dve.bn_aggr(mean_var[:, s, half, :], bn_raw[:, s, half, :])
                last.then_inc(stats_done, 1)

            def norm_q(n, v):
                s = v % 2
                dve.wait_ge(rstd_ready, n + 1)
                for half in range(HALVES):
                    last = dve.tensor_scalar(q_nat[s][:, half * HID:(half + 1) * HID], x_of(n, half),
                                             mean_var[:, s, half, 0:1], rstd[:, s, half, 0:1], ALU.subtract, ALU.mult)
                last.then_inc(q_ready, 1)

            def query_low(n, v):
                s = v % 2
                dve.wait_ge(q_hi, n + 1)
                dve.scalar_tensor_tensor(q_parts[s][:, KT * SEQ:], bank[s][:, :], Q_UNIT, q_parts[s][:, 0:KT * SEQ],
                                         ALU.mult, ALU.subtract).then_inc(qt_ready, 1)

            def context_low(n, v):
                s = v % 2
                dve.wait_ge(c_hi, n + 1)
                dve.scalar_tensor_tensor(c_parts[s][:, KT * SEQ:], ctx_of(n), col(MUL_C), c_parts[s][:, 0:KT * SEQ],
                                         ALU.mult, ALU.subtract).then_inc(c_lo, 1)

            def step1(b, u):
                lagging(norm_q, 1, b, u)
                lagging(stats, 0, b, u)
                lagging(context_low, 1, b, u)
                lagging(query_low, 1, b, u)

            for b in range(UNROLL):
                step1(b, b)
            with dve.Fori(1, BATCH // UNROLL) as it:
                reg[0] = it
                for u in range(UNROLL):
                    step1(it * UNROLL + u, u)
            step1(BATCH, 0)

            dve.wait_ge(gates_evac, BATCH)
            raw = gates_raw.rearrange("p s b (i j g) -> p (s b) i j g", i=2, j=2)
            dve.tensor_tensor(gate_sum[:, :, :, :], raw[:, :, :, 0, :], raw[:, :, :, 1, :], ALU.add).then_inc(m_gsum, 1)
            dve.wait_ge(m_gsum, 1)
            gates_flat = gates[:, :, :, :].rearrange("p s b g -> p (s b) g")
            dve.tensor_scalar(gate_sum[:, :, 1, 0:2 * NH], gate_sum[:, :, 1, 0:2 * NH], col(FAC_QG), None, ALU.mult).then_inc(m_gq, 1)
            dve.tensor_scalar(gates_flat[:, :, 2 * NH:GC], gate_sum[:, :, 0, 2 * NH:GC], col(FAC_C), None, ALU.mult)
            dve.wait_ge(m_gq, 1)
            dve.scalar_tensor_tensor(gates_flat[:, :, 0:2 * NH], gate_sum[:, :, 0, 0:2 * NH], col(FAC_CG),
                                     gate_sum[:, :, 1, 0:2 * NH], ALU.mult, ALU.add).then_inc(m_gates, 1)
            dve.wait_ge(m_gates, 1)
            bias_bc = lambda i: gate_bias[:, i * NH:(i + 1) * NH].unsqueeze(1).unsqueeze(1).broadcast_to([P, HALVES, BATCH, NH])
            dve.tensor_tensor(fz, gates[:, :, :, NH:2 * NH], bias_bc(1), ALU.add).then_inc(m_fz, 1)
            dve.wait_ge(m_fz, 1)
            dve.tensor_tensor(csum, gates[:, :, :, 0:NH], bias_bc(0), ALU.add).then_inc(m_ib, 1)
            dve.wait_ge(m_ln, 1)
            flat = lambda t: t.rearrange("p s b h -> p (s b h)")
            dve.scalar_tensor_tensor(flat(lf), flat(fz), 0.0, flat(fln), ALU.min, ALU.subtract).then_inc(m_lf, 1)
            dve.wait_ge(m_cs, 1)
            dve.wait_ge(m_ib, 1)
            dve.tensor_copy(flat(eneg), bank[0][:, 0:P]).then_inc(m_csc, 1)
            dve.wait_ge(m_csc, 1)
            dve.tensor_tensor(a_nat[:, :, :].rearrange("p s c -> p (s c)"), flat(csum), flat(eneg), ALU.subtract).then_inc(m_a, 1)
            dve.wait_ge(m_at, 1)
            dve.tensor_copy(a_row, bank[1][0:BATCH * NH, 0:SEQ]).then_inc(m_ac, 1)
            dve.wait_ge(m_ac, 1)
            dve.tensor_tensor_scan(run_max[:, :], a_row, a_row, -3.0e38, ALU.max, ALU.max).then_inc(m_scan, 1)
            dve.wait_ge(m_mt, 1)
            dve.tensor_tensor(flat(eneg), flat(eneg), bank[2][:, 0:P], ALU.add).then_inc(m_add, 1)

            def head_center(n, v):
                s = v % 2
                dve.wait_ge(pv_done, n + 1)
                for half in range(HALVES):
                    o = bank[2 * s + half][:, 0:NH * VC].rearrange("p (h c) -> p h c", h=NH)
                    last = dve.tensor_copy(o_cols[:, s, half * NH:(half + 1) * NH, :], o[:, :, DH:VC])
                last.then_inc(cols_ready, 1)
                dve.wait_ge(cols_ready, n + 1)
                if due(n - 1):
                    dve.wait_ge(x1_ready, n - 1)
                for half in range(HALVES):
                    o = bank[2 * s + half][:, 0:NH * VC].rearrange("p (h c) -> p h c", h=NH)
                    mean = o_cols[:, s, half * NH:(half + 1) * NH, 1:2].broadcast_to([P, NH, DH])
                    last = dve.tensor_tensor(head[s][:, half * HID:(half + 1) * HID].rearrange("p (h c) -> p h c", h=NH),
                                             o[:, :, 0:DH], mean, ALU.subtract)
                last.then_inc(head_ready, 1)
                fl = floor_nat[:, :, n * NH:(n + 1) * NH] if isinstance(n, int) else floor_nat[:, :, bass.ds(n * NH, NH)]
                dve.scalar_tensor_tensor(floor_n[:, s, :].rearrange("p (s h) -> p s h", s=HALVES),
                                         o_cols[:, s, :, 0].rearrange("p (s h) -> p s h", s=HALVES), -1.0, fl,
                                         ALU.mult, ALU.max).then_inc(n_half, 1)
                dve.wait_ge(n_half, n + 1)
                dve.tensor_tensor(floor_n[:, s, :], floor_n[:, s, :], o_cols[:, s, :, 0], ALU.max).then_inc(n_ready, 1)
                dve.wait_ge(n_ready, n + 1)
                dve.tensor_scalar(floor_w[:, s, :], floor_n[:, s, :], NORM_EPS, LN_EPS ** 0.5, ALU.add, ALU.mult).then_inc(w_ready, 1)

            def products(n, v, half):
                off, size = ((0, NH * SEQ), (NH * SEQ, NH * P))[half]
                part = decay[v % 2][:, off:off + size]
                dve.wait_ge(exp_done, 2 * n + (half + 1))
                dve.tensor_tensor(part, part, scores_of(n, off, size), ALU.mult).then_inc(c_ready, 1)

            def head_variance(n, v):
                s = v % 2
                dve.wait_ge(w_ready, n + 1)
                dve.tensor_tensor(floor_w2[:, s, :], floor_w[:, s, :], floor_w[:, s, :], ALU.mult)
                dve.wait_ge(sq_ready, n + 1)
                dve.tensor_reduce(sumsq[:, s, :], square.rearrange("p (g c) -> p g c", c=DH), AX.X, ALU.add).then_inc(ssq_ready, 1)
                dve.wait_ge(ssq_ready, n + 1)
                dve.scalar_tensor_tensor(head_var[:, s, :], sumsq[:, s, :], 1.0 / DH, floor_w2[:, s, :],
                                         ALU.mult, ALU.add).then_inc(var_ready, 1)

            def head_scale(n, v):
                s = v % 2
                dve.wait_ge(gain_ready, n + 1)
                h3 = head[s].rearrange("p (g c) -> p g c", c=DH)
                dve.tensor_tensor(h3, h3, head_gain[:, s, :].unsqueeze(2).broadcast_to([P, HALVES * NH, DH]),
                                  ALU.mult).then_inc(y_ready, 1)

            def stats2(n, v):
                s = v % 2
                dve.wait_ge(x1_ready, n + 1)
                for half in range(HALVES):
                    last = dve.bn_stats(bn_raw[:, s, half, :], x_of(n, half))
                last.then_inc(bn2_raw, 1)
                dve.wait_ge(bn2_raw, n + 1)
                apart(dve, n + 1)
                for half in range(HALVES):
                    last = dve.bn_aggr(mean_var[:, s, half, :], bn_raw[:, s, half, :])
                last.then_inc(bn2_done, 1)

            def norm2(n, v):
                s = v % 2
                dve.wait_ge(rstd2_ready, n + 1)
                if due(n):
                    dve.wait_ge(xnt_psum, n)
                for half in range(HALVES):
                    last = dve.tensor_scalar(xn[s][:, half * HID:(half + 1) * HID], x_of(n, half),
                                             mean_var[:, s, half, 0:1], rstd[:, s, half, 0:1], ALU.subtract, ALU.mult)
                last.then_inc(xn_ready, 1)

            def max_xn(n, v):
                dve.wait_ge(xnt_ready, n + 1)
                dst = xmax[:, n:n + 1] if isinstance(n, int) else xmax[:, bass.ds(n, 1)]
                dve.tensor_reduce(dst, scores_of(n, 0, 512), AX.X, ALU.max, apply_absolute_value=True).then_inc(xmax_ready, 1)

            def step3(b, u):
                lagging(head_center, 2, b, u)
                lagging(lambda n, v: products(n, v, 0), 0, b, u)
                lagging(head_variance, 2, b, u)
                lagging(lambda n, v: products(n, v, 1), 0, b, u)
                lagging(stats2, 3, b, u)
                lagging(max_xn, 4, b, u)
                lagging(head_scale, 2, b, u)
                lagging(norm2, 3, b, u)

            over_batches(dve, step3, 4)

            def partition_max(i, src, name):
                dve.tensor_reduce(red[:, i:i + 1], src, AX.X, ALU.max).then_inc(name, 1)

            dve.wait_ge(xmax_ready, BATCH)
            partition_max(1, xmax[:, :], red_x)
            dve.wait_ge(all_x, 1)
            dve.tensor_scalar(col(SX), allmax[:, 1:2], 1.0 / QMAX16, TINY, ALU.mult, ALU.max).then_inc(sx0, 1)
            dve.wait_ge(sx0, 1)
            dve.reciprocal(col(INV_X), col(SX)).then_inc(inv_x, 1)
            dve.tensor_tensor(col(CG), col(SX), col(WFAC), ALU.mult).then_inc(sx1, 1)
            dve.wait_ge(sx1, 1)

            dve.wait_ge(x1_stored, 16 * PAIRS)

            def split_x(c):
                dve.wait_ge(xi_ready, c + 1)
                o = c * (4 * CH)
                view = lambda part: (xq[:, o + part * 2 * CH:o + (part + 1) * 2 * CH] if isinstance(c, int)
                                     else xq[:, bass.ds(o + part * 2 * CH, 2 * CH)])
                dve.tensor_copy(view(0), x_int[0]).then_inc(x_hi, 1)
                dve.wait_ge(x_hi, c + 1)
                dve.tensor_tensor(view(1), x_int[0], view(0), ALU.subtract).then_inc(xq_ready, 1)

            def max_proj(evac, table, slot_of, done):
                def f(c):
                    for j in range(FP):
                        dve.wait_ge(evac, c * FP + (j + 1))
                        i = c * FP + j
                        dst = table[:, i:i + 1] if isinstance(i, int) else table[:, bass.ds(i, 1)]
                        dve.tensor_reduce(dst, slot_pair(slot_of(c), j), AX.X, ALU.max, apply_absolute_value=True).then_inc(done, 1)
                return f

            max_g = max_proj(g_evac, gmax, lambda c: c, gmax_done)
            split_x(0)
            with dve.Fori(1, CHUNKS) as c:
                split_x(c)
                max_g(c - 1)
            max_g(CHUNKS - 1)
            dve.wait_ge(gmax_done, CHUNKS * FP)
            partition_max(2, gmax[:, :], red_g)
            dve.wait_ge(all_g, 1)
            dve.tensor_tensor(col(SG), allmax[:, 2:3], col(CG), ALU.mult).then_inc(g_scale_step, 1)
            dve.wait_ge(g_scale_step, 1)
            dve.tensor_scalar(col(SG), col(SG), 1.0 / QMAX16, TINY, ALU.mult, ALU.max).then_inc(g_scale_step, 1)
            dve.wait_ge(g_scale_step, 2)
            dve.reciprocal(col(INV_G), col(SG)).then_inc(g_scale_step, 1)
            dve.wait_ge(g_scale_step, 3)
            dve.tensor_scalar(col(SGK), col(SG), 1.0 / 65536.0, None, ALU.mult)
            dve.tensor_tensor(col(INV_G), col(INV_G), col(CG), ALU.mult).then_inc(inv_g, 1)

            def max_gs(c, j):
                dve.wait_ge(gs_ready, c * FP + (j + 1))
                i = c * FP + j
                dst = gsmax[:, i:i + 1] if isinstance(i, int) else gsmax[:, bass.ds(i, 1)]
                dve.tensor_reduce(dst, int_pair(c, j), AX.X, ALU.max, apply_absolute_value=True).then_inc(gsmax_done, 1)

            def gate_chain(c, up_slot):
                for j in range(FP):
                    i = c * FP + j
                    dve.wait_ge(u_evac, c * FP + (j + 1))
                    dst = umax[:, i:i + 1] if isinstance(i, int) else umax[:, bass.ds(i, 1)]
                    dve.tensor_reduce(dst, slot_pair(up_slot, j), AX.X, ALU.max, apply_absolute_value=True).then_inc(umax_done, 1)
                    dve.wait_ge(sig_ready, c * FP + (j + 1))
                    dve.tensor_scalar(sigq[j], sig[j], 65536.0, 65535.0, ALU.mult, ALU.min).then_inc(sigq_ready, 1)
                    if j > 0:
                        max_gs(c, j - 1)
                    elif not isinstance(c, int) or c > 0:
                        max_gs(c - 1, FP - 1)

            gate_chain(0, 8)
            with dve.Fori(1, 4) as c:
                gate_chain(c, c + 8)
            with dve.Fori(4, CHUNKS) as c:
                gate_chain(c, c + 4)
            max_gs(CHUNKS - 1, FP - 1)

            dve.wait_ge(umax_done, CHUNKS * FP)
            dve.wait_ge(gsmax_done, CHUNKS * FP)
            dve.tensor_reduce(red[:, 3:4], gsmax[:, :], AX.X, ALU.max).then_inc(red_gs, 1)
            dve.tensor_reduce(red[:, 4:5], umax[:, :], AX.X, ALU.max).then_inc(red_u, 1)
            dve.wait_ge(all_gs, 1)
            dve.tensor_tensor(col(SGS), allmax[:, 3:4], col(SGK), ALU.mult).then_inc(gs_scale_step, 1)
            dve.wait_ge(gs_scale_step, 1)
            dve.tensor_scalar(col(SGS), col(SGS), 1.0 / QMAX16, TINY, ALU.mult, ALU.max).then_inc(gs_scale_step, 1)
            dve.wait_ge(gs_scale_step, 2)
            dve.reciprocal(col(INV_GS), col(SGS)).then_inc(gs_scale_step, 1)
            dve.wait_ge(gs_scale_step, 3)
            dve.tensor_tensor(col(INV_GS), col(INV_GS), col(SGK), ALU.mult).then_inc(inv_gs, 1)
            dve.wait_ge(inv_gs, 1)
            dve.wait_ge(all_u, 1)
            dve.tensor_tensor(col(SU), allmax[:, 4:5], col(CG), ALU.mult).then_inc(u_scale_step, 1)
            dve.wait_ge(u_scale_step, 1)
            dve.tensor_scalar(col(SU), col(SU), 1.0 / QMAX16, TINY, ALU.mult, ALU.max).then_inc(u_scale_step, 1)
            dve.wait_ge(u_scale_step, 2)
            dve.reciprocal(col(CU), col(SU)).then_inc(u_scale_step, 1)
            dve.wait_ge(u_scale_step, 3)
            dve.tensor_tensor(col(INV_U), col(CU), col(CG), ALU.mult).then_inc(inv_u, 1)
            dve.tensor_tensor(col(SGU), col(SGS), col(SU), ALU.mult).then_inc(u_scale_step, 1)
            dve.wait_ge(u_scale_step, 4)

            def max_o(k, j, slot):
                if j == 0:
                    dve.wait_ge(o_first, k + 1)
                else:
                    dve.wait_ge(o_rest, k * (FP - 1) + j)
                i = k * FP + j
                dst = omax[:, i:i + 1] if isinstance(i, int) else omax[:, bass.ds(i, 1)]
                dve.tensor_reduce(dst, int_pair(slot, j), AX.X, ALU.max, apply_absolute_value=True).then_inc(omax_done, 1)

            def combine(k, gate_slot, up_slot, last_slot):
                g, o = int_pair(gate_slot, 0), int_pair(up_slot, 0)
                dve.tensor_scalar(g, g, col(INV_GS), None, ALU.mult).then_inc(gsq_first, 1)
                if last_slot is not None:
                    max_o(k - 1, 1, last_slot)
                dve.wait_ge(gsq_first, k + 1)
                dve.wait_ge(uq_ready, k * FP + 1)
                dve.tensor_tensor(o, g, o, ALU.mult).then_inc(o_first, 1)
                if last_slot is not None:
                    max_o(k - 1, 2, last_slot)
                max_o(k, 0, up_slot)

            combine(0, 4, O_SLOTS[0], None)
            with dve.Fori(1, 4) as k:
                combine(k, k + 4, k + 8, k + 7)
            for k in range(4, CHUNKS):
                combine(k, k - 4, O_SLOTS[k], O_SLOTS[k - 1])
            for j in (1, 2):
                max_o(CHUNKS - 1, j, O_SLOTS[CHUNKS - 1])

            dve.wait_ge(omax_done, CHUNKS * FP)
            partition_max(5, omax[:, :], red_o)
            dve.wait_ge(all_o, 1)
            dve.tensor_tensor(col(SO), allmax[:, 5:6], col(SGU), ALU.mult).then_inc(o_scale_step, 1)
            dve.wait_ge(o_scale_step, 1)
            dve.tensor_scalar(col(SO), col(SO), 1.0 / QMAX16, TINY, ALU.mult, ALU.max).then_inc(o_scale_step, 1)
            dve.wait_ge(o_scale_step, 2)
            dve.reciprocal(col(CO), col(SO)).then_inc(o_scale_step, 1)
            dve.wait_ge(o_scale_step, 3)
            dve.tensor_tensor(col(INV_O), col(CO), col(SGU), ALU.mult).then_inc(inv_o, 1)
            dve.tensor_tensor(col(SO_), col(SO), col(WFAC), ALU.mult).then_inc(co_ready, 1)
            dve.wait_ge(co_ready, 1)

            def split_o(n, v):
                for j in range(2):
                    dve.wait_ge(oi_ready, 2 * n + (j + 1))
                    if due(4 * n - 4):
                        dve.wait_ge(y_psum, 4 * n - 4)
                    hi, lo = (o_parts[v][:, (i * FT + 3 * j) * CH:(i * FT + 3 * j + 3) * CH] for i in range(2))
                    dve.tensor_copy(hi, o_int[j]).then_inc(o_hi, 1)
                    dve.wait_ge(o_hi, 2 * n + (j + 1))
                    dve.tensor_tensor(lo, o_int[j], hi, ALU.subtract).then_inc(op_ready, 1)

            def finish(n, v, count):
                dve.wait_ge(x1_back[v], count * 16 + 16)
                if due(count * 16):
                    dve.wait_ge(y_stored[v], count * 16)
                for t in range(4):
                    dve.wait_ge(y_psum, 4 * n + (t + 1))
                    sl = slice(t * HID, (t + 1) * HID)
                    dve.scalar_tensor_tensor(y_out[v][:, sl], bank[t][:, 0:HID], col(SO_), x1_in[v][:, sl],
                                             ALU.mult, ALU.add).then_inc(yo_ready, 1)

            split_o(0, 0)
            split_o(1, 1)
            finish(0, 0, 0)
            def two_chunks(g):
                split_o(g * 2, 0)
                finish(g * 2 - 1, 1, g - 1)
                split_o(g * 2 + 1, 1)
                finish(g * 2, 0, g)

            two_chunks(1)
            with dve.Fori(2, CHUNKS // 2) as g:
                two_chunks(g)
            finish(CHUNKS - 1, 1, CHUNKS // 2 - 1)


def kernel(x, ctx_1024, L0_xattn_igate_kernel, L0_xattn_igate_bias, L0_xattn_fgate_kernel, L0_xattn_fgate_bias,
           L0_xattn_outnorm_scale, L0_ffn_w_gate, L0_ffn_w_up, L0_ffn_w_down):
    import numpy as np
    import concourse.bacc as bacc
    from concourse.bass_utils import run_bass_kernel_spmd

    x, c = np.asarray(x), np.asarray(ctx_1024)
    natural = lambda t: t.reshape(PAIRS, PAIR, HALVES, P, HID).transpose(0, 3, 1, 2, 4).reshape(PAIRS, P, -1)
    gate_w = np.concatenate([np.asarray(L0_xattn_igate_kernel), np.asarray(L0_xattn_fgate_kernel)], axis=1)
    arrays = {
        "x": natural(x),
        "ctx_nat": natural(c),
        "ctx_t": c.reshape(-1, UNROLL, SEQ, KT, P).transpose(0, 4, 1, 3, 2).reshape(BATCH // UNROLL, P, -1),
        "gate_w": gate_w.reshape(3 * KT, P, 2 * NH).transpose(1, 0, 2).reshape(P, -1),
        "gate_b": np.concatenate([np.asarray(L0_xattn_igate_bias), np.asarray(L0_xattn_fgate_bias)]),
        "norm_scale": np.asarray(L0_xattn_outnorm_scale),
        "w_gate": np.asarray(L0_ffn_w_gate),
        "w_up": np.asarray(L0_ffn_w_up),
        "w_down": np.asarray(L0_ffn_w_down),
    }
    arrays = {n: np.ascontiguousarray(a) for n, a in arrays.items()}
    nc = bacc.Bacc("TRN2", target_bir_lowering=False, num_devices=1)
    args = [nc.dram_tensor(n, a.shape, mybir.dt.from_np(a.dtype), kind="ExternalInput").ap() for n, a in arrays.items()]
    out = nc.dram_tensor("out", (PAIRS, P, PAIR * HALVES * HID), F32, kind="ExternalOutput").ap()
    bass_xattn_ffn(nc, *args, out)
    y = run_bass_kernel_spmd(nc, [arrays], core_ids=[0]).results[0]["out"]
    return y.reshape(PAIRS, P, PAIR, HALVES, HID).transpose(0, 2, 3, 1, 4).reshape(BATCH, SEQ, HID)
```

```python
from contextlib import ExitStack

import concourse.bass as bass
from concourse import mybir

F32 = mybir.dt.float32
F16 = mybir.dt.float16
I16 = mybir.dt.int16
I32 = mybir.dt.int32
U32 = mybir.dt.uint32
ALU = mybir.AluOpType
ACT = mybir.ActivationFunctionType
AX = mybir.AxisListType

P = 128
BATCH = 16
SEQ = 256
HID = 256
NH = 4
DH = HID // NH
FF = 768
HALVES = SEQ // P
KT = HID // P
UNROLL = 4
PAIR = 2
PAIRS = BATCH // PAIR
VC = DH + 2
GC = 3 * NH
GW = 2 * GC
SCORES = NH * (SEQ + P)
CH = 512
CHUNKS = BATCH * SEQ // CH
FT = FF // P
SLOT = FT * CH
PAIRC = 2 * CH
FP = FT // 2
ACT_GATES = CHUNKS - 2
BLOCK = 32
STRIPS = 3 * FF * HID // (P * HID)
W_PARTS = BATCH - UNROLL
W_LAG = UNROLL + 1
W_PART = STRIPS * HID // W_PARTS
QMAX16 = 2.0 ** 15 - 1.0
QMAX4 = 7.0
LN_EPS = 1e-5
NORM_EPS = 1e-6
TINY = 1e-12
W_UNIT = 4096.0
Q_UNIT = 256.0
NEVER = 1.0e30


def bass_xattn_ffn(nc, x, ctx_nat, ctx_t, gate_w, gate_b, norm_scale, w_gate, w_up, w_down, out):
    x1_dram = nc.dram_tensor("x1_spill", (PAIRS, P, PAIR * HALVES * HID), F32, kind="Internal").ap()
    max_dram = nc.dram_tensor("running_max", (BATCH * NH, SEQ), F32, kind="Internal").ap()
    up_dram = nc.dram_tensor("up_spill", (4, P, SLOT), F32, kind="Internal").ap()

    es = ExitStack()
    with es:
        def sb(name, shape, dt=F32):
            return es.enter_context(nc.sbuf_tensor(name, shape, dt))

        def sem(name):
            return es.enter_context(nc.semaphore(name))

        A_TMP = 8 * SLOT
        A_X = 12 * SLOT
        arena = sb("arena", [P, A_X + BATCH * HALVES * HID])

        def at(off, n):
            return arena[:, off:off + n]

        def at_dyn(off, n):
            return arena[:, bass.ds(off, n)]

        def slot_pair(slot, j):
            if isinstance(slot, int):
                return at(slot * SLOT + j * PAIRC, PAIRC)
            return at_dyn(slot * SLOT + j * PAIRC, PAIRC)

        def int_pair(slot, j):
            return slot_pair(slot, j).bitcast(I32)

        wg_area = sb("wg_area", [P, 2 * FP * PAIRC], F16)
        wg_parts = wg_area[:, 0:2 * KT * FF].rearrange("p (i k f) -> p i k f", i=2, k=KT)
        wu_parts = sb("wu_parts", [P, 2, KT, FF], F16)
        wd_parts = sb("wd_parts", [P, 2, FT, HID], F16)
        gates = sb("gates", [P, HALVES, BATCH, GC])
        scale_row = sb("scale_row", [P, HID])
        ident = sb("ident", [P, P])
        tri = sb("tri", [P, P])
        ones = sb("ones", [P, P])
        gate_w_raw = sb("gate_w_raw", [P, 3 * KT, 2 * NH])
        gate_w_parts = sb("gate_w_parts", [P, 2 * KT, GW], F16)
        gate_bias = sb("gate_bias", [P, 2 * NH])
        a_nat = sb("a_nat", [P, HALVES, BATCH * NH])
        floor_nat = sb("floor_nat", [P, HALVES, BATCH * NH])
        run_max = sb("run_max", [BATCH * NH, SEQ])
        bn_raw = sb("bn_raw", [P, 2, HALVES, 6])
        mean_var = sb("mean_var", [P, 2, HALVES, 2])
        rstd = sb("rstd", [P, 2, HALVES, 1])
        shift = sb("shift", [P, 2, HALVES])
        minus_half = sb("minus_half", [P, HALVES * NH])
        o_cols = sb("o_cols", [P, 2, HALVES * NH, 2])
        floor_n = sb("floor_n", [P, 2, HALVES * NH])
        floor_w = sb("floor_w", [P, 2, HALVES * NH])
        floor_w2 = sb("floor_w2", [P, 2, HALVES * NH])
        sumsq = sb("sumsq", [P, 2, HALVES * NH])
        head_var = sb("head_var", [P, 2, HALVES * NH])
        head_gain = sb("head_gain", [P, 2, HALVES * NH])
        xmax = sb("xmax", [P, BATCH])
        gmax = sb("gmax", [P, CHUNKS * FP])
        umax = sb("umax", [P, CHUNKS * FP])
        gsmax = sb("gsmax", [P, CHUNKS * FP])
        omax = sb("omax", [P, CHUNKS * FP])
        red = sb("red", [P, 8])
        allmax = sb("allmax", [P, 8])
        sc = sb("sc", [P, 32])

        q_nat = [at(A_TMP + i * 512, 512) for i in range(2)]
        q_parts = [at(A_TMP + 1024 + i * 512, 512).bitcast(F16) for i in range(2)]
        c_parts = [at(A_TMP + 2048 + i * 512, 512).bitcast(F16) for i in range(2)]
        gates_raw = at(A_TMP + 3072, HALVES * BATCH * 2 * GW).rearrange("p (s b g) -> p s b g", s=HALVES, b=BATCH)
        w_int = at(A_TMP + 5376, W_PART // 2).bitcast(I16)
        block_max = at(A_TMP + 5568, STRIPS * HID // BLOCK)
        block_s, block_inv = [at(A_TMP + 5712 + i * W_PART // BLOCK, W_PART // BLOCK) for i in range(2)]
        w_tmp = [at(A_TMP + 6144 + i * 512, 512) for i in range(2)]
        A_W = A_TMP + 7680
        w_nat = at(A_W, STRIPS * HID)
        gate_sum = at(A_TMP + 4608, HALVES * BATCH * 2 * GC).rearrange("p (b i g) -> p b i g", i=2, g=GC)
        A_CTX = BATCH * (SCORES - KT * SEQ)
        gate_w_sum = at(A_TMP + 7168, 4 * KT * NH).rearrange("p (k g) -> p k g", g=2 * NH)
        ctx_scale = at(A_TMP + 7200, 3 * BATCH).rearrange("p (i b) -> p i b", i=3)
        fz, fabs, fexp, fln, lf, csum, eneg = [
            at(A_TMP + i * P, P).rearrange("p (s b h) -> p s b h", s=HALVES, b=BATCH) for i in range(7)]
        a_row = at(A_TMP + 1024, SEQ)[0:BATCH * NH, :]
        max_bc = [at(A_TMP + i * 1024, 1024).rearrange("p (h s) -> p h s", h=NH) for i in range(2)]
        max_hi = [at(A_TMP + 2048 + i * 512, 512).rearrange("p (h s) -> p h s", h=NH) for i in range(2)]
        decay = [at(A_TMP + 9216 + i * SCORES, SCORES) for i in range(2)]
        head = [at(A_TMP + 5184 + i * 512, 512) for i in range(2)]
        square = at(A_TMP + 6208, 512)
        xn = [at(A_TMP + 6720 + i * 512, 512) for i in range(2)]
        v_aug = [at(A_TMP + 3072 + i * PAIR * HALVES * NH * VC, PAIR * HALVES * NH * VC)
                 .rearrange("p (b s h c) -> p b s h c", b=PAIR, s=HALVES, h=NH) for i in range(2)]
        x_int = [at(A_TMP + i * 512, 512).bitcast(I16) for i in range(2)]
        xq = arena[:, A_X:A_X + 8192].bitcast(F16)
        sig = [wg_area[:, 2 * j * PAIRC:2 * (j + 1) * PAIRC].bitcast(F32) for j in range(FP)]
        sigq = [wg_area[:, 2 * j * PAIRC:2 * (j + 1) * PAIRC].bitcast(I32) for j in range(FP)]
        o_parts = [at(i * SLOT, SLOT).bitcast(F16) for i in range(2)]
        o_int = [at(2 * SLOT + i * SLOT // 4, SLOT // 4).bitcast(I16) for i in range(2)]
        x1_in = [at(3 * SLOT + i * 1024, 1024) for i in range(2)]
        y_out = [at(6 * SLOT + i * 1024, 1024) for i in range(2)]

        x_res = at(A_X, BATCH * HALVES * HID)

        SX, INV_X, CG, SG, INV_G, SGK, CU, SU, INV_U, SGS, INV_GS, OUT_SCALE, SO, INV_O, CO, WMUL, WFAC, WP2, SGU, \
            P2_G, P2_C, MUL_G, MUL_C, FAC_G, FAC_QG = range(25)

        def col(i):
            return sc[:, i:i + 1]

        psum = es.enter_context(nc.psum_tensor("psum", [P, 8, CH], F32))
        bank = [psum[:, i, :] for i in range(8)]
        bank_pair = [psum[:, 2 * i:2 * i + 2, :].rearrange("p i n -> p (i n)") for i in range(4)]
        ORDER = [4, 5, 6, 7, 0, 1, 2, 3]
        O_SLOTS = [8, 9, 10, 11, 12, 13, 4, 5]
        passed = sem("passed")
        consts_loaded = sem("consts_loaded")
        w_loaded = sem("w_loaded")
        consts_set = sem("consts_set")
        masks_zeroed = sem("masks_zeroed")
        w_step = sem("w_step")
        w_rowmax = sem("w_rowmax")
        w_allmax = sem("w_allmax")
        w_dq = sem("w_dq")
        w_scale_step = sem("w_scale_step")
        w_rounded = sem("w_rounded")
        w_fac = sem("w_fac")
        w_tr = sem("w_tr")
        w_sc = sem("w_sc")
        w_hi = sem("w_hi")
        w_parts = sem("w_parts")
        stats_raw = sem("stats_raw")
        stats_done = sem("stats_done")
        rstd_eps = sem("rstd_eps")
        rstd_ready = sem("rstd_ready")
        q_ready = sem("q_ready")
        q_trans = sem("q_trans")
        qt_ready = sem("qt_ready")
        gates_done = sem("gates_done")
        gates_evac = sem("gates_evac")
        scores_ready = sem("scores_ready")
        scores_evac = sem("scores_evac")
        gw_zero = sem("gw_zero")
        gw_sum = sem("gw_sum")
        gw_max = sem("gw_max")
        c_max = sem("c_max")
        gc_rowmax = sem("gc_rowmax")
        gc_allmax = sem("gc_allmax")
        gate_scale_step = sem("gate_scale_step")
        gc_scales = sem("gc_scales")
        gw_ready = sem("gw_ready")
        c_hi = sem("c_hi")
        c_lo = sem("c_lo")
        q_hi = sem("q_hi")
        m_gates_step = sem("m_gates_step")
        m_gates = sem("m_gates")
        m_fz = sem("m_fz")
        m_softplus_step = sem("m_softplus_step")
        m_ln = sem("m_ln")
        m_lf = sem("m_lf")
        m_ib = sem("m_ib")
        m_cs = sem("m_cs")
        m_scan_scaled = sem("m_scan_scaled")
        m_a = sem("m_a")
        m_at = sem("m_at")
        m_scan = sem("m_scan")
        m_max_stored = sem("m_max_stored")
        m_mt = sem("m_mt")
        m_add = sem("m_add")
        m_floor = sem("m_floor")
        masked = sem("masked")
        v_ready = sem("v_ready")
        exp_done = sem("exp_done")
        c_ready = sem("c_ready")
        pv_done = sem("pv_done")
        cols_ready = sem("cols_ready")
        head_ready = sem("head_ready")
        sq_ready = sem("sq_ready")
        ssq_ready = sem("ssq_ready")
        n_half = sem("n_half")
        n_ready = sem("n_ready")
        w_ready = sem("w_ready")
        w2_ready = sem("w2_ready")
        var_ready = sem("var_ready")
        gain_ready = sem("gain_ready")
        y_ready = sem("y_ready")
        ys_ready = sem("ys_ready")
        x1_ready = sem("x1_ready")
        bn2_raw = sem("bn2_raw")
        bn2_done = sem("bn2_done")
        rstd2_eps = sem("rstd2_eps")
        rstd2_ready = sem("rstd2_ready")
        last_scaled = sem("last_scaled")
        last_x1 = sem("last_x1")
        shift_ready = sem("shift_ready")
        xn_ready = sem("xn_ready")
        xnt_psum = sem("xnt_psum")
        xnt_ready = sem("xnt_ready")
        xmax_ready = sem("xmax_ready")
        x1_stored = sem("x1_stored")
        red_x = sem("red_x")
        all_x = sem("all_x")
        x_scale_step = sem("x_scale_step")
        inv_x = sem("inv_x")
        xi_ready = sem("xi_ready")
        x_hi = sem("x_hi")
        xq_ready = sem("xq_ready")
        g_psum = sem("g_psum")
        g_evac = sem("g_evac")
        gmax_done = sem("gmax_done")
        red_g = sem("red_g")
        all_g = sem("all_g")
        g_scale_step = sem("g_scale_step")
        inv_g = sem("inv_g")
        u_psum = sem("u_psum")
        u_evac = sem("u_evac")
        umax_done = sem("umax_done")
        gq_ready = sem("gq_ready")
        sig_ready = sem("sig_ready")
        sigq_ready = sem("sigq_ready")
        gs_ready = sem("gs_ready")
        gsmax_done = sem("gsmax_done")
        red_gs = sem("red_gs")
        all_gs = sem("all_gs")
        gs_scale_step = sem("gs_scale_step")
        inv_gs = sem("inv_gs")
        red_u = sem("red_u")
        all_u = sem("all_u")
        u_scale_step = sem("u_scale_step")
        inv_u = sem("inv_u")
        uq_ready = sem("uq_ready")
        gsq_first = sem("gsq_first")
        gsq_first_act = sem("gsq_first_act")
        gsq_rest = sem("gsq_rest")
        o_first = sem("o_first")
        o_rest = sem("o_rest")
        omax_done = sem("omax_done")
        red_o = sem("red_o")
        all_o = sem("all_o")
        o_scale_step = sem("o_scale_step")
        inv_o = sem("inv_o")
        co_ready = sem("co_ready")
        oi_ready = sem("oi_ready")
        oi_first = sem("oi_first")
        o_hi = sem("o_hi")
        op_ready = sem("op_ready")
        y_psum = sem("y_psum")
        yo_ready = sem("yo_ready")
        x_loaded = [sem(f"x_loaded{i}") for i in range(2)]
        ctx_loaded = [sem(f"ctx_loaded{i}") for i in range(BATCH // UNROLL)]
        max_loaded = [sem(f"max_loaded{i}") for i in range(2)]
        v_loaded = [sem(f"v_loaded{i}") for i in range(2)]
        up_spilled = [sem(f"up_spilled{i}") for i in range(4)]
        up_back = [sem(f"up_back{i}") for i in range(4)]
        x1_back = [sem(f"x1_back{i}") for i in range(2)]
        y_stored = [sem(f"y_stored{i}") for i in range(2)]

        def due(count):
            return not isinstance(count, int) or count > 0

        def apart(eng, count):
            if not isinstance(count, int):
                eng.sem_inc(passed, 1)

        def over_batches(eng, steps, tail=0, groups=1):
            for b in range(groups * UNROLL):
                steps(b, b % UNROLL)
            with eng.Fori(groups, BATCH // UNROLL) as it:
                for u in range(UNROLL):
                    steps(it * UNROLL + u, u)
            for b in range(BATCH, BATCH + tail):
                steps(b, b % UNROLL)

        def lagging(part, lag, b, u):
            n = b - lag
            if isinstance(b, int) and not 0 <= n < BATCH:
                return
            part(n, (u - lag) % UNROLL)

        def lagging_from(first, part, lag, b, u):
            if not isinstance(b, int) or b - lag >= first:
                lagging(part, lag, b, u)

        def place(h):
            return (h % 2) * 2 + h // 2

        def x_of(n, half):
            off = A_X + n * (HALVES * HID) + half * HID
            return at(off, HID) if isinstance(n, int) else at_dyn(off, HID)

        def x_batch(n):
            off = A_X + n * (HALVES * HID)
            return at(off, HALVES * HID) if isinstance(n, int) else at_dyn(off, HALVES * HID)

        def ctx_of(n):
            off = A_CTX + n * (KT * SEQ)
            return at(off, KT * SEQ) if isinstance(n, int) else at_dyn(off, KT * SEQ)

        def scale_of(i, n):
            return ctx_scale[:, i, n:n + 1] if isinstance(n, int) else ctx_scale[:, i, bass.ds(n, 1)]

        def scores_of(n, off, size):
            o = n * SCORES + off
            return at(o, size) if isinstance(n, int) else at_dyn(o, size)

        def chunk_xq(c, part, k):
            o = c * (4 * CH) + part * (2 * CH) + k * CH
            return xq[:, o:o + CH] if isinstance(c, int) else xq[:, bass.ds(o, CH)]

        block = es.enter_context(nc.Block())

        @block.sync
        def _(sp):
            sp.dma_start(gate_w_raw[:, :, :].rearrange("p k g -> p (k g)"), gate_w).then_inc(consts_loaded, 16)
            sp.dma_start(gate_bias[:, :], gate_b.partition_broadcast(P)).then_inc(consts_loaded, 16)
            sp.dma_start(scale_row[:, :], norm_scale.partition_broadcast(P)).then_inc(consts_loaded, 16)

            def x_pair(b):
                off = A_X + b * (HALVES * HID)
                return at(off, PAIR * HALVES * HID) if isinstance(b, int) else at_dyn(off, PAIR * HALVES * HID)

            def dram_pair(t, pair):
                return t[pair, :, :] if isinstance(pair, int) else t[bass.ds(pair, 1), :, :].rearrange("a p n -> (a p) n")

            def load_x(g):
                for p in range(UNROLL // PAIR):
                    sp.wait_ge(x_loaded[p], g * 16)
                    sp.dma_start(x_pair(g * UNROLL + p * PAIR), dram_pair(x, g * (UNROLL // PAIR) + p)).then_inc(x_loaded[p], 16)

            sp.dma_start(x_pair(0), dram_pair(x, 0)).then_inc(x_loaded[0], 16)
            for i in range(BATCH // UNROLL):
                n = UNROLL * KT * SEQ
                sp.dma_start(at(A_CTX + i * n, n), ctx_t[i, :, :]).then_inc(ctx_loaded[i], 16)
                if i == 1:
                    sp.dma_start(x_pair(PAIR), dram_pair(x, 1)).then_inc(x_loaded[1], 16)
            for i, w in enumerate((w_gate, w_up)):
                sp.dma_start(w_nat[:, i * FT * HID:(i + 1) * FT * HID].rearrange("p (s k) -> p s k", k=HID),
                             w.rearrange("(s p) k -> p s k", p=P)).then_inc(w_loaded, 16)
            sp.dma_start(w_nat[:, 2 * FT * HID:].rearrange("p (r k) -> p r k", k=FF),
                         w_down.rearrange("(r p) k -> p r k", p=P)).then_inc(w_loaded, 16)
            with sp.Fori(1, BATCH // UNROLL) as g:
                load_x(g)

            def load_v(pair, p):
                for i in range(PAIR):
                    sp.dma_start(v_aug[p][:, i, :, :, 0:DH],
                                 dram_pair(ctx_nat, pair)[:, i * HALVES * HID:(i + 1) * HALVES * HID]
                                 .rearrange("p (s h c) -> p s h c", s=HALVES, h=NH)).then_inc(v_loaded[p], 16)

            sp.wait_ge(m_gates, 1)
            for p in range(2):
                load_v(p, p)

            sp.wait_ge(m_scan, 1)
            sp.dma_start(max_dram, run_max[:, :]).then_inc(m_max_stored, 16)
            sp.wait_ge(m_max_stored, 16)
            sp.wait_ge(m_floor, 1)

            def load_max(n, u):
                if due((n - 1) * 2):
                    sp.wait_ge(exp_done, (n - 1) * 2)
                rows = max_dram[n * NH:(n + 1) * NH, :] if isinstance(n, int) else max_dram[bass.ds(n * NH, NH), :]
                sp.dma_start(max_bc[u % 2].rearrange("p h s -> p (h s)"),
                             rows.rearrange("h s -> (h s)").partition_broadcast(P)).then_inc(max_loaded[u % 2], 16)

            def loads3(g):
                for u in range(UNROLL):
                    n = g * UNROLL + u
                    load_max(n, u)
                    if u % PAIR == 0:
                        sp.wait_ge(pv_done, n - 2)
                        load_v(g * (UNROLL // PAIR) + u // PAIR, u // PAIR)
                    if u % PAIR == 1:
                        store_x1(g - 1, u)

            def store_x1(g, u):
                if isinstance(g, int) and g < 0:
                    return
                n = g * UNROLL + u
                sp.wait_ge(x1_ready, n + 1)
                sp.dma_start(dram_pair(x1_dram, g * (UNROLL // PAIR) + u // PAIR), x_pair(n - 1)).then_inc(x1_stored, 16)

            for u in range(UNROLL):
                load_max(u, u)
            with sp.Fori(1, BATCH // UNROLL) as g:
                loads3(g)
            store_x1(BATCH // UNROLL - 1, 1)
            sp.wait_ge(last_x1, 2)
            sp.dma_start(dram_pair(x1_dram, PAIRS - 1), x_pair(BATCH - PAIR)).then_inc(x1_stored, 16)

            for c in range(4):
                sp.wait_ge(umax_done, (c + 1) * FP)
                sp.dma_start(up_dram[c, :, :], at((c + 8) * SLOT, SLOT)).then_inc(up_spilled[c], 16)
            for c in range(4):
                sp.wait_ge(up_spilled[c], 16)
            sp.wait_ge(u_psum, CHUNKS * FP)
            for c in range(4):
                if c >= 2:
                    sp.wait_ge(o_first, c - 1)
                    sp.wait_ge(o_rest, (FP - 1) * (c - 1))
                sp.dma_start(at(O_SLOTS[c + 4] * SLOT, SLOT), up_dram[c, :, :]).then_inc(up_back[c], 16)

            sp.wait_ge(omax_done, CHUNKS * FP)
            def store_y(k):
                sp.wait_ge(yo_ready, (k + 1) * 4)
                sp.dma_start(out[ORDER[k], :, :], y_out[k % 2]).then_inc(y_stored[k % 2], 16)

            for k in range(CHUNKS):
                if due((k - 1) * 4):
                    sp.wait_ge(yo_ready, (k - 1) * 4)
                sp.dma_start(x1_in[k % 2], x1_dram[ORDER[k], :, :]).then_inc(x1_back[k % 2], 16)
                if k >= 1:
                    store_y(k - 1)
            store_y(CHUNKS - 1)
            for i in range(2):
                sp.wait_ge(y_stored[i], 16 * CHUNKS // 2)

        @block.gpsimd
        def _(pool):
            pool.memset(ident[:, :], 0.0).then_inc(masks_zeroed, 1)
            pool.memset(tri[:, :], 1.0).then_inc(masks_zeroed, 1)
            pool.memset(ones[:, :], 1.0)
            pool.memset(minus_half[:, :], -0.5)
            pool.wait_ge(masks_zeroed, 1)
            pool.affine_select(out=ident[:, :], in_=ident[:, :], compare_op=ALU.not_equal, fill=1.0, base=0,
                               pattern=[[-1, P]], channel_multiplier=1)
            pool.wait_ge(masks_zeroed, 2)
            pool.affine_select(out=tri[:, :], in_=tri[:, :], compare_op=ALU.is_ge, fill=0.0, base=0,
                               pattern=[[1, P]], channel_multiplier=-1).then_inc(consts_set, 1)

            def rstd1(n, v):
                s = v % 2
                pool.wait_ge(stats_done, n + 1)
                apart(pool, n + 1)
                pool.tensor_scalar(rstd[:, s, :, :], mean_var[:, s, :, 1:2], LN_EPS, None, ALU.add).then_inc(rstd_eps, 1)
                pool.wait_ge(rstd_eps, n + 1)
                apart(pool, n + 1)
                pool.tensor_tensor(rstd[:, s, :, 0], rstd[:, s, :, 0], minus_half[:, 0:HALVES], ALU.pow).then_inc(rstd_ready, 1)

            rstd1(0, 0)
            rstd1(1, 1)
            pool.wait_ge(gw_max, 1)
            pool.wait_ge(gc_rowmax, 1)
            pool.partition_all_reduce(allmax[:, 6:8], red[:, 6:8], P, bass.bass_isa.ReduceOp.max).then_inc(gc_allmax, 1)

            rstd1(2, 2)
            rstd1(3, 3)
            pool.wait_ge(gc_rowmax, 2)
            pool.partition_all_reduce(allmax[:, 5:6], red[:, 5:6], P, bass.bass_isa.ReduceOp.max).then_inc(gc_allmax, 1)
            over_batches(pool, lambda b, u: lagging_from(UNROLL, rstd1, 0, b, u))

            pool.wait_ge(w_rowmax, 1)
            pool.partition_all_reduce(allmax[:, 0:1], red[:, 0:1], P, bass.bass_isa.ReduceOp.max).then_inc(w_allmax, 1)

            pool.wait_ge(m_gates, 1)
            for i in range(2):
                pool.memset(v_aug[i][:, :, :, :, DH:DH + 1], 1.0)
            pool.wait_ge(m_floor, 1)

            def v_means(n, v):
                p = v // PAIR
                loads = (n // UNROLL + 1) * 32 if isinstance(n, int) else v_count(v)
                pool.wait_ge(v_loaded[p], loads)
                apart(pool, loads)
                mean = gates[:, :, n, 2 * NH:GC] if isinstance(n, int) else gates[:, :, bass.ds(n, 1), 2 * NH:GC].rearrange("p s b h -> p s (b h)")
                pool.tensor_copy(v_aug[p][:, v % PAIR, :, :, DH + 1], mean).then_inc(v_ready, 1)

            def masks(n, v):
                s = v % 2
                loads = (n // 2 + 1) * 16 if isinstance(n, int) else max_count(v)
                pool.wait_ge(max_loaded[s], loads)
                apart(pool, loads)
                pool.affine_select(out=max_hi[s], in_=max_bc[s][:, :, P:SEQ], compare_op=ALU.is_ge, fill=NEVER, base=0,
                                   pattern=[[0, NH], [1, P]], channel_multiplier=-1)
                pool.affine_select(out=max_bc[s][:, :, 0:P], in_=max_bc[s][:, :, 0:P], compare_op=ALU.is_ge, fill=NEVER,
                                   base=0, pattern=[[0, NH], [1, P]], channel_multiplier=-1).then_inc(masked, 1)

            reg = [None]

            def v_count(v):
                return reg[0] * 32 if v == UNROLL - 1 else reg[0] * 32 + 32

            def max_count(v):
                return reg[0] * 32 + (v // 2 + 1) * 16

            def gain(n, v):
                s = v % 2
                pool.wait_ge(var_ready, n + 1)
                apart(pool, n + 1)
                pool.tensor_tensor(head_gain[:, s, :], head_var[:, s, :], minus_half[:, :], ALU.pow).then_inc(gain_ready, 1)

            def output_scale(n, v):
                s = v % 2
                pool.wait_ge(y_ready, n + 1)
                apart(pool, n + 1)
                h2 = head[s].rearrange("p (s c) -> p s c", s=HALVES)
                pool.tensor_tensor(h2, h2, scale_row[:, :].unsqueeze(1).broadcast_to([P, HALVES, HID]), ALU.mult).then_inc(ys_ready, 1)

            def residual(n, v):
                s = v % 2
                pool.wait_ge(ys_ready, n + 1)
                apart(pool, n + 1)
                pool.tensor_tensor(x_batch(n), x_batch(n), head[s], ALU.add).then_inc(x1_ready, 1)

            def rstd2(n, v):
                s = v % 2
                pool.wait_ge(rstd2_eps, n + 1)
                apart(pool, n + 1)
                pool.tensor_tensor(rstd[:, s, :, 0], rstd[:, s, :, 0], minus_half[:, 0:HALVES], ALU.pow).then_inc(rstd2_ready, 1)

            def step3(b, u):
                lagging(masks, 0, b, u)
                lagging(v_means, 1, b, u)
                lagging(gain, 3, b, u)
                lagging(rstd2, 4, b, u)
                lagging(output_scale, 3, b, u)
                lagging(residual, 3, b, u)

            for b in range(UNROLL):
                step3(b, b)
            with pool.Fori(1, BATCH // UNROLL) as it:
                reg[0] = it
                for u in range(UNROLL):
                    step3(it * UNROLL + u, u)
            step3(BATCH, 0)
            gain(BATCH - 2, 2)
            rstd2(BATCH - 3, 1)
            gain(BATCH - 1, 3)
            rstd2(BATCH - 2, 2)
            rstd2(BATCH - 1, 3)

            def over_partitions(i, local, everywhere):
                pool.wait_ge(local, 1)
                pool.partition_all_reduce(allmax[:, i:i + 1], red[:, i:i + 1], P, bass.bass_isa.ReduceOp.max).then_inc(everywhere, 1)

            over_partitions(1, red_x, all_x)
            over_partitions(2, red_g, all_g)

            def gated(c, j):
                pool.wait_ge(sigq_ready, c * FP + (j + 1))
                apart(pool, c * FP + (j + 1))
                pool.tensor_tensor(int_pair(c, j), int_pair(c, j), sigq[j], ALU.mult).then_inc(gs_ready, 1)

            with pool.Fori(0, CHUNKS - 1) as c:
                for j in range(FP):
                    gated(c, j)
            for j in range(FP - 1):
                gated(CHUNKS - 1, j)
            over_partitions(4, red_u, all_u)
            gated(CHUNKS - 1, FP - 1)
            over_partitions(3, red_gs, all_gs)

            def combine_rest(k, gate_slot, up_slot):
                for j in range(1, FP):
                    pool.wait_ge(gsq_rest, k * (FP - 1) + j)
                    apart(pool, k * (FP - 1) + j)
                    pool.wait_ge(uq_ready, k * FP + (j + 1))
                    apart(pool, k * FP + (j + 1))
                    pool.tensor_tensor(int_pair(up_slot, j), int_pair(gate_slot, j), int_pair(up_slot, j), ALU.mult).then_inc(o_rest, 1)

            combine_rest(0, 4, O_SLOTS[0])
            with pool.Fori(1, 4) as k:
                combine_rest(k, k + 4, k + 8)
            for k in range(4, CHUNKS):
                combine_rest(k, k - 4, O_SLOTS[k])

            over_partitions(5, red_o, all_o)

        @block.scalar
        def _(act):
            def context_high(n, v):
                if due((n - 1) * 2):
                    act.wait_ge(scores_ready, (n - 1) * 2)
                    apart(act, (n - 1) * 2)
                act.wait_ge(gc_scales, 1 if isinstance(n, int) else 2)
                act.activation(c_parts[v % 2][:, 0:KT * SEQ], ctx_of(n), ACT.Copy, scale=scale_of(0, n)).then_inc(c_hi, 1)

            def query_high(n, v):
                act.wait_ge(q_trans, n + 1)
                apart(act, n + 1)
                if due((n - 1) * 2):
                    act.wait_ge(scores_ready, (n - 1) * 2)
                    apart(act, (n - 1) * 2)
                act.activation(q_parts[v % 2][:, 0:KT * SEQ], bank[v % 2][:, :], ACT.Copy, scale=Q_UNIT).then_inc(q_hi, 1)

            def evac_gates(n, v):
                act.wait_ge(gates_done, n + 1)
                apart(act, n + 1)
                dst = gates_raw[:, :, n, :] if isinstance(n, int) else \
                    gates_raw[:, :, bass.ds(n, 1), :].rearrange("p s b g -> p s (b g)")
                act.activation(dst, bank[2][:, 0:HALVES * 2 * GW].rearrange("p (s g) -> p s g", s=HALVES), ACT.Copy).then_inc(gates_evac, 1)

            def evac_scores(n, v):
                for key_half in range(HALVES):
                    width = 2 * (SEQ - key_half * P)
                    act.wait_ge(scores_ready, n * 2 + (key_half + 1))
                    apart(act, n * 2 + (key_half + 1))
                    act.activation(scores_of(n, key_half * NH * SEQ, 2 * width).rearrange("p (i n) -> p i n", i=2),
                                   psum[:, 3 + 2 * key_half:5 + 2 * key_half, 0:width], ACT.Copy,
                                   scale=scale_of(2, n)).then_inc(scores_evac, 1)

            def step1(b, u):
                lagging(context_high, 1, b, u)
                lagging_from(1, query_high, 1, b, u)
                lagging(evac_gates, 2, b, u)
                lagging(evac_scores, 2, b, u)

            query_high(0, 0)
            over_batches(act, step1, 1)
            evac_gates(BATCH - 1, UNROLL - 1)

            def scale_weights(r):
                act.wait_ge(w_tr, r + 1)
                if due(r - 1):
                    act.wait_ge(w_parts, r - 1)
                act.activation(w_tmp[r % 2], bank[7 - 7 * (r % 2)][:, :], ACT.Copy, scale=col(WMUL)).then_inc(w_sc, 1)

            act.wait_ge(m_fz, 1)
            act.activation(fabs, fz, ACT.Abs).then_inc(m_softplus_step, 1)
            act.wait_ge(m_softplus_step, 1)
            act.activation(fexp, fabs, ACT.Exp, scale=-1.0).then_inc(m_softplus_step, 1)
            act.wait_ge(m_softplus_step, 2)
            act.activation(fln, fexp, ACT.Ln, bias=1.0).then_inc(m_ln, 1)
            evac_scores(BATCH - 1, UNROLL - 1)
            act.wait_ge(w_fac, 1)
            for r in range(2):
                scale_weights(r)
            act.wait_ge(m_add, 1)
            act.activation(floor_nat[:, :, :], eneg.rearrange("p s b h -> p s (b h)"), ACT.Exp, scale=-1.0).then_inc(m_floor, 1)
            for r in range(2, 9):
                scale_weights(r)

            def a_col(half, n, h):
                return a_nat[:, half, n * NH + h:n * NH + h + 1] if isinstance(n, int) else \
                    a_nat[:, half, bass.ds(n * NH + h, 1)]

            def decays_low(n, v):
                s = v % 2
                act.wait_ge(masked, n + 1)
                apart(act, n + 1)
                if due(n - 1):
                    act.wait_ge(pv_done, n - 1)
                    apart(act, n - 1)
                for h in range(NH):
                    last = act.activation(decay[s][:, place(h) * SEQ:(place(h) + 1) * SEQ], max_bc[s][:, h, :], ACT.Exp,
                                          bias=a_col(0, n, h), scale=-1.0)
                last.then_inc(exp_done, 1)

            def decays_high(n, v):
                s = v % 2
                for h in range(NH):
                    last = act.activation(decay[s][:, NH * SEQ + place(h) * P:NH * SEQ + (place(h) + 1) * P], max_hi[s][:, h, :], ACT.Exp,
                                          bias=a_col(1, n, h), scale=-1.0)
                last.then_inc(exp_done, 1)

            def squares(n, v):
                act.wait_ge(head_ready, n + 1)
                apart(act, n + 1)
                if due(n):
                    act.wait_ge(ssq_ready, n)
                    apart(act, n)
                act.activation(square, head[v % 2], ACT.Square).then_inc(sq_ready, 1)

            def norm2(n, v):
                s = v % 2
                act.wait_ge(shift_ready, n + 1)
                apart(act, n + 1)
                if due(n - 1):
                    act.wait_ge(xnt_psum, n - 1)
                    apart(act, n - 1)
                for half in range(HALVES):
                    last = act.activation(xn[s][:, half * HID:(half + 1) * HID], x_of(n, half), ACT.Identity,
                                          bias=shift[:, s, half:half + 1], scale=rstd[:, s, half, 0:1])
                last.then_inc(xn_ready, 1)

            def evac_xnt(n, v):
                act.wait_ge(xnt_psum, n + 1)
                apart(act, n + 1)
                act.activation(scores_of(n, 0, 512), bank[4 + v % 2][:, :], ACT.Copy).then_inc(xnt_ready, 1)

            def step3(b, u):
                lagging(decays_low, 0, b, u)
                lagging(norm2, 4, b, u)
                lagging(squares, 2, b, u)
                lagging(decays_high, 0, b, u)
                lagging(evac_xnt, 5, b, u)

            over_batches(act, step3, 0, 2)
            norm2(BATCH - 4, 0)
            squares(BATCH - 2, 2)
            evac_xnt(BATCH - 5, 3)
            squares(BATCH - 1, 3)
            for n in range(BATCH - 3, BATCH):
                norm2(n, n % UNROLL)
                evac_xnt(n - 1, (n - 1) % UNROLL)
            evac_xnt(BATCH - 1, 3)

            def quant_x(c):
                o = c * (PAIR * SCORES)
                v = at(o, PAIR * SCORES) if isinstance(c, int) else at_dyn(o, PAIR * SCORES)
                if due(c):
                    act.wait_ge(xq_ready, c)
                    apart(act, c)
                act.activation(x_int[0].rearrange("p (k b t) -> p b k t", k=KT, b=PAIR),
                               v.rearrange("p (b n) -> p b n", b=PAIR)[:, :, 0:512].rearrange("p b (k t) -> p b k t", k=KT),
                               ACT.Copy, scale=col(INV_X)).then_inc(xi_ready, 1)

            def evac_proj(psum_sem, evac_sem, c, slot):
                for j in range(FP):
                    act.wait_ge(psum_sem, c * FP + (j + 1))
                    apart(act, c * FP + (j + 1))
                    act.activation(slot_pair(slot, j), bank_pair[j], ACT.Copy).then_inc(evac_sem, 1)

            act.wait_ge(inv_x, 1)
            quant_x(0)
            with act.Fori(1, CHUNKS) as c:
                quant_x(c)
                evac_proj(g_psum, g_evac, c - 1, c - 1)
            evac_proj(g_psum, g_evac, CHUNKS - 1, CHUNKS - 1)

            def evac_up(c, j, slot):
                act.wait_ge(u_psum, c * FP + (j + 1))
                apart(act, c * FP + (j + 1))
                act.activation(slot_pair(slot, j), bank_pair[j], ACT.Copy).then_inc(u_evac, 1)

            def quant_up(slot, j):
                act.activation(int_pair(slot, j), slot_pair(slot, j), ACT.Copy, scale=col(INV_U)).then_inc(uq_ready, 1)

            def gate_chain(c, between):
                for j in range(FP):
                    act.activation(int_pair(c, j), slot_pair(c, j), ACT.Copy, scale=col(INV_G)).then_inc(gq_ready, 1)
                    between(j)
                    act.wait_ge(gq_ready, c * FP + (j + 1))
                    apart(act, c * FP + (j + 1))
                    if due((c - 1) * FP + (j + 1)):
                        act.wait_ge(gs_ready, (c - 1) * FP + (j + 1))
                        apart(act, (c - 1) * FP + (j + 1))
                    act.activation(sig[j], int_pair(c, j), ACT.Sigmoid, scale=col(SG)).then_inc(sig_ready, 1)

            act.wait_ge(inv_g, 1)
            gate_chain(0, lambda j: evac_up(0, j, 8))
            with act.Fori(1, 4) as c:
                gate_chain(c, lambda j: evac_up(c, j, c + 8))
            for c in range(4, CHUNKS):
                act.wait_ge(up_spilled[c - 4], 16)
                gate_chain(c, lambda j: evac_up(c, j, c + 4))

            def quant(k, gate_slot, up_slot):
                for j in range(FP):
                    g = int_pair(gate_slot, j)
                    if j > 0:
                        act.activation(g, g, ACT.Copy, scale=col(INV_GS)).then_inc(gsq_rest, 1)
                    elif isinstance(k, int) and k >= ACT_GATES:
                        act.activation(g, g, ACT.Copy, scale=col(INV_GS)).then_inc(gsq_first_act, 1)
                    if up_slot is not None:
                        quant_up(up_slot, j)

            act.wait_ge(inv_u, 1)
            for j in range(FP):
                quant_up(O_SLOTS[0], j)
            act.wait_ge(inv_gs, 1)
            quant(0, 4, None)
            with act.Fori(1, 4) as k:
                quant(k, k + 4, k + 8)
            for k in range(4, CHUNKS):
                act.wait_ge(up_back[k - 4], 16)
                quant(k, k - 4, O_SLOTS[k])

            act.wait_ge(inv_o, 1)
            for k in range(CHUNKS):
                for j in range(2):
                    if k == 0 and j == 1:
                        continue
                    if due(2 * k + j - 1):
                        act.wait_ge(op_ready, 2 * k + j - 1)
                        apart(act, 2 * k + j - 1)
                    act.activation(o_int[j], at(O_SLOTS[k] * SLOT + j * SLOT // 2, SLOT // 2).bitcast(I32), ACT.Copy,
                                   scale=col(INV_O)).then_inc(oi_ready, 1)

        @block.tensor
        def _(pe):
            pe.wait_ge(consts_set, 1)

            def transposes(n, v):
                s = v % 2
                pe.wait_ge(q_ready, n + 1)
                for k in range(KT):
                    for half in range(HALVES):
                        last = pe.transpose(bank[s][:, k * SEQ + half * P:k * SEQ + (half + 1) * P],
                                            q_nat[s][:, half * HID + k * P:half * HID + (k + 1) * P], ident[:, :])
                last.then_inc(q_trans, 1)

            def gates_and_scores(n, v):
                s = v % 2
                ct, qt = (t[s].rearrange("p (i k t) -> p i k t", i=2, k=KT) for t in (c_parts, q_parts))
                if due(n):
                    pe.wait_ge(gates_evac, n)
                pe.wait_ge(qt_ready, n + 1)
                pe.wait_ge(c_lo, n + 1)
                for half in range(HALVES):
                    t = slice(half * P, (half + 1) * P)
                    for i, parts in enumerate((ct, qt)):
                        o = bank[2][:, (half * 2 + i) * GW:(half * 2 + i + 1) * GW]
                        for k in range(KT):
                            pe.matmul(o, parts[:, 0, k, t], gate_w_parts[:, i * KT + k, :], start=(k == 0), stop=False)
                        for k in range(KT):
                            last = pe.matmul(o[:, 0:GC], parts[:, 1, k, t], gate_w_parts[:, i * KT + k, 0:GC],
                                             start=False, stop=(k == KT - 1))
                last.then_inc(gates_done, 1)
                for key_half in range(HALVES):
                    if due((n - 1) * 2 + (key_half + 1)):
                        pe.wait_ge(scores_evac, (n - 1) * 2 + (key_half + 1))
                    width = SEQ - key_half * P
                    for hp in range(NH // 2):
                        for i, (cp, qp) in enumerate(((0, 0), (0, 1), (1, 0))):
                            for odd in range(2):
                                r = DH * odd
                                last = pe.matmul(bank[3 + 2 * key_half + odd][:, hp * width:(hp + 1) * width],
                                                 ct[r:r + DH, cp, hp, key_half * P:(key_half + 1) * P],
                                                 qt[r:r + DH, qp, hp, key_half * P:SEQ], start=(i == 0), stop=(i == 2))
                    last.then_inc(scores_ready, 1)

            def step1(b, u):
                lagging_from(2, transposes, 1, b, u)
                lagging(gates_and_scores, 2, b, u)

            transposes(0, 0)
            transposes(1, 1)
            pe.wait_ge(gw_ready, 1)
            over_batches(pe, step1, 2)

            def transpose_weights(r):
                if due(r - 1):
                    pe.wait_ge(w_sc, r - 1)
                for i in range(2):
                    for j in range(2):
                        if r < 6:
                            src = w_nat[:, ((r // 3) * 6 + 2 * (r % 3) + j) * HID + i * P:][:, 0:P]
                        else:
                            src = w_nat[:, 12 * HID + j * FF + (2 * (r - 6) + i) * P:][:, 0:P]
                        last = pe.transpose(bank[7 - 7 * (r % 2)][:, (2 * i + j) * P:(2 * i + j + 1) * P], src, ident[:, :])
                last.then_inc(w_tr, 1)

            pe.wait_ge(w_dq, W_PARTS)
            for r in range(2):
                transpose_weights(r)

            pe.wait_ge(m_lf, 1)
            lfv = lf.rearrange("p s b h -> p s (b h)")
            C = BATCH * NH
            pe.matmul(bank[1][:, 0:C], tri[:, :], lfv[:, 0, :], start=True, stop=True)
            pe.matmul(bank[1][:, C:2 * C], tri[:, :], lfv[:, 1, :], start=True, stop=False)
            pe.matmul(bank[1][:, C:2 * C], ones[:, :], lfv[:, 0, :], start=False, stop=True).then_inc(m_cs, 1)
            pe.wait_ge(m_a, 1)
            for half in range(HALVES):
                last = pe.transpose(bank[2][0:C, half * P:(half + 1) * P], a_nat[:, half, :], ident[:, :])
            last.then_inc(m_at, 1)
            pe.wait_ge(m_scan, 1)
            for half in range(HALVES):
                last = pe.transpose(bank[1][:, half * C:(half + 1) * C], run_max[:, half * P:(half + 1) * P], ident[0:C, 0:C])
            last.then_inc(m_mt, 1)
            for r in range(2, 9):
                transpose_weights(r)

            def weighted_sum(n, v, half):
                s = v % 2
                if half == 0:
                    pe.wait_ge(v_ready, n + 1)
                    if due(n - 1):
                        pe.wait_ge(head_ready, n - 1)
                pe.wait_ge(c_ready, 2 * n + (half + 1))
                for h in range(NH):
                    o = bank[2 * s + half][:, h * VC:(h + 1) * VC]
                    last = pe.matmul(o, decay[s][:, place(h) * SEQ + half * P:place(h) * SEQ + (half + 1) * P],
                                     v_aug[v // PAIR][:, v % PAIR, 0, h, :], start=True, stop=(half == 0))
                    if half == 1:
                        last = pe.matmul(o, decay[s][:, NH * SEQ + place(h) * P:NH * SEQ + (place(h) + 1) * P],
                                         v_aug[v // PAIR][:, v % PAIR, 1, h, :], start=False, stop=True)
                if half == HALVES - 1:
                    last.then_inc(pv_done, 1)

            def xn_transposes(n, v):
                s = v % 2
                pe.wait_ge(xn_ready, n + 1)
                if due(n - 1):
                    pe.wait_ge(xnt_ready, n - 1)
                for k in range(KT):
                    for half in range(HALVES):
                        last = pe.transpose(bank[4 + s][:, k * SEQ + half * P:k * SEQ + (half + 1) * P],
                                            xn[s][:, half * HID + k * P:half * HID + (k + 1) * P], ident[:, :])
                last.then_inc(xnt_psum, 1)

            def step3(b, u):
                lagging(lambda n, v: weighted_sum(n, v, 0), 0, b, u)
                lagging(lambda n, v: weighted_sum(n, v, 1), 0, b, u)
                lagging(xn_transposes, 3, b, u)

            over_batches(pe, step3, 3)

            def project(parts, sem_name, evac_name):
                def f(c):
                    for j in range(FP):
                        if due((c - 1) * FP + (j + 1)):
                            pe.wait_ge(evac_name, (c - 1) * FP + (j + 1))
                        for i in range(2):
                            ft = 2 * j + i
                            for n, (wp, xp) in enumerate(((0, 0), (0, 1), (1, 0))):
                                for k in range(KT):
                                    last = pe.matmul(bank[ft][:, :], parts[:, wp, k, ft * P:(ft + 1) * P], chunk_xq(c, xp, k),
                                                     start=(n == 0 and k == 0), stop=(n == 2 and k == KT - 1))
                        last.then_inc(sem_name, 1)
                return f

            gate_of = project(wg_parts, g_psum, g_evac)
            up_of = project(wu_parts, u_psum, u_evac)
            pe.wait_ge(w_parts, 9)
            pe.wait_ge(xnt_ready, BATCH)
            pe.wait_ge(xq_ready, 1)
            gate_of(0)
            with pe.Fori(1, CHUNKS) as c:
                pe.wait_ge(xq_ready, c + 1)
                gate_of(c)
            pe.wait_ge(g_evac, CHUNKS * FP)
            up_of(0)
            with pe.Fori(1, CHUNKS) as c:
                up_of(c)

            def down(n, v, first_k=0, last_k=FT):
                for t in range(4):
                    if first_k == 0 and due(4 * n + (t - 3)):
                        pe.wait_ge(yo_ready, 4 * n + (t - 3))
                    for q, (op, wp) in enumerate(((0, 0), (0, 1), (1, 0))):
                        for k in range(first_k, last_k):
                            o = (op * FT + k) * CH + t * P
                            last = pe.matmul(bank[t][:, 0:HID], o_parts[v][:, o:o + P], wd_parts[:, wp, k, :],
                                             start=(q == 0 and k == 0), stop=(q == 2 and k == FT - 1))
                    if last_k == FT:
                        last.then_inc(y_psum, 1)

            pe.wait_ge(u_evac, CHUNKS * FP)
            pe.wait_ge(op_ready, 1)
            down(0, 0, 0, FT // 2)
            pe.wait_ge(op_ready, 2)
            down(0, 0, FT // 2, FT)
            pe.wait_ge(op_ready, 4)
            down(1, 1)
            with pe.Fori(1, CHUNKS // 2) as g:
                for v in range(2):
                    pe.wait_ge(op_ready, (g * 2 + v) * 2 + 2)
                    down(g * 2 + v, v)

        @block.vector
        def _(dve):
            dve.wait_ge(consts_loaded, 48)
            dve.tensor_reduce(red[:, 6:7], gate_w_raw[:, :, :], AX.XY, ALU.max, apply_absolute_value=True).then_inc(gw_max, 1)
            dve.tensor_copy(gate_w_sum[:, KT:2 * KT, :], gate_w_raw[:, 0:KT, :])
            dve.tensor_tensor(gate_w_sum[:, 0:KT, :], gate_w_raw[:, KT:2 * KT, :], gate_w_raw[:, 2 * KT:3 * KT, :],
                              ALU.add).then_inc(gw_sum, 1)
            dve.memset(gate_w_parts[:, :, :], 0.0).then_inc(gw_zero, 1)
            dve.wait_ge(gw_zero, 1)
            for h in range(NH):
                dve.memset(gate_w_parts[(h % 2) * DH:(h % 2 + 1) * DH, h // 2, 2 * NH + h:2 * NH + h + 1], 1.0 / DH)

            reg = [None]

            def stats(n, v):
                s, p = v % 2, v // PAIR
                dve.wait_ge(x_loaded[p], 16 * (n // UNROLL + 1) if isinstance(n, int) else reg[0] * 16 + 16)
                for half in range(HALVES):
                    last = dve.bn_stats(bn_raw[:, s, half, :], x_of(n, half))
                last.then_inc(stats_raw, 1)

            def stats_join(n, v):
                s = v % 2
                dve.wait_ge(stats_raw, n + 1)
                apart(dve, n + 1)
                for half in range(HALVES):
                    last = dve.bn_aggr(mean_var[:, s, half, :], bn_raw[:, s, half, :])
                last.then_inc(stats_done, 1)

            def norm_q(n, v):
                s = v % 2
                dve.wait_ge(rstd_ready, n + 1)
                for half in range(HALVES):
                    last = dve.tensor_scalar(q_nat[s][:, half * HID:(half + 1) * HID], x_of(n, half),
                                             mean_var[:, s, half, 0:1], rstd[:, s, half, 0:1], ALU.subtract, ALU.mult)
                last.then_inc(q_ready, 1)

            def query_low(n, v):
                s = v % 2
                dve.wait_ge(q_hi, n + 1)
                dve.scalar_tensor_tensor(q_parts[s][:, KT * SEQ:], bank[s][:, :], Q_UNIT, q_parts[s][:, 0:KT * SEQ],
                                         ALU.mult, ALU.subtract).then_inc(qt_ready, 1)

            def context_low(n, v):
                s = v % 2
                dve.wait_ge(c_hi, n + 1)
                dve.scalar_tensor_tensor(c_parts[s][:, KT * SEQ:], ctx_of(n), scale_of(0, n), c_parts[s][:, 0:KT * SEQ],
                                         ALU.mult, ALU.subtract).then_inc(c_lo, 1)

            for n in range(2):
                stats(n, n)
                stats_join(n, n)
            norm_q(0, 0)

            def context_max(i):
                n = UNROLL * KT * SEQ
                dve.wait_ge(ctx_loaded[i], 16)
                dve.tensor_reduce(red[:, 7:8] if i == 0 else xmax[:, i:i + 1], at(A_CTX + i * n, n), AX.X, ALU.max,
                                  apply_absolute_value=True).then_inc(gc_rowmax if i == 0 else c_max, 1)

            def power_of_two(src, dst, inverse, step):
                dve.tensor_scalar(dst.bitcast(U32), src.bitcast(U32), 0x7F800000, None, ALU.bitwise_and).then_inc(gate_scale_step, 1)
                dve.wait_ge(gate_scale_step, step + 1)
                dve.tensor_scalar(dst, dst, 2.0 ** -60, None, ALU.max).then_inc(gate_scale_step, 1)
                dve.wait_ge(gate_scale_step, step + 2)
                dve.reciprocal(inverse, dst).then_inc(gate_scale_step, 1)
                dve.wait_ge(gate_scale_step, step + 3)

            def context_scales(first, last):
                row = lambda i: ctx_scale[:, i, first:last]
                spread = lambda i: col(i).broadcast_to([P, last - first])
                dve.tensor_scalar(row(0), spread(MUL_C), W_UNIT, None, ALU.mult)
                dve.tensor_scalar(row(1), spread(P2_C), 1.0 / W_UNIT, None, ALU.mult)
                dve.tensor_scalar(row(2), spread(P2_C), DH ** -0.5 / (Q_UNIT * W_UNIT), None, ALU.mult).then_inc(gc_scales, 1)

            context_max(0)
            dve.wait_ge(gc_allmax, 1)
            power_of_two(allmax[:, 6:8], sc[:, P2_G:P2_C + 1], sc[:, MUL_G:MUL_C + 1], 0)
            context_scales(0, UNROLL)
            norm_q(1, 1)
            dve.tensor_scalar(col(MUL_G), col(MUL_G), W_UNIT, None, ALU.mult).then_inc(gate_scale_step, 1)
            dve.tensor_scalar(col(FAC_G), col(P2_G), 1.0 / W_UNIT, None, ALU.mult).then_inc(gate_scale_step, 1)
            dve.wait_ge(gate_scale_step, 5)
            dve.tensor_scalar(col(FAC_QG), col(FAC_G), 1.0 / Q_UNIT, None, ALU.mult).then_inc(gate_scale_step, 1)
            dve.wait_ge(gw_sum, 1)
            dve.tensor_scalar(gate_w_sum, gate_w_sum, col(MUL_G), None, ALU.mult).then_inc(gate_scale_step, 1)
            dve.wait_ge(gate_scale_step, 7)
            dve.tensor_copy(gate_w_parts[:, :, 0:2 * NH], gate_w_sum).then_inc(gate_scale_step, 1)
            dve.wait_ge(gate_scale_step, 8)
            dve.tensor_tensor(gate_w_parts[:, :, GC:GC + 2 * NH], gate_w_sum, gate_w_parts[:, :, 0:2 * NH],
                              ALU.subtract).then_inc(gw_ready, 1)

            def step1(b, u):
                lagging_from(2, stats, 0, b, u)
                lagging_from(2, stats_join, 0, b, u)
                lagging(context_low, 1, b, u)
                lagging(query_low, 1, b, u)
                lagging_from(2, norm_q, 0, b, u)

            def part_of(t, off, size):
                return at_dyn(off + t * size, size)

            def blocks(t):
                return t.rearrange("p (b k) -> p b k", k=BLOCK)

            def of_blocks(t):
                return t.unsqueeze(2).broadcast_to([P, W_PART // BLOCK, BLOCK])

            def block_scales(t):
                bm = part_of(t, A_TMP + 5568, W_PART // BLOCK)
                dve.wait_ge(w_step, t * 4 + 1)
                dve.tensor_scalar(block_s, bm, 1.0 / QMAX4, TINY, ALU.mult, ALU.max).then_inc(w_step, 1)

            def step_with_weights(b, u):
                t = b - W_LAG
                w = part_of(t, A_W, W_PART)
                dve.tensor_reduce(part_of(t, A_TMP + 5568, W_PART // BLOCK), blocks(w), AX.X, ALU.max,
                                  apply_absolute_value=True).then_inc(w_step, 1)
                lagging(stats, 0, b, u)
                block_scales(t)
                lagging(stats_join, 0, b, u)
                dve.wait_ge(w_step, t * 4 + 2)
                dve.reciprocal(block_inv, block_s).then_inc(w_step, 1)
                lagging(context_low, 1, b, u)
                dve.wait_ge(w_step, t * 4 + 3)
                dve.tensor_tensor(blocks(w), blocks(w), of_blocks(block_inv), ALU.mult).then_inc(w_step, 1)
                lagging(query_low, 1, b, u)
                dve.wait_ge(w_step, t * 4 + 4)
                apart(dve, t * 4 + 4)
                dve.tensor_copy(w_int, w).then_inc(w_rounded, 1)
                lagging(norm_q, 0, b, u)
                dve.wait_ge(w_rounded, t + 1)
                dve.tensor_tensor(blocks(w), blocks(w_int), of_blocks(block_s), ALU.mult).then_inc(w_dq, 1)

            for b in range(UNROLL - 1):
                step1(b, b)
            context_max(1)
            step1(UNROLL - 1, UNROLL - 1)
            for i in range(2, BATCH // UNROLL):
                context_max(i)
            dve.wait_ge(c_max, BATCH // UNROLL - 1)
            dve.tensor_reduce(red[:, 5:6], xmax[:, 1:BATCH // UNROLL], AX.X, ALU.max).then_inc(gc_rowmax, 1)
            dve.wait_ge(gc_allmax, 2)
            power_of_two(allmax[:, 5:6], col(P2_C), col(MUL_C), 8)
            context_scales(UNROLL, BATCH)
            for b in range(UNROLL, W_LAG):
                step1(b, b % UNROLL)
            dve.wait_ge(w_loaded, 48)
            for b in range(W_LAG, 2 * UNROLL):
                step_with_weights(b, b % UNROLL)
            with dve.Fori(2, BATCH // UNROLL) as it:
                reg[0] = it
                for u in range(UNROLL):
                    step_with_weights(it * UNROLL + u, u)
            step_with_weights(BATCH, 0)
            dve.wait_ge(w_dq, W_PARTS)
            dve.tensor_reduce(red[:, 0:1], block_max, AX.X, ALU.max).then_inc(w_rowmax, 1)
            def split_weights(r):
                dve.wait_ge(w_sc, r + 1)
                t4 = w_tmp[r % 2].rearrange("p (i n) -> p i n", i=2)
                if r < 6:
                    w = (wg_parts, wu_parts)[r // 3]
                    hi, lo = (w[:, i, :, 2 * (r % 3) * P:(2 * (r % 3) + 2) * P] for i in range(2))
                else:
                    hi, lo = (wd_parts[:, i, 2 * (r - 6):2 * (r - 6) + 2, :] for i in range(2))
                dve.tensor_copy(hi, t4).then_inc(w_hi, 1)
                dve.wait_ge(w_hi, r + 1)
                dve.tensor_tensor(lo, t4, hi, ALU.subtract).then_inc(w_parts, 1)

            dve.wait_ge(gates_evac, BATCH)
            raw = gates_raw.rearrange("p s b (i j g) -> p (s b) i j g", i=2, j=2)
            dve.tensor_tensor(gate_sum[:, :, :, :], raw[:, :, :, 0, :], raw[:, :, :, 1, :], ALU.add).then_inc(m_gates_step, 1)
            dve.wait_ge(m_gates_step, 1)
            gates_flat = gates[:, :, :, :].rearrange("p s b g -> p (s b) g")
            dve.tensor_scalar(gate_sum[:, :, 1, 0:2 * NH], gate_sum[:, :, 1, 0:2 * NH], col(FAC_QG), None, ALU.mult).then_inc(m_gates_step, 1)
            for half in range(HALVES):
                gs = gate_sum[:, half * BATCH:(half + 1) * BATCH, 0, :]
                dve.tensor_tensor(gs, gs, ctx_scale[:, 1, :].unsqueeze(2).broadcast_to([P, BATCH, GC]), ALU.mult).then_inc(m_gates_step, 1)
            dve.wait_ge(m_gates_step, 4)
            dve.tensor_copy(gates_flat[:, :, 2 * NH:GC], gate_sum[:, :, 0, 2 * NH:GC])
            dve.scalar_tensor_tensor(gates_flat[:, :, 0:2 * NH], gate_sum[:, :, 0, 0:2 * NH], col(FAC_G),
                                     gate_sum[:, :, 1, 0:2 * NH], ALU.mult, ALU.add).then_inc(m_gates, 1)
            dve.wait_ge(m_gates, 1)
            bias_bc = lambda i: gate_bias[:, i * NH:(i + 1) * NH].unsqueeze(1).unsqueeze(1).broadcast_to([P, HALVES, BATCH, NH])
            dve.tensor_tensor(fz, gates[:, :, :, NH:2 * NH], bias_bc(1), ALU.add).then_inc(m_fz, 1)
            dve.wait_ge(m_fz, 1)
            dve.tensor_tensor(csum, gates[:, :, :, 0:NH], bias_bc(0), ALU.add).then_inc(m_ib, 1)
            dve.wait_ge(w_allmax, 1)
            dve.tensor_scalar(sc[:, WP2:WP2 + 1].bitcast(U32), allmax[:, 0:1].bitcast(U32), 0x7F800000, None, ALU.bitwise_and).then_inc(w_scale_step, 1)
            dve.wait_ge(w_scale_step, 1)
            dve.tensor_scalar(col(WP2), col(WP2), 2.0 ** -100, None, ALU.max).then_inc(w_scale_step, 1)
            dve.wait_ge(w_scale_step, 2)
            dve.reciprocal(col(CO), col(WP2)).then_inc(w_scale_step, 1)
            dve.wait_ge(w_scale_step, 3)
            dve.tensor_scalar(col(WMUL), col(CO), W_UNIT, None, ALU.mult)
            dve.tensor_scalar(col(WFAC), col(WP2), 1.0 / W_UNIT, None, ALU.mult).then_inc(w_fac, 1)
            dve.wait_ge(m_ln, 1)
            flat = lambda t: t.rearrange("p s b h -> p (s b h)")
            dve.scalar_tensor_tensor(flat(lf), flat(fz), 0.0, flat(fln), ALU.min, ALU.subtract).then_inc(m_lf, 1)
            dve.wait_ge(m_cs, 1)
            dve.wait_ge(m_ib, 1)
            dve.tensor_copy(flat(eneg), bank[1][:, 0:P]).then_inc(m_scan_scaled, 1)
            dve.wait_ge(m_scan_scaled, 1)
            dve.tensor_tensor(a_nat[:, :, :].rearrange("p s c -> p (s c)"), flat(csum), flat(eneg), ALU.subtract).then_inc(m_a, 1)
            dve.wait_ge(m_at, 1)
            dve.tensor_copy(a_row, bank[2][0:BATCH * NH, 0:SEQ]).then_inc(m_scan_scaled, 1)
            dve.wait_ge(m_scan_scaled, 2)
            dve.tensor_tensor_scan(run_max[:, :], a_row, a_row, -3.0e38, ALU.max, ALU.max).then_inc(m_scan, 1)
            split_weights(0)
            dve.wait_ge(m_mt, 1)
            dve.tensor_tensor(flat(eneg), flat(eneg), bank[1][:, 0:P], ALU.add).then_inc(m_add, 1)
            for r in range(1, 9):
                split_weights(r)

            def head_sums(n, v):
                s = v % 2
                dve.wait_ge(pv_done, n + 1)
                o = psum[:, 2 * s:2 * s + HALVES, 0:NH * VC].rearrange("p s (h c) -> p s h c", h=NH)
                dve.tensor_copy(o_cols[:, s, :, :].rearrange("p (s h) c -> p s h c", s=HALVES),
                                o[:, :, :, DH:VC]).then_inc(cols_ready, 1)

            def head_center(n, v):
                s = v % 2
                o = psum[:, 2 * s:2 * s + HALVES, 0:NH * VC].rearrange("p s (h c) -> p s h c", h=NH)
                cols = o_cols[:, s, :, :].rearrange("p (s h) c -> p s h c", s=HALVES)
                if due(n - 1):
                    dve.wait_ge(x1_ready, n - 1)
                dve.wait_ge(cols_ready, n + 1)
                dve.tensor_tensor(head[s].rearrange("p (s h c) -> p s h c", s=HALVES, h=NH), o[:, :, :, 0:DH],
                                  cols[:, :, :, 1:2].broadcast_to([P, HALVES, NH, DH]), ALU.subtract).then_inc(head_ready, 1)

            def normaliser_half(n, v):
                s = v % 2
                fl = floor_nat[:, :, n * NH:(n + 1) * NH] if isinstance(n, int) else floor_nat[:, :, bass.ds(n * NH, NH)]
                dve.wait_ge(cols_ready, n + 1)
                dve.scalar_tensor_tensor(floor_n[:, s, :].rearrange("p (s h) -> p s h", s=HALVES),
                                         o_cols[:, s, :, 0].rearrange("p (s h) -> p s h", s=HALVES), -1.0, fl,
                                         ALU.mult, ALU.max).then_inc(n_half, 1)

            def normaliser(n, v):
                s = v % 2
                dve.wait_ge(n_half, n + 1)
                dve.tensor_tensor(floor_n[:, s, :], floor_n[:, s, :], o_cols[:, s, :, 0], ALU.max).then_inc(n_ready, 1)

            def normaliser_eps(n, v):
                s = v % 2
                dve.wait_ge(n_ready, n + 1)
                dve.tensor_scalar(floor_w[:, s, :], floor_n[:, s, :], NORM_EPS, LN_EPS ** 0.5, ALU.add, ALU.mult).then_inc(w_ready, 1)

            def products(n, v, half):
                off, size = ((0, NH * SEQ), (NH * SEQ, NH * P))[half]
                part = decay[v % 2][:, off:off + size]
                dve.wait_ge(exp_done, 2 * n + (half + 1))
                dve.tensor_tensor(part, part, scores_of(n, off, size), ALU.mult).then_inc(c_ready, 1)

            def head_squares(n, v):
                s = v % 2
                dve.wait_ge(sq_ready, n + 1)
                dve.tensor_reduce(sumsq[:, s, :], square.rearrange("p (g c) -> p g c", c=DH), AX.X, ALU.add).then_inc(ssq_ready, 1)

            def head_variance(n, v):
                s = v % 2
                dve.wait_ge(w_ready, n + 1)
                dve.tensor_tensor(floor_w2[:, s, :], floor_w[:, s, :], floor_w[:, s, :], ALU.mult).then_inc(w2_ready, 1)
                dve.wait_ge(ssq_ready, n + 1)
                dve.wait_ge(w2_ready, n + 1)
                dve.scalar_tensor_tensor(head_var[:, s, :], sumsq[:, s, :], 1.0 / DH, floor_w2[:, s, :],
                                         ALU.mult, ALU.add).then_inc(var_ready, 1)

            def head_scale(n, v):
                s = v % 2
                dve.wait_ge(gain_ready, n + 1)
                h3 = head[s].rearrange("p (g c) -> p g c", c=DH)
                dve.tensor_tensor(h3, h3, head_gain[:, s, :].unsqueeze(2).broadcast_to([P, HALVES * NH, DH]),
                                  ALU.mult).then_inc(y_ready, 1)

            def stats2_raw(n, v):
                s = v % 2
                if not isinstance(n, int) or n < BATCH - 2:
                    dve.wait_ge(x1_ready, n + 1)
                for half in range(HALVES):
                    last = dve.bn_stats(bn_raw[:, s, half, :], x_of(n, half))
                last.then_inc(bn2_raw, 1)

            def stats2(n, v):
                s = v % 2
                dve.wait_ge(bn2_raw, n + 1)
                apart(dve, n + 1)
                for half in range(HALVES):
                    last = dve.bn_aggr(mean_var[:, s, half, :], bn_raw[:, s, half, :])
                last.then_inc(bn2_done, 1)

            def stats2_eps(n, v):
                s = v % 2
                dve.wait_ge(bn2_done, n + 1)
                dve.tensor_scalar(rstd[:, s, :, :], mean_var[:, s, :, 1:2], LN_EPS, None, ALU.add).then_inc(rstd2_eps, 1)

            def shift2(n, v):
                s = v % 2
                dve.wait_ge(rstd2_ready, n + 1)
                dve.scalar_tensor_tensor(shift[:, s, :], mean_var[:, s, :, 0], -1.0, rstd[:, s, :, 0],
                                         ALU.mult, ALU.mult).then_inc(shift_ready, 1)

            def max_xn(n, v):
                dve.wait_ge(xnt_ready, n + 1)
                dst = xmax[:, n:n + 1] if isinstance(n, int) else xmax[:, bass.ds(n, 1)]
                dve.tensor_reduce(dst, scores_of(n, 0, 512), AX.X, ALU.max, apply_absolute_value=True).then_inc(xmax_ready, 1)

            def step3(b, u):
                lagging(head_sums, 2, b, u)
                lagging(shift2, 4, b, u)
                lagging(normaliser_half, 2, b, u)
                lagging(head_center, 2, b, u)
                lagging(normaliser, 2, b, u)
                lagging(lambda n, v: products(n, v, 0), 0, b, u)
                lagging(normaliser_eps, 2, b, u)
                lagging(head_squares, 2, b, u)
                lagging(head_variance, 2, b, u)
                lagging(stats2_raw, 3, b, u)
                lagging(lambda n, v: products(n, v, 1), 0, b, u)
                lagging(stats2, 3, b, u)
                lagging(stats2_eps, 3, b, u)
                lagging(head_scale, 2, b, u)
                lagging(max_xn, 5, b, u)

            over_batches(dve, step3, 0, 2)

            def center_all(n, v, between=None):
                head_sums(n, v)
                if between:
                    between()
                normaliser_half(n, v)
                head_center(n, v)
                normaliser(n, v)
                normaliser_eps(n, v)

            def stats2_all(n, v):
                stats2_raw(n, v)
                stats2(n, v)
                dve.wait_ge(xn_ready, n - 1)
                stats2_eps(n, v)

            def scale_and_residual(n, v, count):
                h2 = head[v % 2].rearrange("p (s c) -> p s c", s=HALVES)
                head_scale(n, v)
                dve.wait_ge(y_ready, n + 1)
                dve.tensor_tensor(h2, h2, scale_row[:, :].unsqueeze(1).broadcast_to([P, HALVES, HID]), ALU.mult).then_inc(last_scaled, 1)
                dve.wait_ge(last_scaled, count)
                dve.tensor_tensor(x_batch(n), x_batch(n), head[v % 2], ALU.add).then_inc(last_x1, 1)

            center_all(BATCH - 2, 2, lambda: shift2(BATCH - 4, 0))
            head_squares(BATCH - 2, 2)
            head_variance(BATCH - 2, 2)
            stats2_all(BATCH - 3, 1)
            center_all(BATCH - 1, 3)
            head_squares(BATCH - 1, 3)
            head_variance(BATCH - 1, 3)
            scale_and_residual(BATCH - 2, 2, 1)
            shift2(BATCH - 3, 1)
            dve.wait_ge(last_x1, 1)
            stats2_all(BATCH - 2, 2)
            scale_and_residual(BATCH - 1, 3, 2)
            max_xn(BATCH - 5, 3)
            shift2(BATCH - 2, 2)
            dve.wait_ge(last_x1, 2)
            stats2_all(BATCH - 1, 3)
            max_xn(BATCH - 4, 0)
            shift2(BATCH - 1, 3)
            for n in range(BATCH - 3, BATCH):
                max_xn(n, n % UNROLL)

            def partition_max(i, src, name):
                dve.tensor_reduce(red[:, i:i + 1], src, AX.X, ALU.max).then_inc(name, 1)

            dve.wait_ge(xmax_ready, BATCH)
            partition_max(1, xmax[:, :], red_x)
            dve.wait_ge(all_x, 1)
            dve.tensor_scalar(col(SX), allmax[:, 1:2], 1.0 / QMAX16, TINY, ALU.mult, ALU.max).then_inc(x_scale_step, 1)
            dve.wait_ge(x_scale_step, 1)
            dve.reciprocal(col(INV_X), col(SX)).then_inc(inv_x, 1)
            dve.tensor_tensor(col(CG), col(SX), col(WFAC), ALU.mult).then_inc(x_scale_step, 1)
            dve.wait_ge(x_scale_step, 2)

            dve.wait_ge(x1_stored, 16 * PAIRS)

            def split_x(c):
                dve.wait_ge(xi_ready, c + 1)
                o = c * (4 * CH)
                view = lambda part: (xq[:, o + part * 2 * CH:o + (part + 1) * 2 * CH] if isinstance(c, int)
                                     else xq[:, bass.ds(o + part * 2 * CH, 2 * CH)])
                dve.tensor_copy(view(0), x_int[0]).then_inc(x_hi, 1)
                dve.wait_ge(x_hi, c + 1)
                dve.tensor_tensor(view(1), x_int[0], view(0), ALU.subtract).then_inc(xq_ready, 1)

            def max_proj(evac, table, slot_of, done):
                def f(c):
                    for j in range(FP):
                        dve.wait_ge(evac, c * FP + (j + 1))
                        i = c * FP + j
                        dst = table[:, i:i + 1] if isinstance(i, int) else table[:, bass.ds(i, 1)]
                        dve.tensor_reduce(dst, slot_pair(slot_of(c), j), AX.X, ALU.max, apply_absolute_value=True).then_inc(done, 1)
                return f

            def max_up(c, j, slot):
                i = c * FP + j
                dve.wait_ge(u_evac, c * FP + (j + 1))
                dst = umax[:, i:i + 1] if isinstance(i, int) else umax[:, bass.ds(i, 1)]
                dve.tensor_reduce(dst, slot_pair(slot, j), AX.X, ALU.max, apply_absolute_value=True).then_inc(umax_done, 1)

            max_g = max_proj(g_evac, gmax, lambda c: c, gmax_done)
            split_x(0)
            with dve.Fori(1, CHUNKS) as c:
                split_x(c)
                max_g(c - 1)
            max_g(CHUNKS - 1)
            dve.wait_ge(gmax_done, CHUNKS * FP)
            partition_max(2, gmax[:, :], red_g)
            dve.wait_ge(all_g, 1)
            dve.tensor_tensor(col(SG), allmax[:, 2:3], col(CG), ALU.mult).then_inc(g_scale_step, 1)
            dve.wait_ge(g_scale_step, 1)
            dve.tensor_scalar(col(SG), col(SG), 1.0 / QMAX16, TINY, ALU.mult, ALU.max).then_inc(g_scale_step, 1)
            dve.wait_ge(g_scale_step, 2)
            dve.reciprocal(col(INV_G), col(SG)).then_inc(g_scale_step, 1)
            dve.wait_ge(g_scale_step, 3)
            dve.tensor_scalar(col(SGK), col(SG), 1.0 / 65536.0, None, ALU.mult)
            dve.tensor_tensor(col(INV_G), col(INV_G), col(CG), ALU.mult).then_inc(inv_g, 1)

            def max_gs(c, j):
                dve.wait_ge(gs_ready, c * FP + (j + 1))
                i = c * FP + j
                dst = gsmax[:, i:i + 1] if isinstance(i, int) else gsmax[:, bass.ds(i, 1)]
                dve.tensor_reduce(dst, int_pair(c, j), AX.X, ALU.max, apply_absolute_value=True).then_inc(gsmax_done, 1)

            def integer_sigmoid(c, j):
                dve.wait_ge(sig_ready, c * FP + (j + 1))
                dve.tensor_scalar(sigq[j], sig[j], 65536.0, 65535.0, ALU.mult, ALU.min).then_inc(sigq_ready, 1)

            def gate_chain(c, up_slot, pairs=FP):
                for j in range(pairs):
                    max_up(c, j, up_slot)
                    integer_sigmoid(c, j)
                    if j > 0:
                        max_gs(c, j - 1)
                    elif not isinstance(c, int) or c > 0:
                        max_gs(c - 1, FP - 1)

            gate_chain(0, 8)
            with dve.Fori(1, 4) as c:
                gate_chain(c, c + 8)
            with dve.Fori(4, CHUNKS - 1) as c:
                gate_chain(c, c + 4)
            gate_chain(CHUNKS - 1, CHUNKS + 3, FP - 1)
            max_up(CHUNKS - 1, FP - 1, CHUNKS + 3)
            dve.wait_ge(umax_done, CHUNKS * FP)
            dve.tensor_reduce(red[:, 4:5], umax[:, :], AX.X, ALU.max).then_inc(red_u, 1)
            integer_sigmoid(CHUNKS - 1, FP - 1)
            max_gs(CHUNKS - 1, FP - 2)
            dve.wait_ge(all_u, 1)
            dve.tensor_tensor(col(SU), allmax[:, 4:5], col(CG), ALU.mult).then_inc(u_scale_step, 1)
            dve.wait_ge(u_scale_step, 1)
            dve.tensor_scalar(col(SU), col(SU), 1.0 / QMAX16, TINY, ALU.mult, ALU.max).then_inc(u_scale_step, 1)
            dve.wait_ge(u_scale_step, 2)
            dve.reciprocal(col(CU), col(SU)).then_inc(u_scale_step, 1)
            dve.wait_ge(u_scale_step, 3)
            dve.tensor_tensor(col(INV_U), col(CU), col(CG), ALU.mult).then_inc(inv_u, 1)

            max_gs(CHUNKS - 1, FP - 1)
            dve.wait_ge(gsmax_done, CHUNKS * FP)
            dve.tensor_reduce(red[:, 3:4], gsmax[:, :], AX.X, ALU.max).then_inc(red_gs, 1)
            dve.wait_ge(all_gs, 1)
            dve.tensor_tensor(col(SGS), allmax[:, 3:4], col(SGK), ALU.mult).then_inc(gs_scale_step, 1)
            dve.wait_ge(gs_scale_step, 1)
            dve.tensor_scalar(col(SGS), col(SGS), 1.0 / QMAX16, TINY, ALU.mult, ALU.max).then_inc(gs_scale_step, 1)
            dve.wait_ge(gs_scale_step, 2)
            dve.reciprocal(col(INV_GS), col(SGS)).then_inc(gs_scale_step, 1)
            dve.wait_ge(gs_scale_step, 3)
            dve.tensor_tensor(col(INV_GS), col(INV_GS), col(SGK), ALU.mult).then_inc(inv_gs, 1)
            dve.tensor_tensor(col(SGU), col(SGS), col(SU), ALU.mult).then_inc(u_scale_step, 1)
            dve.wait_ge(inv_gs, 1)
            dve.wait_ge(u_scale_step, 4)

            def max_o(k, j, slot):
                if j == 0:
                    dve.wait_ge(o_first, k + 1)
                else:
                    dve.wait_ge(o_rest, k * (FP - 1) + j)
                i = k * FP + j
                dst = omax[:, i:i + 1] if isinstance(i, int) else omax[:, bass.ds(i, 1)]
                dve.tensor_reduce(dst, int_pair(slot, j), AX.X, ALU.max, apply_absolute_value=True).then_inc(omax_done, 1)

            def combine(k, gate_slot, up_slot, last_slot):
                g, o = int_pair(gate_slot, 0), int_pair(up_slot, 0)
                if not isinstance(k, int) or k < ACT_GATES:
                    dve.tensor_scalar(g, g, col(INV_GS), None, ALU.mult).then_inc(gsq_first, 1)
                if last_slot is not None:
                    max_o(k - 1, 1, last_slot)
                if isinstance(k, int) and k >= ACT_GATES:
                    dve.wait_ge(gsq_first_act, k - ACT_GATES + 1)
                else:
                    dve.wait_ge(gsq_first, k + 1)
                dve.wait_ge(uq_ready, k * FP + 1)
                dve.tensor_tensor(o, g, o, ALU.mult).then_inc(o_first, 1)
                if last_slot is not None:
                    max_o(k - 1, 2, last_slot)
                max_o(k, 0, up_slot)

            combine(0, 4, O_SLOTS[0], None)
            with dve.Fori(1, 4) as k:
                combine(k, k + 4, k + 8, k + 7)
            for k in range(4, CHUNKS):
                combine(k, k - 4, O_SLOTS[k], O_SLOTS[k - 1])
            for j in (1, 2):
                max_o(CHUNKS - 1, j, O_SLOTS[CHUNKS - 1])

            dve.wait_ge(omax_done, CHUNKS * FP)
            partition_max(5, omax[:, :], red_o)
            dve.wait_ge(all_o, 1)
            dve.tensor_tensor(col(SO), allmax[:, 5:6], col(SGU), ALU.mult).then_inc(o_scale_step, 1)
            dve.wait_ge(o_scale_step, 1)
            dve.tensor_scalar(col(SO), col(SO), 1.0 / QMAX16, TINY, ALU.mult, ALU.max).then_inc(o_scale_step, 1)
            dve.wait_ge(o_scale_step, 2)
            dve.reciprocal(col(CO), col(SO)).then_inc(o_scale_step, 1)
            dve.wait_ge(o_scale_step, 3)
            dve.tensor_tensor(col(INV_O), col(CO), col(SGU), ALU.mult).then_inc(inv_o, 1)
            dve.tensor_tensor(col(OUT_SCALE), col(SO), col(WFAC), ALU.mult).then_inc(co_ready, 1)
            dve.wait_ge(co_ready, 1)

            dve.wait_ge(inv_o, 1)
            dve.tensor_scalar(o_int[1], at(O_SLOTS[0] * SLOT + SLOT // 2, SLOT // 2).bitcast(I32), col(INV_O), None,
                              ALU.mult).then_inc(oi_first, 1)

            def split_o(n, v):
                for j in range(2):
                    if isinstance(n, int) and n == 0 and j == 1:
                        dve.wait_ge(oi_first, 1)
                    else:
                        dve.wait_ge(oi_ready, 1 if isinstance(n, int) and n == 0 else 2 * n + j)
                    if due(4 * n - 4):
                        dve.wait_ge(y_psum, 4 * n - 4)
                    hi, lo = (o_parts[v][:, (i * FT + 3 * j) * CH:(i * FT + 3 * j + 3) * CH] for i in range(2))
                    dve.tensor_copy(hi, o_int[j]).then_inc(o_hi, 1)
                    dve.wait_ge(o_hi, 2 * n + (j + 1))
                    dve.tensor_tensor(lo, o_int[j], hi, ALU.subtract).then_inc(op_ready, 1)

            def finish(n, v, count):
                dve.wait_ge(x1_back[v], count * 16 + 16)
                if due(count * 16):
                    dve.wait_ge(y_stored[v], count * 16)
                for t in range(4):
                    dve.wait_ge(y_psum, 4 * n + (t + 1))
                    sl = slice(t * HID, (t + 1) * HID)
                    dve.scalar_tensor_tensor(y_out[v][:, sl], bank[t][:, 0:HID], col(OUT_SCALE), x1_in[v][:, sl],
                                             ALU.mult, ALU.add).then_inc(yo_ready, 1)

            split_o(0, 0)
            split_o(1, 1)
            finish(0, 0, 0)
            def two_chunks(g):
                split_o(g * 2, 0)
                finish(g * 2 - 1, 1, g - 1)
                split_o(g * 2 + 1, 1)
                finish(g * 2, 0, g)

            two_chunks(1)
            with dve.Fori(2, CHUNKS // 2) as g:
                two_chunks(g)
            finish(CHUNKS - 1, 1, CHUNKS // 2 - 1)


def kernel(x, ctx_1024, L0_xattn_igate_kernel, L0_xattn_igate_bias, L0_xattn_fgate_kernel, L0_xattn_fgate_bias,
           L0_xattn_outnorm_scale, L0_ffn_w_gate, L0_ffn_w_up, L0_ffn_w_down):
    import numpy as np
    import concourse.bacc as bacc
    from concourse.bass_utils import run_bass_kernel_spmd

    x, c = np.asarray(x), np.asarray(ctx_1024)
    natural = lambda t: t.reshape(PAIRS, PAIR, HALVES, P, HID).transpose(0, 3, 1, 2, 4).reshape(PAIRS, P, -1)
    gate_w = np.concatenate([np.asarray(L0_xattn_igate_kernel), np.asarray(L0_xattn_fgate_kernel)], axis=1)
    arrays = {
        "x": natural(x),
        "ctx_nat": natural(c),
        "ctx_t": c.reshape(-1, UNROLL, SEQ, KT, P).transpose(0, 4, 1, 3, 2).reshape(BATCH // UNROLL, P, -1),
        "gate_w": gate_w.reshape(3 * KT, P, 2 * NH).transpose(1, 0, 2).reshape(P, -1),
        "gate_b": np.concatenate([np.asarray(L0_xattn_igate_bias), np.asarray(L0_xattn_fgate_bias)]),
        "norm_scale": np.asarray(L0_xattn_outnorm_scale),
        "w_gate": np.asarray(L0_ffn_w_gate),
        "w_up": np.asarray(L0_ffn_w_up),
        "w_down": np.asarray(L0_ffn_w_down),
    }
    arrays = {n: np.ascontiguousarray(a) for n, a in arrays.items()}
    nc = bacc.Bacc("TRN2", target_bir_lowering=False, num_devices=1)
    args = [nc.dram_tensor(n, a.shape, mybir.dt.from_np(a.dtype), kind="ExternalInput").ap() for n, a in arrays.items()]
    out = nc.dram_tensor("out", (PAIRS, P, PAIR * HALVES * HID), F32, kind="ExternalOutput").ap()
    bass_xattn_ffn(nc, *args, out)
    y = run_bass_kernel_spmd(nc, [arrays], core_ids=[0]).results[0]["out"]
    return y.reshape(PAIRS, P, PAIR, HALVES, HID).transpose(0, 2, 3, 1, 4).reshape(BATCH, SEQ, HID)
```
